# Optimizing a Trainium2 kernel written in Bass

```python
import numpy as np
import jax
import jax.numpy as jnp

def _softmax(x, axis=-1):
    return jax.nn.softmax(x, axis=axis)
def _gelu(x):
    return jax.nn.gelu(x, approximate=True)
def _silu(x):
    return jax.nn.silu(x)
def _sigmoid(x):
    return jax.nn.sigmoid(x)
def _layernorm(x, axis=-1, eps=1e-5):
    m = jnp.mean(x, axis=axis, keepdims=True)
    v = jnp.var(x, axis=axis, keepdims=True)
    return (x - m) / jnp.sqrt(v + eps)
def _scatter_add(tgt, idx, src, axis=0):
    return tgt.at[idx].add(src)
def _segment_sum(src, seg, n):
    return jax.ops.segment_sum(src, seg, n)

kernel_name = 'mk_conv_preact_d2_conv_nhwc768_a0687b'

def setup_inputs(seed: int = 0):
    np.random.seed(seed)
    _w = jnp.asarray
    def _rec_inputs():
        import jax
        import jax.numpy as jnp
        _gk = jax.random.key(seed)
        x = -0.0005058 + 1 * jax.random.normal(jax.random.fold_in(_gk, 1), (2, 48, 48, 768), jnp.float32)
        return x
    x = _rec_inputs()
    def _L0_conv_setup():
        import jax, jax.numpy as jnp
        import numpy as np
        DIM = 768
        NUM_HEADS = 12
        HEAD_DIM = DIM // NUM_HEADS
        H = W = 48

        def _get_rel_pos(size, rel_pos):
            coords = jnp.arange(size)[:, None] - jnp.arange(size)[None, :] + (size - 1)
            return rel_pos[coords]
        key = jax.random.key(seed)
        ks = jax.random.split(key, 7)
        x = jax.random.normal(ks[0], (2, H, W, DIM), dtype=jnp.float32)
        qkv_w = jax.random.normal(ks[1], (DIM, 3 * DIM), dtype=jnp.float32) * DIM ** (-0.5)
        qkv_b = jax.random.normal(ks[2], (3 * DIM,), dtype=jnp.float32) * 0.02
        proj_w = jax.random.normal(ks[3], (DIM, DIM), dtype=jnp.float32) * DIM ** (-0.5)
        proj_b = jax.random.normal(ks[4], (DIM,), dtype=jnp.float32) * 0.02
        rel_pos_h = jax.random.normal(ks[5], (2 * H - 1, HEAD_DIM), dtype=jnp.float32) * 0.02
        rel_pos_w = jax.random.normal(ks[6], (2 * W - 1, HEAD_DIM), dtype=jnp.float32) * 0.02
        return {'x': x, 'qkv_w': qkv_w, 'qkv_b': qkv_b, 'proj_w': proj_w, 'proj_b': proj_b, 'rel_pos_h': rel_pos_h, 'rel_pos_w': rel_pos_w}
    _L0_conv_all = _L0_conv_setup()
    _L0_conv_in = {k: v for k, v in _L0_conv_all.items() if k in ('qkv_w', 'qkv_b', 'proj_w', 'proj_b', 'rel_pos_h', 'rel_pos_w', )}
    del _L0_conv_all

    def _L1_conv_setup():
        import jax, jax.numpy as jnp
        import numpy as np
        SPARSITY = 0.01
        NUM_BLOCKS = 8

        def _softshrink(v, lam):
            return jnp.sign(v) * jnp.maximum(jnp.abs(v) - lam, 0.0)
        key = jax.random.key(seed)
        ks = jax.random.split(key, 5)
        B, H, W, C = (4, 128, 128, 768)
        nb, bs = (NUM_BLOCKS, C // NUM_BLOCKS)
        return {'x': jax.random.normal(ks[0], (B, H, W, C), dtype=jnp.float32), 'w1': jax.random.normal(ks[1], (2, nb, bs, bs), dtype=jnp.float32) * 0.02, 'b1': jax.random.normal(ks[2], (2, nb, bs), dtype=jnp.float32) * 0.02, 'w2': jax.random.normal(ks[3], (2, nb, bs, bs), dtype=jnp.float32) * 0.02, 'b2': jax.random.normal(ks[4], (2, nb, bs), dtype=jnp.float32) * 0.02}
    _L1_conv_all = _L1_conv_setup()
    _L1_conv_in = {k: v for k, v in _L1_conv_all.items() if k in ('w1', 'b1', 'w2', 'b2', )}
    del _L1_conv_all

    return {
        "x": x,
        "L0_conv_qkv_w": _L0_conv_in["qkv_w"],
        "L0_conv_qkv_b": _L0_conv_in["qkv_b"],
        "L0_conv_proj_w": _L0_conv_in["proj_w"],
        "L0_conv_proj_b": _L0_conv_in["proj_b"],
        "L0_conv_rel_pos_h": _L0_conv_in["rel_pos_h"],
        "L0_conv_rel_pos_w": _L0_conv_in["rel_pos_w"],
        "L1_conv_w1": _L1_conv_in["w1"],
        "L1_conv_b1": _L1_conv_in["b1"],
        "L1_conv_w2": _L1_conv_in["w2"],
        "L1_conv_b2": _L1_conv_in["b2"],
    }

def reference(x, L0_conv_qkv_w, L0_conv_qkv_b, L0_conv_proj_w, L0_conv_proj_b, L0_conv_rel_pos_h, L0_conv_rel_pos_w, L1_conv_w1, L1_conv_b1, L1_conv_w2, L1_conv_b2):
    import jax
    import jax.numpy as jnp
    def _L0_conv_ref(x, qkv_w, qkv_b, proj_w, proj_b, rel_pos_h, rel_pos_w):
        import jax, jax.numpy as jnp
        import numpy as np
        DIM = 768
        NUM_HEADS = 12
        HEAD_DIM = DIM // NUM_HEADS
        H = W = 48

        def _get_rel_pos(size, rel_pos):
            coords = jnp.arange(size)[:, None] - jnp.arange(size)[None, :] + (size - 1)
            return rel_pos[coords]
        B, h, w, dim = x.shape
        nh, hd = (NUM_HEADS, HEAD_DIM)
        S = h * w
        scale = hd ** (-0.5)
        qkv = (x.reshape(B, S, dim) @ qkv_w + qkv_b).reshape(B, S, 3, nh, hd)
        qkv = jnp.transpose(qkv, (2, 0, 3, 1, 4)).reshape(3, B * nh, S, hd)
        q, k, v = (qkv[0], qkv[1], qkv[2])
        attn = jnp.einsum('bqc,bkc->bqk', q * scale, k)
        Rh = _get_rel_pos(h, rel_pos_h)
        Rw = _get_rel_pos(w, rel_pos_w)
        r_q = q.reshape(B * nh, h, w, hd)
        rel_h = jnp.einsum('bhwc,hkc->bhwk', r_q, Rh)
        rel_w = jnp.einsum('bhwc,wkc->bhwk', r_q, Rw)
        attn = (attn.reshape(B * nh, h, w, h, w) + rel_h[:, :, :, :, None] + rel_w[:, :, :, None, :]).reshape(B * nh, S, S)
        attn = jax.nn.softmax(attn, axis=-1)
        out = (attn @ v).reshape(B, nh, h, w, hd)
        out = jnp.transpose(out, (0, 2, 3, 1, 4)).reshape(B, h, w, dim)
        return out @ proj_w + proj_b

    def _L1_conv_ref(x, w1, b1, w2, b2):
        import jax, jax.numpy as jnp
        import numpy as np
        SPARSITY = 0.01
        NUM_BLOCKS = 8

        def _softshrink(v, lam):
            return jnp.sign(v) * jnp.maximum(jnp.abs(v) - lam, 0.0)
        B, H, W, C = x.shape
        nb = NUM_BLOCKS
        bs = C // nb
        xf = jnp.fft.rfft2(x, axes=(1, 2), norm='ortho')
        Hf, Wf = (xf.shape[1], xf.shape[2])
        xr = xf.real.reshape(B, Hf, Wf, nb, bs)
        xi = xf.imag.reshape(B, Hf, Wf, nb, bs)
        o1r = jax.nn.gelu(jnp.einsum('bhwni,nio->bhwno', xr, w1[0]) - jnp.einsum('bhwni,nio->bhwno', xi, w1[1]) + b1[0], approximate=False)
        o1i = jax.nn.gelu(jnp.einsum('bhwni,nio->bhwno', xi, w1[0]) + jnp.einsum('bhwni,nio->bhwno', xr, w1[1]) + b1[1], approximate=False)
        o2r = jnp.einsum('bhwni,nio->bhwno', o1r, w2[0]) - jnp.einsum('bhwni,nio->bhwno', o1i, w2[1]) + b2[0]
        o2i = jnp.einsum('bhwni,nio->bhwno', o1i, w2[0]) + jnp.einsum('bhwni,nio->bhwno', o1r, w2[1]) + b2[1]
        o2r = _softshrink(o2r, SPARSITY)
        o2i = _softshrink(o2i, SPARSITY)
        xc = (o2r + 1j * o2i).reshape(B, Hf, Wf, C)
        out = jnp.fft.irfft2(xc, s=(H, W), axes=(1, 2), norm='ortho')
        return out

    def _gn(v, G=32, eps=1e-5):
        B_, H_, W_, C_ = v.shape
        g = v.reshape(B_, H_, W_, G, C_ // G)
        m = jnp.mean(g, axis=(1, 2, 4), keepdims=True)
        s = jnp.var(g, axis=(1, 2, 4), keepdims=True)
        return ((g - m) / jnp.sqrt(s + eps)).reshape(v.shape)

    def _ln_c(v, eps=1e-6):
        m = jnp.mean(v, axis=-1, keepdims=True)
        s = jnp.var(v, axis=-1, keepdims=True)
        return (v - m) / jnp.sqrt(s + eps)

    def _ln_t(v, eps=1e-5):
        m = jnp.mean(v, axis=-1, keepdims=True)
        s = jnp.var(v, axis=-1, keepdims=True)
        return (v - m) / jnp.sqrt(s + eps)

    def _to_tokens(v):
        B_, H_, W_, C_ = v.shape
        return v.reshape(B_, H_ * W_, C_)
    def _from_tokens(t, like):
        return t.reshape(like.shape)

    x = x + _L0_conv_ref(_gn(x), L0_conv_qkv_w, L0_conv_qkv_b, L0_conv_proj_w, L0_conv_proj_b, L0_conv_rel_pos_h, L0_conv_rel_pos_w)
    x = x + _L1_conv_ref(_gn(x), L1_conv_w1, L1_conv_b1, L1_conv_w2, L1_conv_b2)
    return x


_drawn_inputs = setup_inputs


def setup_inputs(seed=0):
    import zlib

    import numpy as np

    out = dict(_drawn_inputs(seed))
    spreads = {}
    factors = {'L0_conv_qkv_b': 2.96,
     'L0_conv_proj_b': 2.779,
     'L0_conv_rel_pos_h': 8.0,
     'L0_conv_rel_pos_w': 8.0,
     'L1_conv_b1': 8.0}
    for name, (base, spread) in spreads.items():
        noise = np.random.default_rng([zlib.crc32(name.encode()), seed]).standard_normal(out[name].shape)
        drawn = base * np.exp(spread * noise) if base else spread * noise
        out[name] = jnp.asarray(drawn.astype(out[name].dtype))
    for name, factor in factors.items():
        out[name] = (out[name] * factor).astype(out[name].dtype)
    return out
```

```python
from contextlib import ExitStack

import concourse.bass as bass
import numpy as np
from concourse import mybir
from concourse.alu_op_type import AluOpType as ALU

F32 = mybir.dt.float32
F32R = mybir.dt.float32r
ACT = mybir.ActivationFunctionType
AX_X = mybir.AxisListType.X

P = 128
B, H, W, C = 2, 48, 48, 768
S = H * W
CT = C // P
HEADS, D = 12, 64
PAIRS = HEADS // 2
NP = B * PAIRS
KT = S // P
KG = 3
GK = S // KG
KW = W // KG
KR = P // KW
GROUPS = 32
GC = C // GROUPS
EPS = 1e-5
SCALE = D ** -0.5
NREL = 2 * H - 1

QC = 5
ROWS = [10, 10, 10, 10, 8]
QN = [r * W for r in ROWS]
Q0 = [10 * W * c for c in range(QC)]
QMAX = QN[0]

TG = 384
NTG = S // TG
TPG = TG // P

SPARSITY = 0.01
NB, BS = 8, 96
KWF = W // 2 + 1
RI = 2


def natural(ap):
    return ap.rearrange("p (j h w) -> p h j w", j=KG, w=KW)


def project(nc, x, qkv_w, qk_bias, qkv_b, ident_d, ind_d, indT_d, qF, qHL, kHL, vD):
    with ExitStack() as ctx:
        def sb(name, shape, dt=F32):
            return ctx.enter_context(nc.sbuf_tensor("project_" + name, shape, dt))

        def sem(name):
            return ctx.enter_context(nc.semaphore("project_" + name))

        xh = sb("xn_hi", [P, CT, S], F32R)
        xl = sb("xn_lo", [P, CT, S], F32R)
        xtok = sb("x_tokens", [P, 2, TPG, C])
        ident = sb("ident", [P, P])
        ind = sb("ind", [P, CT, GROUPS])
        indT = sb("indT", [GROUPS, C])
        qb = sb("q_bias", [P, 2 * PAIRS])
        vb = sb("v_bias", [P, C])
        stats = sb("stats", [P, CT, NTG, 6])
        mv = sb("mean_var", [P, CT, 2])
        gate = sb("gate", [P, 1])
        dev = sb("deviation", [P, CT])
        within = sb("within", [P, CT])
        gm = sb("group_mean", [GROUPS, 1])
        gv = sb("group_var", [GROUPS, 1])
        gs = sb("group_std", [GROUPS, 1])
        gr = sb("group_rstd", [GROUPS, 1])
        epst = sb("eps", [GROUPS, 1])
        cm = sb("channel_mean", [P, CT])
        cr = sb("channel_rstd", [P, CT])
        cb = sb("channel_shift", [P, CT])
        xn = sb("xn", [P, 4, TG])
        wraw = sb("w_raw", [P, 2, CT, P])
        whl = sb("w_split", [P, 2, 2, CT, P], F32R)
        row = sb("qk_row", [P, 2, QMAX])
        hl = sb("qk_split", [P, 2, S], F32R)
        wv = sb("wv_split", [P, 2, CT, TG], F32R)
        vout = sb("v_out", [P, 2, TG])
        ps = [ctx.enter_context(nc.psum_tensor(f"project_ps{i}", [P, 512], F32)) for i in range(8)]

        consts = sem("consts")
        eps_set = sem("eps_set")
        x_loaded = [sem(f"x_loaded{i}") for i in range(2)]
        transposed = sem("transposed")
        st_done = sem("st_done")
        chain = sem("dve_chain")
        gsum_ready = sem("gsum_ready")
        gmean_set = sem("gmean_set")
        within_set = sem("within_set")
        gvar_set = sem("gvar_set")
        gstd_set = sem("gstd_set")
        grstd_set = sem("grstd_set")
        shift_set = sem("shift_set")
        xn_written = sem("xn_written")
        xh_set = sem("xh_set")
        xhl_written = sem("xhl_written")
        w_loaded = [sem(f"w_loaded{i}") for i in range(2)]
        wh_set = sem("wh_set")
        w_split = sem("w_split_done")
        qk_product = sem("qk_product")
        qk_biased = sem("qk_biased")
        qk_hi = sem("qk_hi")
        qk_lo = sem("qk_lo")
        qrow_stored = [sem(f"qrow_stored{i}") for i in range(2)]
        qk_stored = sem("qk_stored")
        wv_loaded = [sem(f"wv_loaded{i}") for i in range(2)]
        wvh_set = sem("wvh_set")
        wv_split = sem("wv_split_done")
        v_product = sem("v_product")
        v_biased = sem("v_biased")
        v_stored = [sem(f"v_stored{i}") for i in range(2)]

        NTP = NTG * CT
        OT = 2 * PAIRS
        NVH = C // TG
        x_view = x.rearrange("b (g t p) c -> b g p t c", t=TPG, p=P)
        w_view = qkv_w.rearrange("(t p) n -> p t n", p=P)

        with nc.Block() as block:

            @block.sync
            def _(sp):
                for dst, src in ((ident[:], ident_d), (ind[:], ind_d), (indT[:], indT_d),
                                 (qb[:], qk_bias),
                                 (vb[:], qkv_b[2 * C:3 * C].rearrange("(a c) -> a c", a=1).broadcast_to([P, C]))):
                    sp.dma_start(dst, src).then_inc(consts, 16)
                with sp.Fori(0, B) as b:
                    for pas in range(2):
                        for g in range(NTG):
                            n = pas * NTG + g
                            if n >= 2:
                                sp.wait_ge(transposed, b * (2 * NTP) + (n - 1) * CT)
                            sp.dma_start(xtok[:, g % 2], x_view[b, g]).then_inc(x_loaded[g % 2], 16)
                    for o in range(OT + 1):
                        if o < OT:
                            if o >= 2:
                                sp.wait_ge(w_split, b * OT + o - 1)
                            sp.dma_start(wraw[:, o % 2], w_view[:, :, o * P:(o + 1) * P]).then_inc(w_loaded[o % 2], 16)
                        if o == 0:
                            continue
                        m = o - 1
                        if m < PAIRS:
                            for c in range(QC):
                                n = m * QC + c
                                sp.wait_ge(qk_biased, b * (OT * QC) + n + 1)
                                sp.dma_start(qF[b * PAIRS + m][:, Q0[c]:Q0[c] + QN[c]],
                                             row[:, n % 2, 0:QN[c]]).then_inc(qrow_stored[n % 2], 16)
                        sp.wait_ge(qk_lo, b * (OT * QC) + m * QC + QC)
                        dst = qHL if m < PAIRS else kHL
                        sp.dma_start(dst[b * PAIRS + m % PAIRS], hl[:].bitcast(F32)).then_inc(qk_stored, 16)
                    for vh in range(NVH):
                        sp.wait_ge(transposed, (b + 1) * (2 * NTP))
                        sp.dma_start(xtok[:, vh].rearrange("p a (c n) -> p (a c) n", n=TG),
                                     w_view[:, :, 2 * C + vh * TG:2 * C + (vh + 1) * TG]).then_inc(wv_loaded[vh], 16)
                    for n in range(NVH * KT):
                        sp.wait_ge(v_biased, b * (NVH * KT) + n + 1)
                        sp.dma_start(vD.rearrange("(b v o) p t d -> b v t p o d", b=B, v=NVH)[b, n // KT, n % KT],
                                     vout[:, n % 2].rearrange("p (o d) -> p o d", d=P)
                                     ).then_inc(v_stored[n % 2], 16)
                sp.wait_ge(qk_stored, B * OT * 16)
                for i in range(2):
                    sp.wait_ge(qrow_stored[i], B * PAIRS * QC * 8)
                for i in range(2):
                    sp.wait_ge(v_stored[i], B * NVH * KT // 2 * 16)

            @block.tensor
            def _(pe):
                pe.wait_ge(consts, 5 * 16)
                with pe.Fori(0, B) as b:
                    for pas in range(2):
                        for g in range(NTG):
                            pe.wait_ge(x_loaded[g % 2], (b * NTG + pas * (NTG // 2) + g // 2 + 1) * 16)
                            for ct in range(CT):
                                n = g * CT + ct
                                if pas == 0 and n >= 4:
                                    pe.wait_ge(st_done, b * NTP + n - 3)
                                if pas == 0 and n == 0:
                                    pe.wait_ge(v_biased, b * (NVH * KT))
                                if pas == 1 and n >= 4:
                                    pe.wait_ge(xn_written, b * NTP + n - 3)
                                for t in range(TPG):
                                    mm = nc.tensor.transpose(ps[n % 4][:, t * P:(t + 1) * P],
                                                             xtok[:, g % 2, t, ct * P:(ct + 1) * P], ident[:])
                                mm.then_inc(transposed, 1)
                        if pas == 0:
                            pe.wait_ge(chain, b * 3 + 1)
                            for ct in range(CT):
                                mm = nc.tensor.matmul(ps[4][0:GROUPS, 0:1], ind[:, ct], mv[:, ct, 0:1],
                                                      start=ct == 0, stop=ct == CT - 1)
                            mm.then_inc(gsum_ready, 1)
                            pe.wait_ge(gmean_set, b + 1)
                            for ct in range(CT):
                                mm = nc.tensor.matmul(ps[5][:, ct:ct + 1], indT[:, ct * P:(ct + 1) * P], gm[:],
                                                      start=True, stop=True)
                            mm.then_inc(gsum_ready, 1)
                            pe.wait_ge(within_set, b + 1)
                            for ct in range(CT):
                                mm = nc.tensor.matmul(ps[6][0:GROUPS, 0:1], ind[:, ct], within[:, ct:ct + 1],
                                                      start=ct == 0, stop=ct == CT - 1)
                            mm.then_inc(gsum_ready, 1)
                            pe.wait_ge(grstd_set, b + 1)
                            for ct in range(CT):
                                mm = nc.tensor.matmul(ps[7][:, ct:ct + 1], indT[:, ct * P:(ct + 1) * P], gr[:],
                                                      start=True, stop=True)
                            mm.then_inc(gsum_ready, 1)
                    pe.wait_ge(xhl_written, (b + 1) * NTP)
                    for o in range(OT):
                        pe.wait_ge(w_split, b * OT + o + 1)
                        for c in range(QC):
                            n = o * QC + c
                            if n >= 2:
                                pe.wait_ge(qk_biased, b * (OT * QC) + n - 1)
                            k = 0
                            for wp, xp in ((0, xh), (0, xl), (1, xh)):
                                for ct in range(CT):
                                    cols = (natural(xp[:, ct])[:, 10 * c:10 * c + ROWS[c]] if o < PAIRS
                                            else xp[:, ct, Q0[c]:Q0[c] + QN[c]])
                                    mm = nc.tensor.matmul(ps[4 + n % 2][:, 0:QN[c]], whl[:, o % 2, wp, ct],
                                                          cols, start=k == 0, stop=k == 3 * CT - 1)
                                    k += 1
                            mm.then_inc(qk_product, 1)
                    for n in range(NVH * KT):
                        vh, t = n // KT, n % KT
                        if t == 0:
                            pe.wait_ge(wv_split, b * NVH + vh + 1)
                        if n >= 2:
                            pe.wait_ge(v_biased, b * (NVH * KT) + n - 1)
                        k = 0
                        for xp, wp in ((xh, 0), (xh, 1), (xl, 0)):
                            for ct in range(CT):
                                mm = nc.tensor.matmul(ps[6 + n % 2][:, 0:TG], xp[:, ct, t * P:(t + 1) * P], wv[:, wp, ct],
                                                      start=k == 0, stop=k == 3 * CT - 1)
                                k += 1
                        mm.then_inc(v_product, 1)

            @block.scalar
            def _(act):
                act.wait_ge(consts, 5 * 16)
                act.wait_ge(eps_set, 1)
                with act.Fori(0, B) as b:
                    act.wait_ge(gvar_set, b + 1)
                    nc.scalar.activation(gs[:], gv[:], ACT.Sqrt, bias=epst[:]).then_inc(gstd_set, 1)
                    act.wait_ge(shift_set, b + 1)
                    for n in range(NTP):
                        ct = n % CT
                        act.wait_ge(transposed, b * (2 * NTP) + NTP + n + 1)
                        if n >= 4:
                            act.wait_ge(xhl_written, b * NTP + n - 3)
                        nc.scalar.activation(xn[:, n % 4], ps[n % 4][:, 0:TG], ACT.Identity,
                                             bias=cb[:, ct:ct + 1], scale=cr[:, ct:ct + 1]).then_inc(xn_written, 1)
                    for o in range(OT):
                        for c in range(QC):
                            n = o * QC + c
                            act.wait_ge(qk_product, b * (OT * QC) + n + 1)
                            if n >= 2:
                                act.wait_ge(qk_lo, b * (OT * QC) + n - 1)
                            if o < PAIRS:
                                act.wait_ge(qrow_stored[n % 2], b * (PAIRS * QC * 8) + n // 2 * 16)
                            elif n < PAIRS * QC + 2:
                                act.wait_ge(qrow_stored[n % 2], (b + 1) * (PAIRS * QC * 8))
                            nc.scalar.activation(row[:, n % 2, 0:QN[c]], ps[4 + n % 2][:, 0:QN[c]], ACT.Identity,
                                                 bias=qb[:, o:o + 1], scale=1.0).then_inc(qk_biased, 1)

            @block.vector
            def _(dve):
                nc.vector.memset(epst[:], EPS).then_inc(eps_set, 1)
                dve.wait_ge(consts, 5 * 16)
                with dve.Fori(0, B) as b:
                    for g in range(NTG):
                        for ct in range(CT):
                            n = g * CT + ct
                            dve.wait_ge(transposed, b * (2 * NTP) + n + 1)
                            nc.vector.bn_stats(stats[:, ct, g], ps[n % 4][:, 0:TG]).then_inc(st_done, 1)
                    dve.wait_ge(st_done, (b + 1) * NTP)
                    nc.vector.memset(gate[:], 0.0)
                    for ct in range(CT):
                        ins = nc.vector.bn_aggr(mv[:, ct], stats[:, ct])
                    ins.then_inc(chain, 1)
                    dve.wait_ge(gsum_ready, b * 4 + 1)
                    nc.vector.tensor_scalar(gm[:], ps[4][0:GROUPS, 0:1], 1.0 / GC, None, ALU.mult).then_inc(gmean_set, 1)
                    dve.wait_ge(gsum_ready, b * 4 + 2)
                    nc.vector.tensor_copy(cm[:], ps[5][:, 0:CT]).then_inc(chain, 1)
                    dve.wait_ge(chain, b * 3 + 2)
                    nc.vector.tensor_tensor(dev[:], mv[:, :, 0], cm[:], ALU.subtract).then_inc(chain, 1)
                    dve.wait_ge(chain, b * 3 + 3)
                    for ct in range(CT):
                        ins = nc.vector.scalar_tensor_tensor(out=within[:, ct:ct + 1], in0=dev[:, ct:ct + 1],
                                                             scalar=dev[:, ct:ct + 1], in1=mv[:, ct, 1:2],
                                                             op0=ALU.mult, op1=ALU.add)
                    ins.then_inc(within_set, 1)
                    dve.wait_ge(gsum_ready, b * 4 + 3)
                    nc.vector.tensor_scalar(gv[:], ps[6][0:GROUPS, 0:1], 1.0 / GC, None, ALU.mult).then_inc(gvar_set, 1)
                    dve.wait_ge(gstd_set, b + 1)
                    nc.vector.reciprocal(gr[:], gs[:]).then_inc(grstd_set, 1)
                    dve.wait_ge(gsum_ready, b * 4 + 4)
                    nc.vector.scalar_tensor_tensor(out=cb[:], in0=ps[7][:, 0:CT], scalar=-1.0, in1=cm[:],
                                                   op0=ALU.mult, op1=ALU.mult)
                    nc.vector.tensor_copy(cr[:], ps[7][:, 0:CT]).then_inc(shift_set, 1)
                    for n in range(NTP):
                        g, ct = n // CT, n % CT
                        dve.wait_ge(xn_written, b * NTP + n + 1)
                        if n == 0:
                            dve.wait_ge(v_product, b * (NVH * KT))
                        src = xn[:, n % 4].rearrange("p (h j w) -> p h j w", j=KG, w=KW)
                        hi, lo = (natural(t[:, ct])[:, g * (TG // W):(g + 1) * (TG // W)] for t in (xh, xl))
                        nc.vector.tensor_copy(hi, src).then_inc(xh_set, 1)
                        dve.wait_ge(xh_set, b * NTP + n + 1)
                        nc.vector.tensor_tensor(lo, src, hi.bitcast(F32), ALU.subtract).then_inc(xhl_written, 1)

                    def split_w(o):
                        dve.wait_ge(w_loaded[o % 2], (b * PAIRS + o // 2 + 1) * 16)
                        if o >= 2:
                            dve.wait_ge(qk_product, b * (OT * QC) + (o - 1) * QC)
                        nc.vector.tensor_copy(whl[:, o % 2, 0], wraw[:, o % 2]).then_inc(wh_set, 1)
                        dve.wait_ge(wh_set, b * OT + o + 1)
                        nc.vector.tensor_tensor(whl[:, o % 2, 1], wraw[:, o % 2], whl[:, o % 2, 0].bitcast(F32),
                                                ALU.subtract).then_inc(w_split, 1)

                    split_w(0)
                    for o in range(OT):
                        if o + 1 < OT:
                            split_w(o + 1)
                        s = SCALE if o < PAIRS else 1.0
                        for c in range(QC):
                            n = o * QC + c
                            dve.wait_ge(qk_biased, b * (OT * QC) + n + 1)
                            if c == 0:
                                dve.wait_ge(qk_stored, (b * OT + o) * 16)
                            src = row[:, n % 2, 0:QN[c]]
                            hi, lo = (hl[:, i, Q0[c]:Q0[c] + QN[c]] for i in range(2))
                            nc.vector.tensor_scalar(hi, src, s, None, ALU.mult).then_inc(qk_hi, 1)
                            dve.wait_ge(qk_hi, b * (OT * QC) + n + 1)
                            nc.vector.scalar_tensor_tensor(out=lo, in0=src, scalar=s, in1=hi.bitcast(F32),
                                                           op0=ALU.mult, op1=ALU.subtract).then_inc(qk_lo, 1)
                    for vh in range(NVH):
                        raw = xtok[:, vh].rearrange("p a (c n) -> p (a c) n", n=TG)
                        dve.wait_ge(wv_loaded[vh], (b + 1) * 16)
                        dve.wait_ge(v_product, b * (NVH * KT) + vh * KT)
                        nc.vector.tensor_copy(wv[:, 0], raw).then_inc(wvh_set, 1)
                        dve.wait_ge(wvh_set, b * NVH + vh + 1)
                        nc.vector.tensor_tensor(wv[:, 1], raw, wv[:, 0].bitcast(F32), ALU.subtract).then_inc(wv_split, 1)
                        for t in range(KT):
                            n = vh * KT + t
                            dve.wait_ge(v_product, b * (NVH * KT) + n + 1)
                            dve.wait_ge(v_stored[n % 2], (b * (NVH * KT // 2) + n // 2) * 16)
                            nc.vector.tensor_tensor(vout[:, n % 2], ps[6 + n % 2][:, 0:TG],
                                                    vb[:, vh * TG:(vh + 1) * TG], ALU.add).then_inc(v_biased, 1)


RQ = 4
NU = H
NRP = NU // RQ


def relpos(nc, rev_h, rev_w, qF, relH, relW):
    with ExitStack() as ctx:
        def sb(name, shape, dt=F32):
            return ctx.enter_context(nc.sbuf_tensor("relpos_" + name, shape, dt))

        def sem(name):
            return ctx.enter_context(nc.semaphore("relpos_" + name))

        q = sb("q", [P, PAIRS, S])
        tab = sb("tab", [P, 2, NREL, 2])
        diff = sb("diff", [P, H, H, 2])
        w_hl = sb("w_split", [2 * W, 2, PAIRS, S], F32R)
        h_hl = sb("h_split", [2 * H, 2, 2, PAIRS, RQ * W], F32R)
        ps = [ctx.enter_context(nc.psum_tensor(f"relpos_ps{i}", [2 * H, 512], F32)) for i in range(8)]

        tab_zero = sem("tab_zero")
        tab_loaded = sem("tab_loaded")
        diff_zero = sem("diff_zero")
        diff_set = sem("diff_set")
        q_loaded = sem("q_loaded")
        product = sem("product")
        hi_set = sem("hi_set")
        lo_set = sem("lo_set")
        w_stored = sem("w_stored")
        h_stored = [sem(f"h_stored{i}") for i in range(2)]

        N = PAIRS * W
        UB = 2 * NU

        with nc.Block() as block:

            @block.gpsimd
            def _(pool):
                nc.gpsimd.memset(tab[:], 0.0).then_inc(tab_zero, 1)
                nc.gpsimd.memset(diff[:], 0.0).then_inc(diff_zero, 1)

            @block.sync
            def _(sp):
                sp.wait_ge(tab_zero, 1)
                for i, rev in enumerate((rev_h, rev_w)):
                    for s in range(2):
                        sp.dma_start(tab[s * D:(s + 1) * D, i, :, s:s + 1], rev.rearrange("c (r a) -> c r a", a=1),
                                     allow_slow_non_contiguous=True).then_inc(tab_loaded, 16)
                with sp.Fori(0, B) as b:
                    sp.wait_ge(product, b * UB)
                    sp.dma_start(q[:], qF.rearrange("(b o) p q -> b p o q", b=B)[b]).then_inc(q_loaded, 16)
                    sp.wait_ge(lo_set, b * UB + NU)
                    for part in range(2):
                        sp.dma_start(relW.rearrange("(b o) a r q -> b a r o q", b=B)[b, part],
                                     w_hl[:, part].bitcast(F32)).then_inc(w_stored, 16)
                    for g in range(NRP):
                        sp.wait_ge(lo_set, b * UB + NU + (g + 1) * RQ)
                        for part in range(2):
                            sp.dma_start(relH.rearrange("(b o) a r q -> b a r o q", b=B)[b, part][:, :, g * RQ * W:(g + 1) * RQ * W],
                                         h_hl[:, g % 2, part].bitcast(F32)).then_inc(h_stored[g % 2], 16)
                sp.wait_ge(w_stored, B * 2 * 16)
                for i in range(2):
                    sp.wait_ge(h_stored[i], B * NRP * 16)

            @block.tensor
            def _(pe):
                pe.wait_ge(diff_set, H)
                with pe.Fori(0, B) as b:
                    pe.wait_ge(q_loaded, (b + 1) * 16)
                    for u in range(UB):
                        kind, r = u // NU, u % NU
                        if u >= 8:
                            pe.wait_ge(lo_set, b * UB + u - 7)
                        else:
                            pe.wait_ge(lo_set, b * UB)
                        if kind == 0:
                            cols = q[:].rearrange("p o (h w) -> p o h w", w=W)[:, :, :, r]
                            win = tab[:, 1].rearrange("p r s -> p (r s)")[:, 2 * (W - 1 - r):2 * (W - 1 - r) + 2 * W]
                        else:
                            cols = q[:, :, r * W:(r + 1) * W]
                            win = diff[:, r].rearrange("p k s -> p (k s)")
                        nc.tensor.matmul(ps[u % 8][:, 0:N], win, cols, start=True, stop=True).then_inc(product, 1)

            def part_of(u, part):
                kind, r = u // NU, u % NU
                if kind == 0:
                    return w_hl[:, part].rearrange("p o (h w) -> p o h w", w=W)[:, :, :, r]
                return h_hl[:, r // RQ % 2, part, :, r % RQ * W:(r % RQ + 1) * W]

            @block.scalar
            def _(act):
                with act.Fori(0, B) as b:
                    for u in range(UB):
                        act.wait_ge(product, b * UB + u + 1)
                        if u == 0:
                            act.wait_ge(w_stored, b * 2 * 16)
                        if u >= NU and u % RQ == 0:
                            g = (u - NU) // RQ
                            act.wait_ge(h_stored[g % 2], b * (NRP * 16) + g // 2 * 32)
                        nc.scalar.activation(part_of(u, 0), ps[u % 8][:, 0:N].rearrange("p (o n) -> p o n", n=W),
                                             ACT.Copy).then_inc(hi_set, 1)

            @block.vector
            def _(dve):
                dve.wait_ge(tab_loaded, 4 * 16)
                dve.wait_ge(diff_zero, 1)
                for r in range(H):
                    for s in range(2):
                        rows = slice(s * D, (s + 1) * D)
                        ins = nc.vector.tensor_scalar(diff[rows, r, :, s], tab[rows, 0, H - 1 - r:2 * H - 1 - r, s],
                                                      tab[rows, 0, 2 * H - 2 - r, s:s + 1], None, ALU.subtract)
                    ins.then_inc(diff_set, 1)
                with dve.Fori(0, B) as b:
                    for u in range(UB):
                        dve.wait_ge(hi_set, b * UB + u + 1)
                        nc.vector.tensor_tensor(part_of(u, 1), ps[u % 8][:, 0:N].rearrange("p (o n) -> p o n", n=W),
                                                part_of(u, 0).bitcast(F32), ALU.subtract).then_inc(lo_set, 1)


def rowmax(nc, ident_d, onehot_max, qHL, kHL, relH, relW):
    with ExitStack() as ctx:
        def sb(name, shape, dt=F32):
            return ctx.enter_context(nc.sbuf_tensor("rowmax_" + name, shape, dt))

        def sem(name):
            return ctx.enter_context(nc.semaphore("rowmax_" + name))

        ident = sb("ident", [P, P])
        hot = sb("hot", [P, S])
        qs = [sb(f"q{s}", [P, KG, S], F32R) for s in range(2)]
        ks = [sb(f"k{s}", [P, S], F32R) for s in range(2)]
        part_max = sb("part_max", [P, 2, KT, KG])
        mx = sb("max", [P, 2, KT])
        neg = sb("negated", [KT, 2, P], F32R)
        ps = [ctx.enter_context(nc.psum_tensor(f"rowmax_ps{i}", [P, 2, 512], F32)) for i in range(3)]
        pt = ctx.enter_context(nc.psum_tensor("rowmax_pt", [KT, 512], F32))

        consts = sem("consts")
        hot_set = sem("hot_set")
        loaded = [sem(f"loaded{s}") for s in range(2)]
        scores = sem("scores")
        reduced = sem("reduced")
        max_set = sem("max_set")
        turned = sem("turned")
        neg_set = sem("neg_set")
        stored = [sem(f"stored{s}") for s in range(2)]

        UH = KT * KG
        LOADS = 1 + 3 * KG
        HN = GK // 2

        with nc.Block() as block:

            @block.sync
            def _(sp):
                sp.dma_start(ident[:], ident_d).then_inc(consts, 16)
                sp.dma_start(hot[D:P], onehot_max).then_inc(consts, 16)
                with sp.Fori(0, NP) as n:
                    for s in range(2):
                            sp.wait_ge(scores, n * (2 * UH))
                            sp.dma_start(ks[s][0:D].bitcast(F32), kHL[n, s * D:(s + 1) * D, 0]).then_inc(loaded[s], 16)
                            for j in range(KG):
                                dst = qs[s].bitcast(F32)
                                sp.dma_start(dst[0:D, j], qHL[n, s * D:(s + 1) * D, 0]).then_inc(loaded[s], 16)
                                sp.dma_start(dst[D:D + H, j], relH[n, 0].rearrange("(k s) q -> k s q", s=2)[:, s]
                                             ).then_inc(loaded[s], 16)
                                sp.dma_start(dst[D + H:P, j], relW[n, 0].rearrange("(k s) q -> k s q", s=2)[
                                    j * KW:(j + 1) * KW, s]).then_inc(loaded[s], 16)

            @block.tensor
            def _(pe):
                pe.wait_ge(consts, 32)
                pe.wait_ge(hot_set, 2)
                with pe.Fori(0, NP) as n:
                    for s in range(2):
                        pe.wait_ge(loaded[s], (n + 1) * (LOADS * 16))
                        for u in range(UH):
                            t, j = u // KG, u % KG
                            m = s * UH + u
                            if m >= 3:
                                pe.wait_ge(reduced, n * (2 * UH) + m - 2)
                            else:
                                pe.wait_ge(reduced, n * (2 * UH))
                            for i in range(2):
                                mm = nc.tensor.matmul(ps[m % 3][:, i, 0:HN], qs[s][:, j, t * P:(t + 1) * P],
                                                      ks[s][:, j * GK + i * HN:j * GK + (i + 1) * HN],
                                                      start=True, stop=True)
                            mm.then_inc(scores, 1)
                        pe.wait_ge(max_set, n * 2 + s + 1)
                        pe.wait_ge(neg_set, n * 2 + s)
                        nc.tensor.transpose(pt[:, 0:P], mx[:, s], ident[:]).then_inc(turned, 1)

            @block.scalar
            def _(act):
                with act.Fori(0, NP) as n:
                    for s in range(2):
                            act.wait_ge(neg_set, n * 2 + s + 1)
                            act.dma_start(relH[n, 1, 2 * (H - 1) + s].rearrange("(t p) -> t p", p=P),
                                          neg[:, s].bitcast(F32)).then_inc(stored[s], 16)
                for s in range(2):
                    act.wait_ge(stored[s], NP * 16)

            @block.vector
            def _(dve):
                dve.wait_ge(consts, 32)
                for s in range(2):
                    nc.vector.tensor_copy(ks[s][D:P], hot[D:P]).then_inc(hot_set, 1)
                with dve.Fori(0, NP) as n:
                    for s in range(2):
                        for u in range(UH):
                            m = s * UH + u
                            dve.wait_ge(scores, n * (2 * UH) + m + 1)
                            nc.vector.tensor_reduce(part_max[:, s, u // KG, u % KG:u % KG + 1], ps[m % 3][:, :, 0:HN],
                                                    mybir.AxisListType.XY, ALU.max).then_inc(reduced, 1)
                        dve.wait_ge(reduced, n * (2 * UH) + (s + 1) * UH)
                        nc.vector.tensor_reduce(mx[:, s], part_max[:, s], AX_X, ALU.max).then_inc(max_set, 1)
                        dve.wait_ge(turned, n * 2 + s + 1)
                        dve.wait_ge(stored[s], n * 16)
                        nc.vector.tensor_scalar(neg[:, s], pt[:, 0:P], -1.0, None, ALU.mult).then_inc(neg_set, 1)


SLOTS = QC * KT
NPB = 4


def attend(nc, hot2_d, hot3_d, qHL, kHL, vD, relH, relW, aHL):
    with ExitStack() as ctx:
        def sb(name, shape, dt=F32):
            return ctx.enter_context(nc.sbuf_tensor("attend_" + name, shape, dt))

        def sem(name):
            return ctx.enter_context(nc.semaphore("attend_" + name))

        hot = sb("hot", [P, 2, S])
        qs = [sb(f"q{s}", [P, 3, S], F32R) for s in range(2)]
        ks = [sb(f"k{s}", [P, 2, S], F32R) for s in range(2)]
        k3 = sb("k_hot", [P, S], F32R)
        v = sb("v", [P, KT, P])
        pe_ones = sb("ones", [P, D])
        prob = sb("prob", [P, NPB, 2, QMAX])
        acc = sb("prob_sum", [P, 2, 2, QMAX])
        inv = sb("inverse", [P, QMAX])
        o32 = sb("o", [P, QMAX])
        ohl = sb("o_split", [P, 2, 2, QMAX], F32R)
        psS = [ctx.enter_context(nc.psum_tensor(f"attend_s{i}", [P, 2, 512], F32)) for i in range(2)]
        psO = [ctx.enter_context(nc.psum_tensor(f"attend_o{i}", [P, 512], F32)) for i in range(2)]
        psL = ctx.enter_context(nc.psum_tensor("attend_l", [P, 512], F32))

        hot_loaded = sem("hot_loaded")
        hot_set = sem("hot_set")
        ones_set = sem("ones_set")
        q_loaded = [sem(f"q_loaded{c}") for c in range(QC)]
        kv_loaded = [sem(f"kv_loaded{j}") for j in range(KG)]
        scores = sem("scores")
        exped = sem("exped")
        weighed = sem("weighed")
        added = sem("added")
        summed = sem("summed")
        inv_set = sem("inv_set")
        o_set = sem("o_set")
        ohi_set = sem("ohi_set")
        olo_set = sem("olo_set")
        stored = [sem(f"stored{i}") for i in range(2)]

        QL, KL = 16, 7
        TJ = KT // KG

        def load_q(sp, n, c):
            cols = slice(Q0[c], Q0[c] + QN[c])
            for s in range(2):
                rows = slice(s * D, (s + 1) * D)
                d = qs[s].bitcast(F32)
                rh = [relH[n, a].rearrange("(k s) q -> k s q", s=2)[:, s, cols] for a in range(2)]
                rw = [relW[n, a].rearrange("(k s) q -> k s q", s=2)[:, s, cols] for a in range(2)]
                for dst, src in ((d[0:D, 0, cols], qHL[n, rows, 0, cols]),
                                 (d[D:P, 0, cols], qHL[n, rows, 0, cols]),
                                 (d[0:D, 1, cols], qHL[n, rows, 1, cols]),
                                 (d[D:D + W, 1, cols], rw[0]),
                                 (d[D + W:P, 1, cols], rh[0][0:16]),
                                 (d[0:W, 2, cols], rw[1]),
                                 (d[W:W + H - 16, 2, cols], rh[0][16:H]),
                                 (d[W + H - 16:P, 2, cols], rh[1])):
                    sp.dma_start(dst, src).then_inc(q_loaded[c], 16)

        def load_kv(sp, n, j):
            cols = slice(j * GK, (j + 1) * GK)
            for s in range(2):
                rows = slice(s * D, (s + 1) * D)
                d = ks[s].bitcast(F32)
                for dst, part in ((d[0:D, 0, cols], 0), (d[D:P, 0, cols], 1), (d[0:D, 1, cols], 0)):
                    sp.dma_start(dst, kHL[n, rows, part, cols]).then_inc(kv_loaded[j], 16)
            sp.dma_start(v[:, j * TJ:(j + 1) * TJ], vD[n][:, j * TJ:(j + 1) * TJ]).then_inc(kv_loaded[j], 16)

        with nc.Block() as block:

            @block.sync
            def _(sp):
                sp.dma_start(hot[D:P, 0], hot2_d).then_inc(hot_loaded, 16)
                sp.dma_start(hot[:, 1], hot3_d).then_inc(hot_loaded, 16)
                load_kv(sp, 0, 0)
                load_q(sp, 0, 0)
                for j in range(1, KG):
                    load_kv(sp, 0, j)
                for c in range(1, QC):
                    load_q(sp, 0, c)
                with sp.Fori(0, NP - 1) as n:
                    for c in range(QC - 1):
                        sp.wait_ge(scores, n * SLOTS + (c + 1) * KT)
                        load_q(sp, n + 1, c)
                    for j in range(KG):
                        sp.wait_ge(weighed, n * SLOTS + (QC - 1) * KT + (j + 1) * TJ)
                        load_kv(sp, n + 1, j)
                    sp.wait_ge(scores, (n + 1) * SLOTS)
                    load_q(sp, n + 1, QC - 1)

            @block.gpsimd
            def _(pool):
                nc.gpsimd.memset(pe_ones[:], 1.0).then_inc(ones_set, 1)
                with pool.Fori(0, NP) as n:
                    for c in range(QC):
                        pool.wait_ge(olo_set, n * QC + c + 1)
                        pool.dma_start(aHL[n][:, :, Q0[c]:Q0[c] + QN[c]],
                                       ohl[:, c % 2, :, 0:QN[c]].bitcast(F32)).then_inc(stored[c % 2], 16)
                pool.wait_ge(stored[0], NP * 3 * 16)
                pool.wait_ge(stored[1], NP * 2 * 16)

            @block.tensor
            def _(pe):
                pe.wait_ge(hot_set, 3)
                pe.wait_ge(ones_set, 1)
                with pe.Fori(0, NP) as n:

                    def weigh(m):
                        c, t = m // KT, m % KT
                        pe.wait_ge(exped, n * SLOTS + m + 1)
                        if t == 0:
                            pe.wait_ge(o_set, n * QC + max(c - 1, 0))
                        for s in range(2):
                            mm = nc.tensor.matmul(psO[c % 2][s * D:(s + 1) * D, 0:QN[c]], v[:, t, s * D:(s + 1) * D],
                                                  prob[:, m % NPB, s, 0:QN[c]], start=t == 0, stop=t == KT - 1)
                        mm.then_inc(weighed, 1)

                    def sum_probs(c):
                        pe.wait_ge(added, n * SLOTS + (c + 1) * KT)
                        pe.wait_ge(inv_set, n * QC + c)
                        for s in range(2):
                            mm = nc.tensor.matmul(psL[s * D:(s + 1) * D, 0:QN[c]], pe_ones[:],
                                                  acc[:, c % 2, s, 0:QN[c]], start=True, stop=True)
                        mm.then_inc(summed, 1)

                    for m in range(SLOTS):
                        c, t = m // KT, m % KT
                        if t == 0:
                            pe.wait_ge(q_loaded[c], (n + 1) * (QL * 16))
                        if c == 0 and t % TJ == 0:
                            pe.wait_ge(kv_loaded[t // TJ], (n + 1) * (KL * 16))
                        pe.wait_ge(exped, n * SLOTS + max(m - 1, 0))
                        cols = slice(Q0[c], Q0[c] + QN[c])
                        keys = slice(t * P, (t + 1) * P)
                        for s in range(2):
                            out = psS[m % 2][:, s, 0:QN[c]]
                            nc.tensor.matmul(out, ks[s][:, 0, keys], qs[s][:, 0, cols], start=True, stop=False)
                            nc.tensor.matmul(out, ks[s][:, 1, keys], qs[s][:, 1, cols], start=False, stop=False)
                            mm = nc.tensor.matmul(out, k3[:, keys], qs[s][:, 2, cols], start=False, stop=True)
                        mm.then_inc(scores, 1)
                        if m >= 1:
                            weigh(m - 1)
                        if c >= 1 and t == 2:
                            sum_probs(c - 1)
                    weigh(SLOTS - 1)
                    sum_probs(QC - 1)

            @block.scalar
            def _(act):
                with act.Fori(0, NP) as n:
                    for m in range(SLOTS):
                        c = m // KT
                        act.wait_ge(scores, n * SLOTS + m + 1)
                        act.wait_ge(weighed, n * SLOTS + max(m - NPB + 1, 0))
                        act.wait_ge(added, n * SLOTS + max(m - NPB + 1, 0))
                        nc.scalar.activation(prob[:, m % NPB, :, 0:QN[c]], psS[m % 2][:, :, 0:QN[c]],
                                             ACT.Exp).then_inc(exped, 1)

            @block.vector
            def _(dve):
                dve.wait_ge(hot_loaded, 32)
                for s in range(2):
                    nc.vector.tensor_copy(ks[s][D:P, 1], hot[D:P, 0]).then_inc(hot_set, 1)
                nc.vector.tensor_copy(k3[:], hot[:, 1]).then_inc(hot_set, 1)
                with dve.Fori(0, NP) as n:

                    def normalise(c):
                        w = slice(0, QN[c])
                        dve.wait_ge(summed, n * QC + c + 1)
                        nc.vector.reciprocal(inv[:, w], psL[:, w]).then_inc(inv_set, 1)
                        dve.wait_ge(inv_set, n * QC + c + 1)
                        dve.wait_ge(weighed, n * SLOTS + (c + 1) * KT)
                        nc.vector.tensor_tensor(o32[:, w], psO[c % 2][:, w], inv[:, w], ALU.mult).then_inc(o_set, 1)
                        dve.wait_ge(o_set, n * QC + c + 1)
                        dve.wait_ge(stored[c % 2], n * ((3 - c % 2) * 16) + c // 2 * 16)
                        nc.vector.tensor_copy(ohl[:, c % 2, 0, w], o32[:, w]).then_inc(ohi_set, 1)
                        dve.wait_ge(ohi_set, n * QC + c + 1)
                        nc.vector.tensor_tensor(ohl[:, c % 2, 1, w], o32[:, w], ohl[:, c % 2, 0, w].bitcast(F32),
                                                ALU.subtract).then_inc(olo_set, 1)

                    for m in range(SLOTS):
                        c, t = m // KT, m % KT
                        if t > 0:
                            total = acc[:, c % 2, :, 0:QN[c]]
                            dve.wait_ge(exped, n * SLOTS + m + 1)
                            if t == 1:
                                dve.wait_ge(summed, n * QC + max(c - 1, 0))
                                nc.vector.tensor_tensor(total, prob[:, (m - 1) % NPB, :, 0:QN[c]],
                                                        prob[:, m % NPB, :, 0:QN[c]], ALU.add).then_inc(added, 2)
                            else:
                                dve.wait_ge(added, n * SLOTS + m)
                                nc.vector.tensor_tensor(total, total, prob[:, m % NPB, :, 0:QN[c]],
                                                        ALU.add).then_inc(added, 1)
                        if c >= 1 and t == 3:
                            normalise(c - 1)
                    normalise(QC - 1)


TR = 2
TT = TR * W
NTT = H // TR
FR = KWF * RI
CH = C // 2
TPC = NTT // KG


def out_project(nc, x, proj_w, proj_b, row_dft_d, aHL, x1D, rowsD):
    with ExitStack() as ctx:
        def sb(name, shape, dt=F32):
            return ctx.enter_context(nc.sbuf_tensor("out_" + name, shape, dt))

        def sem(name):
            return ctx.enter_context(nc.semaphore("out_" + name))

        a = sb("attention", [P, KG, 2, CT, GK], F32R)
        wraw = sb("w_raw", [P, 2, CT, CH])
        wp = sb("w_split", [P, 2, CT, C], F32R)
        pb = sb("bias", [TT, C])
        dft = sb("row_dft", [TT, TR * FR])
        xin = sb("x", [TT, 4, C])
        xb = sb("x_plus_bias", [TT, 2, C])
        x1 = sb("x1", [TT, 2, C])
        f = sb("spectrum", [TR * FR, 2, C])
        psA = [ctx.enter_context(nc.psum_tensor(f"out_a{i}", [TT, 2, 512], F32)) for i in range(2)]
        psF = [ctx.enter_context(nc.psum_tensor(f"out_f{i}", [TR * FR, 2, 512], F32)) for i in range(2)]

        consts = sem("consts")
        w_loaded = sem("w_loaded")
        w_hi = sem("w_hi")
        w_set = sem("w_set")
        a_loaded = [sem(f"a_loaded{j}") for j in range(KG)]
        x_loaded = [sem(f"x_loaded{i}") for i in range(4)]
        biased = sem("biased")
        projected = sem("projected")
        x1_set = sem("x1_set")
        transformed = sem("transformed")
        f_set = sem("f_set")
        x1_stored = [sem(f"x1_stored{i}") for i in range(2)]
        f_stored = [sem(f"f_stored{i}") for i in range(2)]

        x_view = x.rearrange("b (t p) c -> b t p c", p=TT)
        x1_view = x1D.rearrange("b (t p) c -> b t p c", p=TT)
        f_view = rowsD.rearrange("b (t h) k r c -> b t (h k r) c", h=TR)
        a_view = aHL.rearrange("(b o) p i q -> b i p o q", b=B)

        with nc.Block() as block:

            @block.sync
            def _(sp):
                for i in range(2):
                    sp.dma_start(wraw[:, i], proj_w.rearrange("(t p) n -> p t n", p=P)[:, :, i * CH:(i + 1) * CH]
                                 ).then_inc(w_loaded, 16)
                sp.dma_start(pb[:], proj_b.rearrange("(a c) -> a c", a=1).broadcast_to([TT, C])).then_inc(consts, 16)
                sp.dma_start(dft[:], row_dft_d).then_inc(consts, 16)
                for b in range(B):
                    for t in range(NTT):
                        n = b * NTT + t
                        if t % TPC == 0:
                            j = t // TPC
                            if b:
                                sp.wait_ge(projected, (b - 1) * NTT + (j + 1) * TPC)
                            for i in range(2):
                                sp.dma_start(a[:, j, i].bitcast(F32), a_view[b, i][:, :, j * GK:(j + 1) * GK]
                                             ).then_inc(a_loaded[j], 16)
                        if n >= 4:
                            sp.wait_ge(biased, n - 3)
                        sp.dma_start(xin[:, n % 4], x_view[b, t]).then_inc(x_loaded[n % 4], 16)

            @block.gpsimd
            def _(pool):
                pool.wait_ge(consts, 32)
                with pool.Fori(0, B) as b:
                    for t in range(NTT):
                        pool.wait_ge(x_loaded[t % 4], b * (NTT // 4 * 16) + (t // 4 + 1) * 16)
                        pool.wait_ge(x1_set, b * NTT + max(t - 1, 0))
                        nc.gpsimd.tensor_tensor(xb[:, t % 2], xin[:, t % 4], pb[:], ALU.add).then_inc(biased, 1)

            @block.tensor
            def _(pe):
                pe.wait_ge(consts, 32)
                pe.wait_ge(w_set, 2)
                with pe.Fori(0, B) as b:

                    def transform(t):
                        pe.wait_ge(x1_set, b * NTT + t + 1)
                        pe.wait_ge(f_set, b * NTT + max(t - 1, 0))
                        for i in range(2):
                            mm = nc.tensor.matmul(psF[t % 2][:, i, 0:CH], dft[:], x1[:, t % 2, i * CH:(i + 1) * CH],
                                                  start=True, stop=True)
                        mm.then_inc(transformed, 1)

                    for t in range(NTT):
                        j, u = t // TPC, t % TPC
                        if u == 0:
                            pe.wait_ge(a_loaded[j], (b + 1) * 32)
                        pe.wait_ge(x1_set, b * NTT + max(t - 1, 0))
                        for i in range(2):
                            k = 0
                            for ap, wq in ((0, 0), (0, 1), (1, 0)):
                                for ct in range(CT):
                                    mm = nc.tensor.matmul(psA[t % 2][:, i, 0:CH], a[:, j, ap, ct, u * TT:(u + 1) * TT],
                                                          wp[:, wq, ct, i * CH:(i + 1) * CH],
                                                          start=k == 0, stop=k == 3 * CT - 1)
                                    k += 1
                        mm.then_inc(projected, 1)
                        if t >= 1:
                            transform(t - 1)
                    transform(NTT - 1)

            @block.vector
            def _(dve):
                dve.wait_ge(w_loaded, 32)
                for i in range(2):
                    cols = slice(i * CH, (i + 1) * CH)
                    nc.vector.tensor_copy(wp[:, 0, :, cols], wraw[:, i]).then_inc(w_hi, 1)
                    dve.wait_ge(w_hi, i + 1)
                    nc.vector.tensor_tensor(wp[:, 1, :, cols], wraw[:, i], wp[:, 0, :, cols].bitcast(F32),
                                            ALU.subtract).then_inc(w_set, 1)
                with dve.Fori(0, B) as b:
                    for t in range(NTT):
                        dve.wait_ge(projected, b * NTT + t + 1)
                        dve.wait_ge(biased, b * NTT + t + 1)
                        dve.wait_ge(x1_stored[t % 2], b * (NTT // 2 * 16) + t // 2 * 16)
                        dve.wait_ge(transformed, b * NTT + max(t - 1, 0))
                        nc.vector.tensor_tensor(x1[:, t % 2].rearrange("p (i c) -> p i c", i=2),
                                                psA[t % 2][:, :, 0:CH],
                                                xb[:, t % 2].rearrange("p (i c) -> p i c", i=2),
                                                ALU.add).then_inc(x1_set, 1)

            @block.scalar
            def _(act):
                with act.Fori(0, B) as b:
                    for t in range(NTT):
                        act.wait_ge(x1_set, b * NTT + t + 1)
                        act.dma_start(x1_view[b, t], x1[:, t % 2]).then_inc(x1_stored[t % 2], 16)
                        act.wait_ge(transformed, b * NTT + t + 1)
                        act.wait_ge(f_stored[t % 2], b * (NTT // 2 * 16) + t // 2 * 16)
                        nc.scalar.activation(f[:, t % 2].rearrange("p (i c) -> p i c", i=2), psF[t % 2][:, :, 0:CH],
                                             ACT.Copy).then_inc(f_set, 1)
                        act.wait_ge(f_set, b * NTT + t + 1)
                        act.dma_start(f_view[b, t], f[:, t % 2]).then_inc(f_stored[t % 2], 16)
                for i in range(2):
                    act.wait_ge(x1_stored[i], B * NTT // 2 * 16)
                    act.wait_ge(f_stored[i], B * NTT // 2 * 16)


NG = (KWF + 1) // 2
NF = KWF * H
NQ = 3
FQ = NF // NQ
GB = BS // GC
BH = NB // 2


def spectrum(nc, w1_d, b1_d, w2_d, b2_d, col_dft_d, icol_dft_d, indb_d, indbT_d, rowsD, specD):
    with ExitStack() as ctx:
        def sb(name, shape, dt=F32):
            return ctx.enter_context(nc.sbuf_tensor("spec_" + name, shape, dt))

        def sem(name):
            return ctx.enter_context(nc.semaphore("spec_" + name))

        col = sb("col_dft", [RI * H, RI * H])
        icol = sb("icol_dft", [2 * H, 3, 2 * H])
        w1 = sb("w1", [BS, NB, 3, BS])
        w1s = sb("w1_scaled", [BS, NB, 3, BS])
        w2 = sb("w2", [BS, NB, 2, 2, BS])
        b1 = sb("b1", [BS, NB, RI])
        b2 = sb("b2", [2 * H, NB, RI, BS])
        indb = sb("indb", [BS, GB])
        indbT = sb("indbT", [GB, BS])
        rows = sb("rows", [RI * H, 3, C])
        xf = sb("xf", [BS, NB, RI, KWF, H])
        dc = sb("dc", [BS, NB])
        dcm = sb("dc_centred", [BS, NB])
        energy = sb("energy", [BS, 2, NB])
        power = sb("power", [BS, NB])
        total = sb("total", [BS, NB])
        gsum = sb("group_sum", [GB, NB])
        gvar = sb("group_var", [GB, NB])
        gstd = sb("group_std", [GB, NB])
        grstd = sb("group_rstd", [GB, NB])
        rstd = sb("rstd", [BS, NB])
        epst = sb("eps", [GB, 1])
        hid = sb("hidden", [BS, 2, RI, NF])
        pre = sb("pre", [2 * H, 2, 2, RI, BS])
        clamped = sb("clamped", [2 * H, 2, 2, RI, BS])
        y = sb("y", [2 * H, NG, RI, CH])
        g = sb("g", [2 * H, 2, RI, CH])
        ps = [ctx.enter_context(nc.psum_tensor(f"spec_ps{i}", [P, 512], F32)) for i in range(8)]

        consts = sem("consts")
        ready = sem("ready")
        rows_loaded = [sem(f"rows_loaded{i}") for i in range(3)]
        column = sem("column")
        col_lo = sem("col_lo")
        col_hi = sem("col_hi")
        dc_set = sem("dc_set")
        dc_zero = sem("dc_zero")
        squared = sem("squared")
        group_pe = sem("group_pe")
        gsum_set = sem("gsum_set")
        dcm_set = sem("dcm_set")
        power_set = sem("power_set")
        sq_set = sem("sq_set")
        total_set = sem("total_set")
        gvar_set = sem("gvar_set")
        gstd_set = sem("gstd_set")
        grstd_set = sem("grstd_set")
        rstd_set = sem("rstd_set")
        normed = sem("normed")
        layer1 = sem("layer1")
        gelued = sem("gelued")
        layer2 = sem("layer2")
        pre_set = sem("pre_set")
        clamp_set = sem("clamp_set")
        y_set = sem("y_set")
        inv_re = sem("inv_re")
        inv_im = sem("inv_im")
        g_re = sem("g_re")
        g_im = sem("g_im")
        g_stored = [sem(f"g_stored{i}") for i in range(2)]

        U1 = NB * NQ * RI
        G2 = (NG + 1) // 2
        U2 = NB * G2
        U3 = 2 * NG
        NCONST = 14

        spec_view = specD.rearrange("b h k r c -> b k h r c")

        def kws(i):
            return min(2, KWF - 2 * i)

        def stores_before(b, u):
            return b * KWF + sum(kws(v % NG) for v in range(u) if v % 2 == u % 2)

        with nc.Block() as block:

            @block.sync
            def _(sp):
                for dst, src in ((col[:], col_dft_d), (icol[:], icol_dft_d), (indb[:], indb_d), (indbT[:], indbT_d),
                                 (b1[:], b1_d),
                                 (b2[:].rearrange("p n r c -> p (n r c)"),
                                  b2_d.rearrange("(a c) -> a c", a=1).broadcast_to([2 * H, NB * RI * BS])),
                                 (w1[:, :, 0], w1_d[0].rearrange("n i o -> i n o")),
                                 (w1[:, :, 1], w1_d[1].rearrange("n i o -> i n o")),
                                 (w2[:, :, 0, 0], w2_d[0].rearrange("n i o -> i n o")),
                                 (w2[:, :, 0, 1], w2_d[1].rearrange("n i o -> i n o")),
                                 (w2[:, :, 1, 1], w2_d[0].rearrange("n i o -> i n o"))):
                    sp.dma_start(dst, src).then_inc(consts, 16)
                for b in range(B):
                    for k in range(KWF):
                        n = b * KWF + k
                        if n >= 3:
                            sp.wait_ge(column, n - 2)
                        for r in range(RI):
                            sp.dma_start(rows[r * H:(r + 1) * H, n % 3], rowsD[b, :, k, r]).then_inc(rows_loaded[n % 3], 16)

            @block.gpsimd
            def _(pool):
                with pool.Fori(0, B) as b:
                    for u in range(U3):
                        half, i = u // NG, u % NG
                        m = kws(i)
                        pool.wait_ge(g_re, b * U3 + u + 1)
                        pool.wait_ge(g_im, b * U3 + u + 1)
                        for k in range(m):
                            pool.dma_start(spec_view[b, 2 * i + k][:, :, half * CH:(half + 1) * CH],
                                           g[k * H:(k + 1) * H, u % 2]).then_inc(g_stored[u % 2], 16)
                for i in range(2):
                    pool.wait_ge(g_stored[i], B * 2 * KWF // 2 * 16)

            @block.tensor
            def _(pe):
                pe.wait_ge(consts, 11 * 16)
                pe.wait_ge(ready, 3)
                for b in range(B):
                    for k in range(KWF):
                        n = b * KWF + k
                        pe.wait_ge(rows_loaded[n % 3], (n // 3 + 1) * 32)
                        if n >= 2:
                            pe.wait_ge(col_lo, n - 1)
                            pe.wait_ge(col_hi, n - 1)
                        if k < 2:
                            pe.wait_ge(gelued, b * U1)
                        for blk in range(NB):
                            bank = ps[2 * (n % 2) + blk // BH]
                            mm = nc.tensor.matmul(bank[0:BS, blk % BH * (RI * H):(blk % BH + 1) * (RI * H)],
                                                  rows[:, n % 3, blk * BS:(blk + 1) * BS], col[:],
                                                  start=True, stop=True)
                        mm.then_inc(column, 1)
                    pe.wait_ge(dc_set, b + 1)
                    pe.wait_ge(pre_set, b * U2)
                    nc.tensor.matmul(ps[4][0:GB, 0:NB], indb[:], dc[:], start=True, stop=True).then_inc(group_pe, 1)
                    pe.wait_ge(gsum_set, b + 1)
                    nc.tensor.matmul(ps[5][0:BS, 0:NB], indbT[:], gsum[:], start=True, stop=True).then_inc(group_pe, 1)
                    pe.wait_ge(total_set, b + 1)
                    pe.wait_ge(g_re, b * U3)
                    nc.tensor.matmul(ps[6][0:GB, 0:NB], indb[:], total[:], start=True, stop=True).then_inc(group_pe, 1)
                    pe.wait_ge(grstd_set, b + 1)
                    pe.wait_ge(g_im, b * U3)
                    nc.tensor.matmul(ps[7][0:BS, 0:NB], indbT[:], grstd[:], start=True, stop=True).then_inc(group_pe, 1)
                    pe.wait_ge(normed, b + 1)

                    def first(blk):
                        for q in range(NQ):
                            for r in range(RI):
                                u = (blk * NQ + q) * RI + r
                                if u >= 4:
                                    pe.wait_ge(gelued, b * U1 + u - 3)
                                elif u == 0:
                                    pe.wait_ge(col_lo, (b + 1) * KWF)
                                    pe.wait_ge(col_hi, (b + 1) * KWF)
                                xs = [xf[:, blk, i].rearrange("p k h -> p (k h)")[:, q * FQ:(q + 1) * FQ] for i in range(RI)]
                                nc.tensor.matmul(ps[u % 4][0:BS, 0:FQ], w1s[:, blk, 0], xs[r], start=True, stop=False)
                                nc.tensor.matmul(ps[u % 4][0:BS, 0:FQ], w1s[:, blk, 2 - r], xs[1 - r],
                                                 start=False, stop=True).then_inc(layer1, 1)

                    def second(blk):
                        pe.wait_ge(gelued, b * U1 + (blk + 1) * (NQ * RI))
                        for i in range(NG):
                            u = blk * G2 + i // 2
                            if i % 2 == 0 and u >= 2:
                                pe.wait_ge(pre_set, b * U2 + u - 1)
                            m = kws(i) * H
                            out = ps[4 + u % 2][0:m, i % 2 * (RI * BS):(i % 2 + 1) * (RI * BS)]
                            for r in range(RI):
                                mm = nc.tensor.matmul(out, hid[:, blk % 2, r, 2 * i * H:2 * i * H + m],
                                                      w2[:, blk, r].rearrange("p a o -> p (a o)"),
                                                      start=r == 0, stop=r == RI - 1)
                            if i % 2 or i == NG - 1:
                                mm.then_inc(layer2, 1)

                    def inverse(half):
                        for i in range(NG):
                            u = half * NG + i
                            m = kws(i) * H
                            if i % 2 == 0:
                                pe.wait_ge(y_set, b * U2 + (half * BH + BH - 1) * G2 + i // 2 + 1)
                            for r, bank, done, read in ((0, ps[6], inv_re, g_re), (1, ps[7], inv_im, g_im)):
                                pe.wait_ge(read, b * U3 + u)
                                nc.tensor.matmul(bank[0:m, 0:CH], icol[0:m, 0, 0:m], y[0:m, i, r], start=True, stop=False)
                                nc.tensor.matmul(bank[0:m, 0:CH], icol[0:m, 2 - r, 0:m], y[0:m, i, 1 - r],
                                                 start=False, stop=True).then_inc(done, 1)

                    first(0)
                    for blk in range(1, NB):
                        first(blk)
                        second(blk - 1)
                        if blk == BH:
                            inverse(0)
                    second(NB - 1)
                    inverse(1)

            @block.scalar
            def _(act):
                act.wait_ge(consts, 11 * 16)
                act.wait_ge(ready, 3)
                for b in range(B):
                    for k in range(KWF):
                        n = b * KWF + k
                        act.wait_ge(column, n + 1)
                        if k == 0:
                            act.wait_ge(layer1, b * U1)
                        nc.scalar.activation(xf[:, 0:BH, :, k],
                                             ps[2 * (n % 2)][0:BS, 0:CH].rearrange("p (n r h) -> p n r h", r=RI, h=H),
                                             ACT.Copy).then_inc(col_lo, 1)
                    act.wait_ge(dc_zero, b + 1)
                    act.wait_ge(layer2, b * U2)
                    for blk in range(NB):
                        nc.scalar.activation(hid[:, 0].rearrange("p r f -> p (r f)")[:, 0:RI * (KWF - 2) * H].rearrange(
                            "p (r k h) -> p r k h", r=RI, h=H), xf[:, blk, :, 1:KWF - 1], ACT.Square,
                            accum_out=energy[:, 0, blk:blk + 1]).then_inc(squared, 1)
                        nc.scalar.activation(hid[:, 1].rearrange("p r f -> p (r f)")[:, 0:RI * 2 * H].rearrange(
                            "p (r k h) -> p r k h", r=RI, h=H), xf[:, blk, :, 0:KWF:KWF - 1], ACT.Square,
                            accum_out=energy[:, 1, blk:blk + 1]).then_inc(squared, 1)
                        act.wait_ge(squared, b * (2 * NB) + 2 * blk + 2)
                    act.wait_ge(gvar_set, b + 1)
                    nc.scalar.activation(gstd[:], gvar[:], ACT.Sqrt, bias=epst[:]).then_inc(gstd_set, 1)

                    def gelu(blk):
                        for q in range(NQ):
                            for r in range(RI):
                                u = (blk * NQ + q) * RI + r
                                act.wait_ge(layer1, b * U1 + u + 1)
                                if q == 0 and r == 0 and blk >= 2:
                                    act.wait_ge(layer2, b * U2 + (blk - 1) * G2)
                                nc.scalar.activation(hid[:, blk % 2, r, q * FQ:(q + 1) * FQ], ps[u % 4][0:BS, 0:FQ],
                                                     ACT.Gelu, bias=b1[:, blk, r:r + 1]).then_inc(gelued, 1)

                    def evacuate(half):
                        for i in range(NG):
                            u = half * NG + i
                            m = kws(i) * H
                            act.wait_ge(inv_re, b * U3 + u + 1)
                            act.wait_ge(g_stored[u % 2], stores_before(b, u) * 16)
                            nc.scalar.activation(g[0:m, u % 2, 0], ps[6][0:m, 0:CH], ACT.Copy).then_inc(g_re, 1)

                    for blk in range(NB):
                        gelu(blk)
                        if blk == BH:
                            evacuate(0)
                    evacuate(1)

            @block.vector
            def _(dve):
                dve.wait_ge(consts, 11 * 16)
                nc.vector.memset(epst[:], EPS).then_inc(ready, 1)
                nc.vector.tensor_scalar(w1[:, :, 2], w1[:, :, 1], -1.0, None, ALU.mult).then_inc(ready, 1)
                nc.vector.tensor_scalar(w2[:, :, 1, 0], w2[:, :, 0, 1], -1.0, None, ALU.mult).then_inc(ready, 1)
                dve.wait_ge(ready, 3)
                for b in range(B):
                    for k in range(KWF):
                        n = b * KWF + k
                        dve.wait_ge(column, n + 1)
                        if k == 0:
                            dve.wait_ge(layer1, b * U1)
                        nc.vector.tensor_copy(xf[:, BH:NB, :, k],
                                              ps[2 * (n % 2) + 1][0:BS, 0:CH].rearrange("p (n r h) -> p n r h", r=RI, h=H)
                                              ).then_inc(col_hi, 1)
                    dve.wait_ge(col_lo, (b + 1) * KWF)
                    dve.wait_ge(col_hi, (b + 1) * KWF)
                    nc.vector.tensor_copy(dc[:], xf[:, :, 0, 0, 0]).then_inc(dc_set, 1)
                    dve.wait_ge(dc_set, b + 1)
                    nc.vector.memset(xf[:, :, 0, 0, 0:1], 0.0).then_inc(dc_zero, 1)
                    dve.wait_ge(group_pe, 4 * b + 1)
                    nc.vector.tensor_scalar(gsum[:], ps[4][0:GB, 0:NB], 1.0 / GC, None, ALU.mult).then_inc(gsum_set, 1)
                    dve.wait_ge(group_pe, 4 * b + 2)
                    nc.vector.tensor_tensor(dcm[:], dc[:], ps[5][0:BS, 0:NB], ALU.subtract).then_inc(dcm_set, 1)
                    dve.wait_ge(squared, (b + 1) * (2 * NB))
                    nc.vector.scalar_tensor_tensor(out=power[:], in0=energy[:, 0], scalar=2.0, in1=energy[:, 1],
                                                   op0=ALU.mult, op1=ALU.add).then_inc(power_set, 1)
                    dve.wait_ge(dcm_set, b + 1)
                    nc.vector.tensor_tensor(total[:], dcm[:], dcm[:], ALU.mult).then_inc(sq_set, 1)
                    dve.wait_ge(power_set, b + 1)
                    dve.wait_ge(sq_set, b + 1)
                    nc.vector.tensor_tensor(total[:], total[:], power[:], ALU.add).then_inc(total_set, 1)
                    dve.wait_ge(group_pe, 4 * b + 3)
                    nc.vector.tensor_scalar(gvar[:], ps[6][0:GB, 0:NB], 1.0 / (GC * S), None, ALU.mult).then_inc(gvar_set, 1)
                    dve.wait_ge(gstd_set, b + 1)
                    nc.vector.reciprocal(grstd[:], gstd[:]).then_inc(grstd_set, 1)
                    dve.wait_ge(group_pe, 4 * b + 4)
                    nc.vector.tensor_copy(rstd[:], ps[7][0:BS, 0:NB]).then_inc(rstd_set, 1)
                    dve.wait_ge(rstd_set, b + 1)
                    nc.vector.tensor_copy(xf[:, :, 0, 0, 0], dcm[:])
                    for blk in range(NB):
                        ins = nc.vector.tensor_scalar(w1s[:, blk], w1[:, blk], rstd[:, blk:blk + 1], None, ALU.mult)
                    ins.then_inc(normed, 1)

                    def shrink(blk):
                        for j in range(G2):
                            u = blk * G2 + j
                            w = min(2, NG - 2 * j)
                            m = kws(2 * j) * H
                            bank = ps[4 + u % 2][0:m, 0:w * RI * BS].rearrange("p (i r c) -> p i r c", r=RI, c=BS)
                            bias = b2[0:m, blk].rearrange("p (a r) c -> p a r c", a=1).broadcast_to([m, w, RI, BS])
                            dve.wait_ge(layer2, b * U2 + u + 1)
                            nc.vector.tensor_tensor(pre[0:m, u % 2, 0:w], bank, bias, ALU.add).then_inc(pre_set, 1)
                            dve.wait_ge(pre_set, b * U2 + u + 1)
                            nc.vector.tensor_scalar(clamped[0:m, u % 2, 0:w], pre[0:m, u % 2, 0:w], -SPARSITY, SPARSITY,
                                                    ALU.max, ALU.min).then_inc(clamp_set, 1)
                            dve.wait_ge(clamp_set, b * U2 + u + 1)
                            if blk % BH == 0:
                                dve.wait_ge(inv_im, b * U3 + (blk // BH) * NG)
                            nc.vector.tensor_tensor(y[0:m, 2 * j:2 * j + w, :, blk % BH * BS:(blk % BH + 1) * BS],
                                                    pre[0:m, u % 2, 0:w], clamped[0:m, u % 2, 0:w],
                                                    ALU.subtract).then_inc(y_set, 1)

                    def evacuate(half):
                        for i in range(NG):
                            u = half * NG + i
                            m = kws(i) * H
                            dve.wait_ge(inv_im, b * U3 + u + 1)
                            dve.wait_ge(g_stored[u % 2], stores_before(b, u) * 16)
                            nc.vector.tensor_copy(g[0:m, u % 2, 1], ps[7][0:m, 0:CH]).then_inc(g_im, 1)

                    for blk in range(NB):
                        shrink(blk)
                        if blk % BH == BH - 1:
                            evacuate(blk // BH)


def image(nc, irow_dft_d, x1D, specD, out):
    with ExitStack() as ctx:
        def sb(name, shape, dt=F32):
            return ctx.enter_context(nc.sbuf_tensor("image_" + name, shape, dt))

        def sem(name):
            return ctx.enter_context(nc.semaphore("image_" + name))

        NBUF = 4
        dft = sb("irow_dft", [TR * FR, TT])
        f = sb("spectrum", [TR * FR, NBUF, C])
        x1 = sb("x1", [TT, NBUF, C])
        o = sb("o", [TT, NBUF, C])
        ps = [ctx.enter_context(nc.psum_tensor(f"image_ps{i}", [TT, 2, 512], F32)) for i in range(4)]
        consts = sem("consts")
        loaded = [sem(f"loaded{i}") for i in range(NBUF)]
        transformed = sem("transformed")
        o_set = sem("o_set")
        stored = [sem(f"stored{i}") for i in range(NBUF)]

        f_view = specD.rearrange("b (t h) k r c -> (b t) (h k r) c", h=TR)
        x_view = x1D.rearrange("b (t p) c -> (b t) p c", p=TT)
        o_view = out.rearrange("b (t p) c -> (b t) p c", p=TT)
        NS = B * NTT // NBUF

        with nc.Block() as block:

            @block.sync
            def _(sp):
                sp.dma_start(dft[:], irow_dft_d).then_inc(consts, 16)
                with sp.Fori(0, NS) as g:
                    for i in range(NBUF):
                        sp.wait_ge(o_set, g * NBUF)
                        sp.dma_start(f[:, i], f_view[g * NBUF + i]).then_inc(loaded[i], 16)
                        sp.dma_start(x1[:, i], x_view[g * NBUF + i]).then_inc(loaded[i], 16)

            @block.tensor
            def _(pe):
                pe.wait_ge(consts, 16)
                with pe.Fori(0, NS) as g:
                    for i in range(NBUF):
                        pe.wait_ge(loaded[i], g * 32 + 32)
                        pe.wait_ge(o_set, g * NBUF)
                        for h in range(2):
                            mm = nc.tensor.matmul(ps[i][:, h, 0:CH], dft[:], f[:, i, h * CH:(h + 1) * CH],
                                                  start=True, stop=True)
                        mm.then_inc(transformed, 1)

            @block.vector
            def _(dve):
                with dve.Fori(0, NS) as g:
                    for i in range(NBUF):
                        dve.wait_ge(transformed, g * NBUF + i + 1)
                        dve.wait_ge(stored[i], g * 16)
                        nc.vector.tensor_tensor(o[:, i].rearrange("p (h c) -> p h c", h=2), ps[i][:, :, 0:CH],
                                                x1[:, i].rearrange("p (h c) -> p h c", h=2), ALU.add).then_inc(o_set, 1)

            @block.scalar
            def _(act):
                with act.Fori(0, NS) as g:
                    for i in range(NBUF):
                        act.wait_ge(o_set, g * NBUF + i + 1)
                        act.dma_start(o_view[g * NBUF + i], o[:, i]).then_inc(stored[i], 16)
                for i in range(NBUF):
                    act.wait_ge(stored[i], NS * 16)


def tables():
    def cs(n, m, size):
        k = np.outer(np.arange(n), np.arange(m)) % size
        c, s = np.cos(2 * np.pi * k / size), np.sin(2 * np.pi * k / size)
        s[(2 * k) % size == 0] = 0
        return c, s

    f32 = np.float32
    t = {"ident": np.eye(P, dtype=f32)}
    gi = (np.arange(C)[:, None] // GC == np.arange(GROUPS)).astype(f32)
    t["ind"] = np.ascontiguousarray(gi.reshape(CT, P, GROUPS).transpose(1, 0, 2))
    t["indT"] = np.ascontiguousarray(gi.T)
    gb = (np.arange(BS)[:, None] // GC == np.arange(GB)).astype(f32)
    t["indb"], t["indbT"] = gb, np.ascontiguousarray(gb.T)
    keys = np.arange(S).reshape(H, KG, KW).transpose(1, 0, 2).reshape(-1)
    kh, kw = keys // W, keys % W
    rows = (np.arange(H)[:, None] == kh).astype(f32)
    cols = (np.arange(W)[:, None] == kw).astype(f32)
    part = (np.arange(KW)[:, None] == kw % KW).astype(f32)
    t["hot_max"] = np.concatenate([rows, part])
    t["hot2"] = np.concatenate([cols, rows[:16]])
    t["hot3"] = np.concatenate([cols, rows[16:], rows[:-1], np.ones((1, S), f32)])
    c, s = cs(W, KWF, W)
    row = np.zeros((TR, W, TR, KWF, RI))
    irow = np.zeros((TR, KWF, RI, TR, W))
    mirrored = np.where((np.arange(KWF) == 0) | (np.arange(KWF) == KWF - 1), 1, 2)[:, None]
    for h in range(TR):
        row[h, :, h, :, 0], row[h, :, h, :, 1] = c, -s
        irow[h, :, 0, h], irow[h, :, 1, h] = mirrored * c.T, -mirrored * s.T
    t["row_dft"] = (row.reshape(TT, TR * FR) / W ** 0.5).astype(f32)
    t["irow_dft"] = (irow.reshape(TR * FR, TT) / W ** 0.5).astype(f32)
    c, s = cs(H, H, H)
    col = np.zeros((RI, H, RI, H))
    col[0, :, 0], col[1, :, 0], col[0, :, 1], col[1, :, 1] = c, s, -s, c
    t["col_dft"] = (col.reshape(RI * H, RI * H) / H ** 0.5).astype(f32)
    icol = np.zeros((2, H, 3, 2, H))
    for k in range(2):
        icol[k, :, 0, k], icol[k, :, 1, k], icol[k, :, 2, k] = c, s, -s
    t["icol_dft"] = (icol.reshape(2 * H, 3, 2 * H) / H ** 0.5).astype(f32)
    return t


def build(nc, a, out):
    def scratch(name, shape):
        return nc.dram_tensor(name, shape, F32).ap()

    x = a["x"].rearrange("b h w c -> b (h w) c")
    qF = scratch("q_scratch", (NP, P, S))
    qHL = scratch("q_split_scratch", (NP, P, 2, S))
    kHL = scratch("k_split_scratch", (NP, P, 2, S))
    vD = scratch("v_scratch", (NP, P, KT, P))
    relH = scratch("row_logits_scratch", (NP, 2, 2 * H, S))
    relW = scratch("column_logits_scratch", (NP, 2, 2 * W, S))
    aHL = scratch("attention_scratch", (NP, P, 2, S))
    x1D = scratch("x1_scratch", (B, S, C))
    rowsD = scratch("row_spectrum_scratch", (B, H, KWF, RI, C))
    specD = scratch("mixed_spectrum_scratch", (B, H, KWF, RI, C))
    project(nc, x, a["qkv_w"], a["qk_bias"], a["qkv_b"], a["ident"], a["ind"], a["indT"], qF, qHL, kHL, vD)
    relpos(nc, a["rev_h"], a["rev_w"], qF, relH, relW)
    rowmax(nc, a["ident"], a["hot_max"], qHL, kHL, relH, relW)
    attend(nc, a["hot2"], a["hot3"], qHL, kHL, vD, relH, relW, aHL)
    out_project(nc, x, a["proj_w"], a["proj_b"], a["row_dft"], aHL, x1D, rowsD)
    spectrum(nc, a["w1"], a["b1"], a["w2"], a["b2"], a["col_dft"], a["icol_dft"], a["indb"], a["indbT"], rowsD, specD)
    image(nc, a["irow_dft"], x1D, specD, out.rearrange("b h w c -> b (h w) c"))


def kernel(**inputs):
    import concourse.bacc as bacc
    from concourse.bass_utils import run_bass_kernel_spmd

    i = {k: np.asarray(v) for k, v in inputs.items()}
    arrays = dict(
        x=i["x"], qkv_w=i["L0_conv_qkv_w"], qkv_b=i["L0_conv_qkv_b"],
        qk_bias=i["L0_conv_qkv_b"][:2 * C].reshape(2 * PAIRS, P).T,
        proj_w=i["L0_conv_proj_w"], proj_b=i["L0_conv_proj_b"],
        rev_h=i["L0_conv_rel_pos_h"][::-1].T, rev_w=i["L0_conv_rel_pos_w"][::-1].T,
        w1=i["L1_conv_w1"], b1=i["L1_conv_b1"].transpose(2, 1, 0),
        w2=i["L1_conv_w2"], b2=i["L1_conv_b2"].transpose(1, 0, 2).reshape(-1), **tables())
    arrays = {k: np.ascontiguousarray(v) for k, v in arrays.items()}
    nc = bacc.Bacc("TRN2", target_bir_lowering=False, num_devices=1)
    aps = {k: nc.dram_tensor(f"in_{k}", v.shape, F32, kind="ExternalInput").ap() for k, v in arrays.items()}
    out = nc.dram_tensor("out_image", (B, H, W, C), F32, kind="ExternalOutput").ap()
    build(nc, aps, out)
    result = run_bass_kernel_spmd(nc, [{f"in_{k}": v for k, v in arrays.items()}], core_ids=[0])
    return result.results[0]["out_image"]
```

```python
from contextlib import ExitStack

import concourse.bass as bass
import numpy as np
from concourse import mybir
from concourse.alu_op_type import AluOpType as ALU

F32 = mybir.dt.float32
F32R = mybir.dt.float32r
ACT = mybir.ActivationFunctionType
AX_X = mybir.AxisListType.X

P = 128
B, H, W, C = 2, 48, 48, 768
S = H * W
CT = C // P
HEADS, D = 12, 64
PAIRS = HEADS // 2
NP = B * PAIRS
KT = S // P
KG = 3
GK = S // KG
KW = W // KG
KR = P // KW
GROUPS = 32
GC = C // GROUPS
EPS = 1e-5
SCALE = D ** -0.5
NREL = 2 * H - 1

QC = 5
ROWS = [10, 10, 10, 10, 8]
QN = [r * W for r in ROWS]
Q0 = [10 * W * c for c in range(QC)]
QMAX = QN[0]

TG = 384
NTG = S // TG
TPG = TG // P

SPARSITY = 0.01
NB, BS = 8, 96
KWF = W // 2 + 1
RI = 2


def natural(ap):
    return ap.rearrange("p (j h w) -> p h j w", j=KG, w=KW)


def project(nc, x, qkv_w, qk_bias, qkv_b, ident_d, ind_d, indT_d, qF, qHL, kHL, vD):
    with ExitStack() as ctx:
        def sb(name, shape, dt=F32):
            return ctx.enter_context(nc.sbuf_tensor("project_" + name, shape, dt))

        def sem(name):
            return ctx.enter_context(nc.semaphore("project_" + name))

        xh = sb("xn_hi", [P, CT, S], F32R)
        xl = sb("xn_lo", [P, CT, S], F32R)
        xtok = sb("x_tokens", [P, 2, TPG, C])
        ident = sb("ident", [P, P])
        ind = sb("ind", [P, CT, GROUPS])
        indT = sb("indT", [GROUPS, C])
        qb = sb("q_bias", [P, 2 * PAIRS])
        vb = sb("v_bias", [P, C])
        stats = sb("stats", [P, CT, NTG, 6])
        mv = sb("mean_var", [P, CT, 2])
        gate = sb("gate", [P, 1])
        dev = sb("deviation", [P, CT])
        within = sb("within", [P, CT])
        gm = sb("group_mean", [GROUPS, 1])
        gv = sb("group_var", [GROUPS, 1])
        gs = sb("group_std", [GROUPS, 1])
        gr = sb("group_rstd", [GROUPS, 1])
        epst = sb("eps", [GROUPS, 1])
        cm = sb("channel_mean", [P, CT])
        cr = sb("channel_rstd", [P, CT])
        cb = sb("channel_shift", [P, CT])
        xn = sb("xn", [P, 4, TG])
        wraw = sb("w_raw", [P, 2, CT, P])
        whl = sb("w_split", [P, 2, 2, CT, P], F32R)
        row = sb("qk_row", [P, 2, QMAX])
        hl = sb("qk_split", [P, 2, S], F32R)
        wv = sb("wv_split", [P, 2, CT, TG], F32R)
        vout = sb("v_out", [P, 2, TG])
        ps = [ctx.enter_context(nc.psum_tensor(f"project_ps{i}", [P, 512], F32)) for i in range(8)]

        consts = sem("consts")
        eps_set = sem("eps_set")
        x_loaded = [sem(f"x_loaded{i}") for i in range(2)]
        transposed = sem("transposed")
        st_done = sem("st_done")
        chain = sem("dve_chain")
        gsum_ready = sem("gsum_ready")
        gmean_set = sem("gmean_set")
        within_set = sem("within_set")
        gvar_set = sem("gvar_set")
        gstd_set = sem("gstd_set")
        grstd_set = sem("grstd_set")
        shift_set = sem("shift_set")
        xn_written = sem("xn_written")
        xh_set = sem("xh_set")
        xhl_written = sem("xhl_written")
        w_loaded = [sem(f"w_loaded{i}") for i in range(2)]
        wh_set = sem("wh_set")
        w_split = sem("w_split_done")
        qk_product = sem("qk_product")
        qk_biased = sem("qk_biased")
        qk_hi = sem("qk_hi")
        qk_lo = sem("qk_lo")
        qrow_stored = [sem(f"qrow_stored{i}") for i in range(2)]
        qk_stored = sem("qk_stored")
        wv_loaded = [sem(f"wv_loaded{i}") for i in range(2)]
        wvh_set = sem("wvh_set")
        wv_split = sem("wv_split_done")
        v_product = sem("v_product")
        v_biased = sem("v_biased")
        v_stored = [sem(f"v_stored{i}") for i in range(2)]

        NTP = NTG * CT
        OT = 2 * PAIRS
        NVH = C // TG
        x_view = x.rearrange("b (g t p) c -> b g p t c", t=TPG, p=P)
        w_view = qkv_w.rearrange("(t p) n -> p t n", p=P)

        with nc.Block() as block:

            @block.sync
            def _(sp):
                for dst, src in ((ident[:], ident_d), (ind[:], ind_d), (indT[:], indT_d),
                                 (qb[:], qk_bias),
                                 (vb[:], qkv_b[2 * C:3 * C].rearrange("(a c) -> a c", a=1).broadcast_to([P, C]))):
                    sp.dma_start(dst, src).then_inc(consts, 16)
                with sp.Fori(0, B) as b:
                    for pas in range(2):
                        for g in range(NTG):
                            n = pas * NTG + g
                            if n >= 2:
                                sp.wait_ge(transposed, b * (2 * NTP) + (n - 1) * CT)
                            sp.dma_start(xtok[:, g % 2], x_view[b, g]).then_inc(x_loaded[g % 2], 16)
                    for o in range(OT + 1):
                        if o < OT:
                            if o >= 2:
                                sp.wait_ge(w_split, b * OT + o - 1)
                            sp.dma_start(wraw[:, o % 2], w_view[:, :, o * P:(o + 1) * P]).then_inc(w_loaded[o % 2], 16)
                        if o == 0:
                            continue
                        m = o - 1
                        if m < PAIRS:
                            for c in range(QC):
                                n = m * QC + c
                                sp.wait_ge(qk_biased, b * (OT * QC) + n + 1)
                                sp.dma_start(qF[b * PAIRS + m][:, Q0[c]:Q0[c] + QN[c]],
                                             row[:, n % 2, 0:QN[c]]).then_inc(qrow_stored[n % 2], 16)
                        sp.wait_ge(qk_lo, b * (OT * QC) + m * QC + QC)
                        dst = qHL if m < PAIRS else kHL
                        sp.dma_start(dst[b * PAIRS + m % PAIRS], hl[:].bitcast(F32)).then_inc(qk_stored, 16)
                    for vh in range(NVH):
                        sp.wait_ge(transposed, (b + 1) * (2 * NTP))
                        sp.dma_start(xtok[:, vh].rearrange("p a (c n) -> p (a c) n", n=TG),
                                     w_view[:, :, 2 * C + vh * TG:2 * C + (vh + 1) * TG]).then_inc(wv_loaded[vh], 16)
                    for n in range(NVH * KT):
                        sp.wait_ge(v_biased, b * (NVH * KT) + n + 1)
                        sp.dma_start(vD.rearrange("(b v o) p t d -> b v t p o d", b=B, v=NVH)[b, n // KT, n % KT],
                                     vout[:, n % 2].rearrange("p (o d) -> p o d", d=P)
                                     ).then_inc(v_stored[n % 2], 16)
                sp.wait_ge(qk_stored, B * OT * 16)
                for i in range(2):
                    sp.wait_ge(qrow_stored[i], B * PAIRS * QC * 8)
                for i in range(2):
                    sp.wait_ge(v_stored[i], B * NVH * KT // 2 * 16)

            @block.tensor
            def _(pe):
                pe.wait_ge(consts, 5 * 16)
                with pe.Fori(0, B) as b:
                    for pas in range(2):
                        for g in range(NTG):
                            pe.wait_ge(x_loaded[g % 2], (b * NTG + pas * (NTG // 2) + g // 2 + 1) * 16)
                            for ct in range(CT):
                                n = g * CT + ct
                                if pas == 0 and n >= 4:
                                    pe.wait_ge(st_done, b * NTP + n - 3)
                                if pas == 0 and n == 0:
                                    pe.wait_ge(v_biased, b * (NVH * KT))
                                if pas == 1 and n >= 4:
                                    pe.wait_ge(xn_written, b * NTP + n - 3)
                                for t in range(TPG):
                                    mm = nc.tensor.transpose(ps[n % 4][:, t * P:(t + 1) * P],
                                                             xtok[:, g % 2, t, ct * P:(ct + 1) * P], ident[:])
                                mm.then_inc(transposed, 1)
                        if pas == 0:
                            pe.wait_ge(chain, b * 3 + 1)
                            for ct in range(CT):
                                mm = nc.tensor.matmul(ps[4][0:GROUPS, 0:1], ind[:, ct], mv[:, ct, 0:1],
                                                      start=ct == 0, stop=ct == CT - 1)
                            mm.then_inc(gsum_ready, 1)
                            pe.wait_ge(gmean_set, b + 1)
                            for ct in range(CT):
                                mm = nc.tensor.matmul(ps[5][:, ct:ct + 1], indT[:, ct * P:(ct + 1) * P], gm[:],
                                                      start=True, stop=True)
                            mm.then_inc(gsum_ready, 1)
                            pe.wait_ge(within_set, b + 1)
                            for ct in range(CT):
                                mm = nc.tensor.matmul(ps[6][0:GROUPS, 0:1], ind[:, ct], within[:, ct:ct + 1],
                                                      start=ct == 0, stop=ct == CT - 1)
                            mm.then_inc(gsum_ready, 1)
                            pe.wait_ge(grstd_set, b + 1)
                            for ct in range(CT):
                                mm = nc.tensor.matmul(ps[7][:, ct:ct + 1], indT[:, ct * P:(ct + 1) * P], gr[:],
                                                      start=True, stop=True)
                            mm.then_inc(gsum_ready, 1)
                    pe.wait_ge(xhl_written, (b + 1) * NTP)
                    for o in range(OT):
                        pe.wait_ge(w_split, b * OT + o + 1)
                        for c in range(QC):
                            n = o * QC + c
                            if n >= 2:
                                pe.wait_ge(qk_biased, b * (OT * QC) + n - 1)
                            k = 0
                            for wp, xp in ((0, xh), (0, xl), (1, xh)):
                                for ct in range(CT):
                                    cols = (natural(xp[:, ct])[:, 10 * c:10 * c + ROWS[c]] if o < PAIRS
                                            else xp[:, ct, Q0[c]:Q0[c] + QN[c]])
                                    mm = nc.tensor.matmul(ps[4 + n % 2][:, 0:QN[c]], whl[:, o % 2, wp, ct],
                                                          cols, start=k == 0, stop=k == 3 * CT - 1)
                                    k += 1
                            mm.then_inc(qk_product, 1)
                    for n in range(NVH * KT):
                        vh, t = n // KT, n % KT
                        if t == 0:
                            pe.wait_ge(wv_split, b * NVH + vh + 1)
                        if n >= 2:
                            pe.wait_ge(v_biased, b * (NVH * KT) + n - 1)
                        k = 0
                        for xp, wp in ((xh, 0), (xh, 1), (xl, 0)):
                            for ct in range(CT):
                                mm = nc.tensor.matmul(ps[6 + n % 2][:, 0:TG], xp[:, ct, t * P:(t + 1) * P], wv[:, wp, ct],
                                                      start=k == 0, stop=k == 3 * CT - 1)
                                k += 1
                        mm.then_inc(v_product, 1)

            @block.scalar
            def _(act):
                act.wait_ge(consts, 5 * 16)
                act.wait_ge(eps_set, 1)
                with act.Fori(0, B) as b:
                    act.wait_ge(gvar_set, b + 1)
                    nc.scalar.activation(gs[:], gv[:], ACT.Sqrt, bias=epst[:]).then_inc(gstd_set, 1)
                    act.wait_ge(shift_set, b + 1)
                    for n in range(NTP):
                        ct = n % CT
                        act.wait_ge(transposed, b * (2 * NTP) + NTP + n + 1)
                        if n >= 4:
                            act.wait_ge(xhl_written, b * NTP + n - 3)
                        nc.scalar.activation(xn[:, n % 4], ps[n % 4][:, 0:TG], ACT.Identity,
                                             bias=cb[:, ct:ct + 1], scale=cr[:, ct:ct + 1]).then_inc(xn_written, 1)
                    for o in range(OT):
                        for c in range(QC):
                            n = o * QC + c
                            act.wait_ge(qk_product, b * (OT * QC) + n + 1)
                            if n >= 2:
                                act.wait_ge(qk_lo, b * (OT * QC) + n - 1)
                            if o < PAIRS:
                                act.wait_ge(qrow_stored[n % 2], b * (PAIRS * QC * 8) + n // 2 * 16)
                            elif n < PAIRS * QC + 2:
                                act.wait_ge(qrow_stored[n % 2], (b + 1) * (PAIRS * QC * 8))
                            nc.scalar.activation(row[:, n % 2, 0:QN[c]], ps[4 + n % 2][:, 0:QN[c]], ACT.Identity,
                                                 bias=qb[:, o:o + 1], scale=1.0).then_inc(qk_biased, 1)

            @block.vector
            def _(dve):
                nc.vector.memset(epst[:], EPS).then_inc(eps_set, 1)
                dve.wait_ge(consts, 5 * 16)
                with dve.Fori(0, B) as b:
                    for g in range(NTG):
                        for ct in range(CT):
                            n = g * CT + ct
                            dve.wait_ge(transposed, b * (2 * NTP) + n + 1)
                            nc.vector.bn_stats(stats[:, ct, g], ps[n % 4][:, 0:TG]).then_inc(st_done, 1)
                    dve.wait_ge(st_done, (b + 1) * NTP)
                    nc.vector.memset(gate[:], 0.0)
                    for ct in range(CT):
                        ins = nc.vector.bn_aggr(mv[:, ct], stats[:, ct])
                    ins.then_inc(chain, 1)
                    dve.wait_ge(gsum_ready, b * 4 + 1)
                    nc.vector.tensor_scalar(gm[:], ps[4][0:GROUPS, 0:1], 1.0 / GC, None, ALU.mult).then_inc(gmean_set, 1)
                    dve.wait_ge(gsum_ready, b * 4 + 2)
                    nc.vector.tensor_copy(cm[:], ps[5][:, 0:CT]).then_inc(chain, 1)
                    dve.wait_ge(chain, b * 3 + 2)
                    nc.vector.tensor_tensor(dev[:], mv[:, :, 0], cm[:], ALU.subtract).then_inc(chain, 1)
                    dve.wait_ge(chain, b * 3 + 3)
                    for ct in range(CT):
                        ins = nc.vector.scalar_tensor_tensor(out=within[:, ct:ct + 1], in0=dev[:, ct:ct + 1],
                                                             scalar=dev[:, ct:ct + 1], in1=mv[:, ct, 1:2],
                                                             op0=ALU.mult, op1=ALU.add)
                    ins.then_inc(within_set, 1)
                    dve.wait_ge(gsum_ready, b * 4 + 3)
                    nc.vector.tensor_scalar(gv[:], ps[6][0:GROUPS, 0:1], 1.0 / GC, None, ALU.mult).then_inc(gvar_set, 1)
                    dve.wait_ge(gstd_set, b + 1)
                    nc.vector.reciprocal(gr[:], gs[:]).then_inc(grstd_set, 1)
                    dve.wait_ge(gsum_ready, b * 4 + 4)
                    nc.vector.scalar_tensor_tensor(out=cb[:], in0=ps[7][:, 0:CT], scalar=-1.0, in1=cm[:],
                                                   op0=ALU.mult, op1=ALU.mult)
                    nc.vector.tensor_copy(cr[:], ps[7][:, 0:CT]).then_inc(shift_set, 1)
                    for n in range(NTP):
                        g, ct = n // CT, n % CT
                        dve.wait_ge(xn_written, b * NTP + n + 1)
                        if n == 0:
                            dve.wait_ge(v_product, b * (NVH * KT))
                        src = xn[:, n % 4].rearrange("p (h j w) -> p h j w", j=KG, w=KW)
                        hi, lo = (natural(t[:, ct])[:, g * (TG // W):(g + 1) * (TG // W)] for t in (xh, xl))
                        nc.vector.tensor_copy(hi, src).then_inc(xh_set, 1)
                        dve.wait_ge(xh_set, b * NTP + n + 1)
                        nc.vector.tensor_tensor(lo, src, hi.bitcast(F32), ALU.subtract).then_inc(xhl_written, 1)

                    def split_w(o):
                        dve.wait_ge(w_loaded[o % 2], (b * PAIRS + o // 2 + 1) * 16)
                        if o >= 2:
                            dve.wait_ge(qk_product, b * (OT * QC) + (o - 1) * QC)
                        nc.vector.tensor_copy(whl[:, o % 2, 0], wraw[:, o % 2]).then_inc(wh_set, 1)
                        dve.wait_ge(wh_set, b * OT + o + 1)
                        nc.vector.tensor_tensor(whl[:, o % 2, 1], wraw[:, o % 2], whl[:, o % 2, 0].bitcast(F32),
                                                ALU.subtract).then_inc(w_split, 1)

                    split_w(0)
                    for o in range(OT):
                        if o + 1 < OT:
                            split_w(o + 1)
                        s = SCALE if o < PAIRS else 1.0
                        for c in range(QC):
                            n = o * QC + c
                            dve.wait_ge(qk_biased, b * (OT * QC) + n + 1)
                            if c == 0:
                                dve.wait_ge(qk_stored, (b * OT + o) * 16)
                            src = row[:, n % 2, 0:QN[c]]
                            hi, lo = (hl[:, i, Q0[c]:Q0[c] + QN[c]] for i in range(2))
                            nc.vector.tensor_scalar(hi, src, s, None, ALU.mult).then_inc(qk_hi, 1)
                            dve.wait_ge(qk_hi, b * (OT * QC) + n + 1)
                            nc.vector.scalar_tensor_tensor(out=lo, in0=src, scalar=s, in1=hi.bitcast(F32),
                                                           op0=ALU.mult, op1=ALU.subtract).then_inc(qk_lo, 1)
                    for vh in range(NVH):
                        raw = xtok[:, vh].rearrange("p a (c n) -> p (a c) n", n=TG)
                        dve.wait_ge(wv_loaded[vh], (b + 1) * 16)
                        dve.wait_ge(v_product, b * (NVH * KT) + vh * KT)
                        nc.vector.tensor_copy(wv[:, 0], raw).then_inc(wvh_set, 1)
                        dve.wait_ge(wvh_set, b * NVH + vh + 1)
                        nc.vector.tensor_tensor(wv[:, 1], raw, wv[:, 0].bitcast(F32), ALU.subtract).then_inc(wv_split, 1)
                        for t in range(KT):
                            n = vh * KT + t
                            dve.wait_ge(v_product, b * (NVH * KT) + n + 1)
                            dve.wait_ge(v_stored[n % 2], (b * (NVH * KT // 2) + n // 2) * 16)
                            nc.vector.tensor_tensor(vout[:, n % 2], ps[6 + n % 2][:, 0:TG],
                                                    vb[:, vh * TG:(vh + 1) * TG], ALU.add).then_inc(v_biased, 1)


RQ = 4
NU = H
NRP = NU // RQ


def relpos(nc, rev_h, rev_w, qF, relH, relW):
    with ExitStack() as ctx:
        def sb(name, shape, dt=F32):
            return ctx.enter_context(nc.sbuf_tensor("relpos_" + name, shape, dt))

        def sem(name):
            return ctx.enter_context(nc.semaphore("relpos_" + name))

        q = sb("q", [P, PAIRS, S])
        tab = sb("tab", [P, 2, NREL, 2])
        diff = sb("diff", [P, H, H, 2])
        w_hl = sb("w_split", [2 * W, 2, PAIRS, S], F32R)
        h_hl = sb("h_split", [2 * H, 2, 2, PAIRS, RQ * W], F32R)
        ps = [ctx.enter_context(nc.psum_tensor(f"relpos_ps{i}", [2 * H, 512], F32)) for i in range(8)]

        tab_zero = sem("tab_zero")
        tab_loaded = sem("tab_loaded")
        diff_zero = sem("diff_zero")
        diff_set = sem("diff_set")
        q_loaded = sem("q_loaded")
        product = sem("product")
        hi_set = sem("hi_set")
        lo_set = sem("lo_set")
        w_stored = sem("w_stored")
        h_stored = [sem(f"h_stored{i}") for i in range(2)]

        N = PAIRS * W
        UB = 2 * NU

        with nc.Block() as block:

            @block.gpsimd
            def _(pool):
                nc.gpsimd.memset(tab[:], 0.0).then_inc(tab_zero, 1)
                nc.gpsimd.memset(diff[:], 0.0).then_inc(diff_zero, 1)

            @block.sync
            def _(sp):
                sp.wait_ge(tab_zero, 1)
                for i, rev in enumerate((rev_h, rev_w)):
                    for s in range(2):
                        sp.dma_start(tab[s * D:(s + 1) * D, i, :, s:s + 1], rev.rearrange("c (r a) -> c r a", a=1),
                                     allow_slow_non_contiguous=True).then_inc(tab_loaded, 16)
                with sp.Fori(0, B) as b:
                    sp.wait_ge(product, b * UB)
                    sp.dma_start(q[:], qF.rearrange("(b o) p q -> b p o q", b=B)[b]).then_inc(q_loaded, 16)
                    sp.wait_ge(lo_set, b * UB + NU)
                    for part in range(2):
                        sp.dma_start(relW.rearrange("(b o) a r q -> b a r o q", b=B)[b, part],
                                     w_hl[:, part].bitcast(F32)).then_inc(w_stored, 16)
                    for g in range(NRP):
                        sp.wait_ge(lo_set, b * UB + NU + (g + 1) * RQ)
                        for part in range(2):
                            sp.dma_start(relH.rearrange("(b o) a r q -> b a r o q", b=B)[b, part][:, :, g * RQ * W:(g + 1) * RQ * W],
                                         h_hl[:, g % 2, part].bitcast(F32)).then_inc(h_stored[g % 2], 16)
                sp.wait_ge(w_stored, B * 2 * 16)
                for i in range(2):
                    sp.wait_ge(h_stored[i], B * NRP * 16)

            @block.tensor
            def _(pe):
                pe.wait_ge(diff_set, H)
                with pe.Fori(0, B) as b:
                    pe.wait_ge(q_loaded, (b + 1) * 16)
                    for u in range(UB):
                        kind, r = u // NU, u % NU
                        if u >= 8:
                            pe.wait_ge(lo_set, b * UB + u - 7)
                        else:
                            pe.wait_ge(lo_set, b * UB)
                        if kind == 0:
                            cols = q[:].rearrange("p o (h w) -> p o h w", w=W)[:, :, :, r]
                            win = tab[:, 1].rearrange("p r s -> p (r s)")[:, 2 * (W - 1 - r):2 * (W - 1 - r) + 2 * W]
                        else:
                            cols = q[:, :, r * W:(r + 1) * W]
                            win = diff[:, r].rearrange("p k s -> p (k s)")
                        nc.tensor.matmul(ps[u % 8][:, 0:N], win, cols, start=True, stop=True).then_inc(product, 1)

            def part_of(u, part):
                kind, r = u // NU, u % NU
                if kind == 0:
                    return w_hl[:, part].rearrange("p o (h w) -> p o h w", w=W)[:, :, :, r]
                return h_hl[:, r // RQ % 2, part, :, r % RQ * W:(r % RQ + 1) * W]

            @block.scalar
            def _(act):
                with act.Fori(0, B) as b:
                    for u in range(UB):
                        act.wait_ge(product, b * UB + u + 1)
                        if u == 0:
                            act.wait_ge(w_stored, b * 2 * 16)
                        if u >= NU and u % RQ == 0:
                            g = (u - NU) // RQ
                            act.wait_ge(h_stored[g % 2], b * (NRP * 16) + g // 2 * 32)
                        nc.scalar.activation(part_of(u, 0), ps[u % 8][:, 0:N].rearrange("p (o n) -> p o n", n=W),
                                             ACT.Copy).then_inc(hi_set, 1)

            @block.vector
            def _(dve):
                dve.wait_ge(tab_loaded, 4 * 16)
                dve.wait_ge(diff_zero, 1)
                for r in range(H):
                    for s in range(2):
                        rows = slice(s * D, (s + 1) * D)
                        ins = nc.vector.tensor_scalar(diff[rows, r, :, s], tab[rows, 0, H - 1 - r:2 * H - 1 - r, s],
                                                      tab[rows, 0, 2 * H - 2 - r, s:s + 1], None, ALU.subtract)
                    ins.then_inc(diff_set, 1)
                with dve.Fori(0, B) as b:
                    for u in range(UB):
                        dve.wait_ge(hi_set, b * UB + u + 1)
                        nc.vector.tensor_tensor(part_of(u, 1), ps[u % 8][:, 0:N].rearrange("p (o n) -> p o n", n=W),
                                                part_of(u, 0).bitcast(F32), ALU.subtract).then_inc(lo_set, 1)


SLOTS = QC * KT
NPB = 4
NSB = 3
UNITS = 2 * KT * KG
UH = KT * KG
PIECES = 4
UP = UNITS // PIECES
AHEAD = SLOTS - 9


def units_of(m):
    return range(-(-m * UNITS // AHEAD), min(-(-(m + 1) * UNITS // AHEAD), UNITS))


def guests():
    slots, done = [], 0
    for m in range(SLOTS):
        c, t = m // KT, m % KT
        units = [("unit", u) for u in units_of(m)]
        before, after = units[:1], units[1:]
        if c >= 1 and t == 2:
            after.append(("sum", c - 1))
        for s in range(2):
            if m >= 2 and (s + 1) * UH - 1 in units_of(m - 2):
                after.append(("turn", s))
        slots.append((before, after))
    order = [g for before, after in slots for g in before + after] + [("sum", QC - 1)]
    return slots, {g: i for i, g in enumerate(order)}


GUESTS, GUEST_AT = guests()


def guest_at(what, ahead):
    return GUEST_AT[what] if ahead else what[1]


GUESTS_OF_PAIR = len(GUEST_AT)
GUESTS_BEFORE = UNITS + 2


def attend(nc, ident_d, hot_max_d, hot2_d, hot3_d, qHL, kHL, vD, relH, relW, maxD, aHL):
    with ExitStack() as ctx:
        def sb(name, shape, dt=F32):
            return ctx.enter_context(nc.sbuf_tensor("attend_" + name, shape, dt))

        def sem(name):
            return ctx.enter_context(nc.semaphore("attend_" + name))

        stage = sb("stage", [P, 2, S])
        qs = [sb(f"q{s}", [P, 3, S], F32R) for s in range(2)]
        ks = [sb(f"k{s}", [P, 2, S], F32R) for s in range(2)]
        k3 = sb("k_hot", [P, S], F32R)
        v = sb("v", [P, KT, P])
        pe_ones = sb("ones", [P, D])
        prob = sb("prob", [P, NPB, 2, QMAX])
        acc = sb("prob_sum", [P, 2, 2, QMAX])
        o_raw = sb("o_raw", [P, QMAX])
        o32 = sb("o", [P, QMAX])
        ohl = sb("o_split", [P, 2, 2, QMAX], F32R)
        qa = [sb(f"qa{i}", [P, KG, S // 2], F32R) for i in range(2)]
        ka = sb("ka", [P, 2, S], F32R)
        ident = sb("ident", [P, P])
        part_max = sb("part_max", [P, 2, KT, KG])
        mx = sb("max", [P, 2, KT])
        neg = sb("negated", [KT, 2, P], F32R)
        psS = [ctx.enter_context(nc.psum_tensor(f"attend_s{i}", [P, 512], F32)) for i in range(NSB)]
        psO = ctx.enter_context(nc.psum_tensor("attend_sum", [P, 512], F32))
        psG = [ctx.enter_context(nc.psum_tensor(f"attend_guest{i}", [P, 2, 512], F32)) for i in range(2)]

        hot_loaded = sem("hot_loaded")
        hot_set = sem("hot_set")
        ones_set = sem("ones_set")
        q_loaded = [sem(f"q_loaded{c}") for c in range(QC)]
        kv_loaded = [sem(f"kv_loaded{j}") for j in range(KG)]
        max_loaded = [sem(f"max_loaded{i}") for i in range(2)]
        qa_loaded = [sem(f"qa_loaded{i}") for i in range(2)]
        ka_loaded = [sem(f"ka_loaded{s}") for s in range(2)]
        scores = sem("scores")
        exped = sem("exped")
        weighed = sem("weighed")
        added = sem("added")
        unit_done = sem("unit_done")
        summed = sem("summed")
        turned = sem("turned")
        guest_read = sem("guest_read")
        max_set = sem("max_set")
        max_stored = [sem(f"max_stored{s}") for s in range(2)]
        o_copied = sem("o_copied")
        normalised = sem("normalised")
        ohi_set = sem("ohi_set")
        olo_set = sem("olo_set")
        stored = [sem(f"stored{i}") for i in range(2)]

        QL, KL, QAL = 18, 7, 3 * KG
        TJ = KT // KG
        HN = GK // 2
        LAST = NP - 1

        def head_rows(rel, n, a, s):
            return rel[n, a].rearrange("(k s) q -> k s q", s=2)[:, s]

        def load_q(sp, n, c):
            cols = slice(Q0[c], Q0[c] + QN[c])
            for s in range(2):
                rows = slice(s * D, (s + 1) * D)
                d = qs[s].bitcast(F32)
                rh = [head_rows(relH, n, a, s)[:, cols] for a in range(2)]
                rw = [head_rows(relW, n, a, s)[:, cols] for a in range(2)]
                for dst, src in ((d[0:D, 0, cols], qHL[n, rows, 0, cols]),
                                 (d[D:P, 0, cols], qHL[n, rows, 0, cols]),
                                 (d[0:D, 1, cols], qHL[n, rows, 1, cols]),
                                 (d[D:D + W, 1, cols], rw[0]),
                                 (d[D + W:P, 1, cols], rh[0][0:16]),
                                 (d[0:W, 2, cols], rw[1]),
                                 (d[W:W + H - 16, 2, cols], rh[0][16:H]),
                                 (d[W + H - 16:P - 16, 2, cols], rh[1][0:32]),
                                 (d[P - 16:P - 1, 2, cols], rh[1][32:H - 1])):
                    sp.dma_start(dst, src).then_inc(q_loaded[c], 16)

        def load_max(sp, n, i):
            cols = slice(0, Q0[QC - 1]) if i == 0 else slice(Q0[QC - 1], S)
            for s in range(2):
                sp.dma_start(qs[s].bitcast(F32)[P - 1:P, 2, cols], maxD[n, s:s + 1, cols]).then_inc(max_loaded[i], 16)

        def load_kv(sp, n, j):
            cols = slice(j * GK, (j + 1) * GK)
            for s in range(2):
                rows = slice(s * D, (s + 1) * D)
                d = ks[s].bitcast(F32)
                for dst, part in ((d[0:D, 0, cols], 0), (d[D:P, 0, cols], 1), (d[0:D, 1, cols], 0)):
                    sp.dma_start(dst, kHL[n, rows, part, cols]).then_inc(kv_loaded[j], 16)
            sp.dma_start(v[:, j * TJ:(j + 1) * TJ], vD[n][:, j * TJ:(j + 1) * TJ]).then_inc(kv_loaded[j], 16)

        def load_qa(eng, n, p):
            s, cols = p // 2, slice(p % 2 * (S // 2), (p % 2 + 1) * (S // 2))
            d = qa[p % 2].bitcast(F32)
            for j in range(KG):
                for dst, src in ((d[D:D + H, j], head_rows(relH, n, 0, s)[:, cols]),
                                 (d[0:D, j], qHL[n, s * D:(s + 1) * D, 0, cols]),
                                 (d[D + H:P, j], head_rows(relW, n, 0, s)[j * KW:(j + 1) * KW, cols])):
                    eng.dma_start(dst, src).then_inc(qa_loaded[p % 2], 16)

        def load_ka(eng, n, s):
            eng.dma_start(ka.bitcast(F32)[0:D, s], kHL[n, s * D:(s + 1) * D, 0]).then_inc(ka_loaded[s], 16)

        def store_max(eng, n, s):
            eng.dma_start(maxD[n, s].rearrange("(t p) -> t p", p=P), neg[:, s].bitcast(F32)).then_inc(max_stored[s], 16)

        with nc.Block() as block:

            @block.sync
            def _(sp):
                sp.dma_start(prob[D:P].rearrange("p a b q -> p (a b q)")[:, 0:S], hot_max_d).then_inc(hot_loaded, 16)
                sp.dma_start(ident[:], ident_d).then_inc(hot_loaded, 16)
                sp.dma_start(stage[D:P, 0], hot2_d).then_inc(hot_loaded, 16)
                sp.dma_start(stage[:, 1], hot3_d).then_inc(hot_loaded, 16)
                for j in range(KG):
                    load_kv(sp, 0, j)
                load_q(sp, 0, 0)
                for c in range(1, QC):
                    load_q(sp, 0, c)
                for s in range(2):
                    sp.wait_ge(max_stored[s], 16)
                for i in range(2):
                    load_max(sp, 0, i)
                with sp.Fori(0, LAST) as n:
                    for c in range(QC - 1):
                        sp.wait_ge(scores, n * (2 * SLOTS) + (c + 1) * (2 * KT))
                        load_q(sp, n + 1, c)
                    for j in range(KG):
                        sp.wait_ge(weighed, n * SLOTS + (QC - 1) * KT + (j + 1) * TJ)
                        load_kv(sp, n + 1, j)
                        if j == 1:
                            for s in range(2):
                                sp.wait_ge(max_stored[s], (n + 2) * 16)
                            load_max(sp, n + 1, 0)
                    sp.wait_ge(scores, (n + 1) * (2 * SLOTS))
                    load_q(sp, n + 1, QC - 1)
                    load_max(sp, n + 1, 1)

            @block.gpsimd
            def _(pool):
                nc.gpsimd.memset(pe_ones[:], 1.0).then_inc(ones_set, 1)
                for s in range(2):
                    load_ka(pool, 0, s)
                    load_qa(pool, 0, s)
                for s in range(2):
                    pool.wait_ge(unit_done, (s + 1) * UP)
                    load_qa(pool, 0, 2 + s)
                    pool.wait_ge(guest_read, (s + 1) * (UH + 1))
                    store_max(pool, 0, s)
                    load_ka(pool, 1, s)
                pool.wait_ge(unit_done, UNITS)
                for p in range(2):
                    load_qa(pool, 1, p)

                def store_out(n, c):
                    pool.wait_ge(olo_set, n * QC + c + 1)
                    pool.dma_start(aHL[n][:, :, Q0[c]:Q0[c] + QN[c]],
                                   ohl[:, c % 2, :, 0:QN[c]].bitcast(F32)).then_inc(stored[c % 2], 16)

                def pair(n, more):
                    store_out(n, 0)
                    for p in range(PIECES):
                        pool.wait_ge(unit_done, (n + 1) * UNITS + (p + 1) * UP)
                        if p % 2 == 1 and more:
                            load_ka(pool, n + 2, p // 2)
                        if p < 2:
                            load_qa(pool, n + 1, p + 2)
                        elif more:
                            load_qa(pool, n + 2, p - 2)
                        if p % 2 == 1:
                            pool.wait_ge(guest_read, GUESTS_BEFORE + n * GUESTS_OF_PAIR + GUEST_AT["turn", p // 2] + 1)
                            store_max(pool, n + 1, p // 2)
                        store_out(n, p + 1)

                with pool.Fori(0, LAST - 1) as n:
                    pair(n, True)
                pair(LAST - 1, False)
                for c in range(QC):
                    store_out(LAST, c)
                pool.wait_ge(stored[0], NP * 3 * 16)
                pool.wait_ge(stored[1], NP * 2 * 16)
                for s in range(2):
                    pool.wait_ge(max_stored[s], NP * 16)

            @block.tensor
            def _(pe):

                def unit(n, u, g):
                    s, t, j = u // UH, u % UH // KG, u % KG
                    p = u // UP
                    if u % UP == 0:
                        pe.wait_ge(qa_loaded[p % 2], n * (2 * QAL * 16) + (p // 2 + 1) * (QAL * 16))
                    if u % UH == 0:
                        pe.wait_ge(ka_loaded[s], (n + 1) * 16)
                    tq = t % (KT // 2)
                    for i in range(2):
                        mm = nc.tensor.matmul(psG[g][:, i, 0:HN], qa[p % 2][:, j, tq * P:(tq + 1) * P],
                                              ka[:, s, j * GK + i * HN:j * GK + (i + 1) * HN], start=True, stop=True)
                    mm.then_inc(unit_done, 1)

                def turn(n, s, g):
                    pe.wait_ge(max_set, n * 2 + s + 1)
                    nc.tensor.transpose(psG[g][0:KT, 0, 0:P], mx[:, s], ident[:]).then_inc(turned, 1)

                def sum_probs(n, c, g):
                    pe.wait_ge(added, n * SLOTS + (c + 1) * KT)
                    for s in range(2):
                        mm = nc.tensor.matmul(psG[g][s * D:(s + 1) * D, 0, 0:QN[c]], pe_ones[:],
                                              acc[:, c % 2, s, 0:QN[c]], start=True, stop=True)
                    mm.then_inc(summed, 1)

                def guest(n, what, ahead):
                    kind, i = what
                    at = guest_at(what, ahead)
                    pe.wait_ge(guest_read, GUESTS_BEFORE + n * GUESTS_OF_PAIR + max(at - 1, 0))
                    if kind == "unit":
                        unit(n + 1, i, at % 2)
                    elif kind == "turn":
                        turn(n + 1, i, at % 2)
                    else:
                        sum_probs(n, i, at % 2)

                def weigh(n, m):
                    c, t = m // KT, m % KT
                    pe.wait_ge(exped, n * (2 * SLOTS) + 2 * m + 2)
                    if t == 0:
                        pe.wait_ge(o_copied, n * QC + c)
                    for s in range(2):
                        mm = nc.tensor.matmul(psO[s * D:(s + 1) * D, 0:QN[c]], v[:, t, s * D:(s + 1) * D],
                                              prob[:, m % NPB, s, 0:QN[c]], start=t == 0, stop=t == KT - 1)
                    mm.then_inc(weighed, 1)

                def pair(n, ahead):
                    for m in range(SLOTS):
                        c, t = m // KT, m % KT
                        before, after = ([g for g in gs if ahead or g[0] == "sum"] for gs in GUESTS[m])
                        for g in before:
                            guest(n, g, ahead)
                        if t == 0:
                            pe.wait_ge(q_loaded[c], (n + 1) * (QL * 16))
                            if c in (0, QC - 1):
                                pe.wait_ge(max_loaded[c // (QC - 1)], (n + 1) * 32)
                        if c == 0 and t % TJ == 0:
                            pe.wait_ge(kv_loaded[t // TJ], (n + 1) * (KL * 16))
                        cols = slice(Q0[c], Q0[c] + QN[c])
                        keys = slice(t * P, (t + 1) * P)
                        for s in range(2):
                            k = 2 * m + s
                            pe.wait_ge(exped, n * (2 * SLOTS) + max(k - NSB + 1, 0))
                            out = psS[k % NSB][:, 0:QN[c]]
                            nc.tensor.matmul(out, ks[s][:, 0, keys], qs[s][:, 0, cols], start=True, stop=False)
                            nc.tensor.matmul(out, ks[s][:, 1, keys], qs[s][:, 1, cols], start=False, stop=False)
                            nc.tensor.matmul(out, k3[:, keys], qs[s][:, 2, cols], start=False, stop=True
                                             ).then_inc(scores, 1)
                        for g in after:
                            guest(n, g, ahead)
                        if m >= 1:
                            weigh(n, m - 1)
                    weigh(n, SLOTS - 1)
                    guest(n, ("sum", QC - 1), ahead)

                pe.wait_ge(hot_set, 5)
                pe.wait_ge(ones_set, 1)
                for s in range(2):
                    for u in range(s * UH, (s + 1) * UH):
                        if u + s >= 2:
                            pe.wait_ge(guest_read, u + s - 1)
                        unit(0, u, (u + s) % 2)
                    pe.wait_ge(guest_read, (s + 1) * (UH + 1) - 2)
                    turn(0, s, ((s + 1) * (UH + 1) - 1) % 2)
                with pe.Fori(0, LAST) as n:
                    pair(n, True)
                pair(LAST, False)

            @block.scalar
            def _(act):

                def copy_out(n, c):
                    act.wait_ge(weighed, n * SLOTS + (c + 1) * KT)
                    act.wait_ge(olo_set, n * QC + c)
                    nc.scalar.activation(o_raw[:, 0:QN[c]], psO[:, 0:QN[c]], ACT.Copy).then_inc(o_copied, 1)

                def round_out(n, c):
                    act.wait_ge(normalised, n * QC + c + 1)
                    act.wait_ge(stored[c % 2], n * ((3 - c % 2) * 16) + c // 2 * 16)
                    nc.scalar.activation(ohl[:, c % 2, 0, 0:QN[c]], o32[:, 0:QN[c]], ACT.Copy).then_inc(ohi_set, 1)

                with act.Fori(0, NP) as n:
                    for m in range(SLOTS):
                        c, t = m // KT, m % KT
                        for s in range(2):
                            act.wait_ge(scores, n * (2 * SLOTS) + 2 * m + s + 1)
                            if s == 0:
                                if m == 0:
                                    act.wait_ge(hot_set, 5)
                                act.wait_ge(weighed, n * SLOTS + max(m - NPB + 1, 0))
                                act.wait_ge(added, n * SLOTS + max(m - NPB + 1, 0))
                            nc.scalar.activation(prob[:, m % NPB, s, 0:QN[c]], psS[(2 * m + s) % NSB][:, 0:QN[c]],
                                                 ACT.Exp).then_inc(exped, 1)
                        if c >= 1 and t == 0:
                            copy_out(n, c - 1)
                        if c >= 1 and t == 4:
                            round_out(n, c - 1)
                    copy_out(n, QC - 1)
                    round_out(n, QC - 1)

            @block.vector
            def _(dve):

                def reduce_unit(n, u, g):
                    s, t, j = u // UH, u % UH // KG, u % KG
                    dve.wait_ge(unit_done, n * UNITS + u + 1)
                    nc.vector.tensor_reduce(part_max[:, s, t, j:j + 1], psG[g][:, :, 0:HN],
                                            mybir.AxisListType.XY, ALU.max).then_inc(guest_read, 1)

                def reduce_head(n, s, units_read):
                    dve.wait_ge(guest_read, units_read)
                    nc.vector.tensor_reduce(mx[:, s], part_max[:, s], AX_X, ALU.max).then_inc(max_set, 1)

                def negate(n, s, g):
                    dve.wait_ge(turned, n * 2 + s + 1)
                    dve.wait_ge(max_stored[s], n * 16)
                    nc.vector.tensor_scalar(neg[:, s], psG[g][0:KT, 0, 0:P], -1.0, None, ALU.mult).then_inc(guest_read, 1)

                def normalise(n, c, g, read):
                    w = slice(0, QN[c])
                    dve.wait_ge(summed, n * QC + c + 1)
                    nc.vector.reciprocal(o32[:, w], psG[g][:, 0, w]).then_inc(guest_read, 1)
                    dve.wait_ge(o_copied, n * QC + c + 1)
                    dve.wait_ge(guest_read, read)
                    nc.vector.tensor_tensor(o32[:, w], o_raw[:, w], o32[:, w], ALU.mult).then_inc(normalised, 1)

                def split_out(n, c):
                    w = slice(0, QN[c])
                    dve.wait_ge(ohi_set, n * QC + c + 1)
                    nc.vector.tensor_tensor(ohl[:, c % 2, 1, w], o32[:, w], ohl[:, c % 2, 0, w].bitcast(F32),
                                            ALU.subtract).then_inc(olo_set, 1)

                def guest(n, what, ahead):
                    kind, i = what
                    g = guest_at(what, ahead) % 2
                    if kind == "unit":
                        reduce_unit(n + 1, i, g)
                    elif kind == "turn":
                        negate(n + 1, i, g)
                    else:
                        normalise(n, i, g, GUESTS_BEFORE + n * GUESTS_OF_PAIR + guest_at(what, ahead) + 1)

                def pair(n, ahead):
                    for m in range(SLOTS):
                        c, t = m // KT, m % KT
                        before, after = ([g for g in gs if ahead or g[0] == "sum"] for gs in GUESTS[m])
                        for g in before:
                            guest(n, g, ahead)
                        if t > 0:
                            total = acc[:, c % 2, :, 0:QN[c]]
                            dve.wait_ge(exped, n * (2 * SLOTS) + 2 * m + 2)
                            if t == 1:
                                dve.wait_ge(summed, n * QC + max(c - 1, 0))
                                nc.vector.tensor_tensor(total, prob[:, (m - 1) % NPB, :, 0:QN[c]],
                                                        prob[:, m % NPB, :, 0:QN[c]], ALU.add).then_inc(added, 2)
                            else:
                                dve.wait_ge(added, n * SLOTS + m)
                                nc.vector.tensor_tensor(total, total, prob[:, m % NPB, :, 0:QN[c]],
                                                        ALU.add).then_inc(added, 1)
                        if c >= 1 and t == 5:
                            split_out(n, c - 1)
                        for g in after:
                            guest(n, g, ahead)
                        for s in range(2):
                            if ahead and (s + 1) * UH - 1 in units_of(m):
                                reduce_head(n + 1, s, GUESTS_BEFORE + n * GUESTS_OF_PAIR + GUEST_AT["unit", (s + 1) * UH - 1] + 1)
                    guest(n, ("sum", QC - 1), ahead)
                    split_out(n, QC - 1)

                dve.wait_ge(hot_loaded, 4 * 16)
                for s in range(2):
                    nc.vector.tensor_copy(ka[D:P, s], prob[D:P].rearrange("p a b q -> p (a b q)")[:, 0:S]
                                          ).then_inc(hot_set, 1)
                for s in range(2):
                    nc.vector.tensor_copy(ks[s][D:P, 1], stage[D:P, 0]).then_inc(hot_set, 1)
                nc.vector.tensor_copy(k3[:], stage[:, 1]).then_inc(hot_set, 1)
                for s in range(2):
                    for u in range(s * UH, (s + 1) * UH):
                        reduce_unit(0, u, (u + s) % 2)
                    reduce_head(0, s, (s + 1) * (UH + 1) - 1)
                    negate(0, s, ((s + 1) * (UH + 1) - 1) % 2)
                with dve.Fori(0, LAST) as n:
                    pair(n, True)
                pair(LAST, False)


TR = 2
TT = TR * W
NTT = H // TR
FR = KWF * RI
CH = C // 2
TPC = NTT // KG


def out_project(nc, x, proj_w, proj_b, row_dft_d, aHL, x1D, rowsD):
    with ExitStack() as ctx:
        def sb(name, shape, dt=F32):
            return ctx.enter_context(nc.sbuf_tensor("out_" + name, shape, dt))

        def sem(name):
            return ctx.enter_context(nc.semaphore("out_" + name))

        a = sb("attention", [P, KG, 2, CT, GK], F32R)
        wraw = sb("w_raw", [P, 2, CT, CH])
        wp = sb("w_split", [P, 2, CT, C], F32R)
        pb = sb("bias", [TT, C])
        dft = sb("row_dft", [TT, TR * FR])
        xin = sb("x", [TT, 4, C])
        xb = sb("x_plus_bias", [TT, 2, C])
        x1 = sb("x1", [TT, 2, C])
        f = sb("spectrum", [TR * FR, 2, C])
        psA = [ctx.enter_context(nc.psum_tensor(f"out_a{i}", [TT, 2, 512], F32)) for i in range(2)]
        psF = [ctx.enter_context(nc.psum_tensor(f"out_f{i}", [TR * FR, 2, 512], F32)) for i in range(2)]

        consts = sem("consts")
        w_loaded = sem("w_loaded")
        w_hi = sem("w_hi")
        w_set = sem("w_set")
        a_loaded = [sem(f"a_loaded{j}") for j in range(KG)]
        x_loaded = [sem(f"x_loaded{i}") for i in range(4)]
        biased = sem("biased")
        projected = sem("projected")
        x1_set = sem("x1_set")
        transformed = sem("transformed")
        f_set = sem("f_set")
        x1_stored = [sem(f"x1_stored{i}") for i in range(2)]
        f_stored = [sem(f"f_stored{i}") for i in range(2)]

        x_view = x.rearrange("b (t p) c -> b t p c", p=TT)
        x1_view = x1D.rearrange("b (t p) c -> b t p c", p=TT)
        f_view = rowsD.rearrange("b (t h) k r c -> b t (h k r) c", h=TR)
        a_view = aHL.rearrange("(b o) p i q -> b i p o q", b=B)

        with nc.Block() as block:

            @block.sync
            def _(sp):
                for i in range(2):
                    sp.dma_start(wraw[:, i], proj_w.rearrange("(t p) n -> p t n", p=P)[:, :, i * CH:(i + 1) * CH]
                                 ).then_inc(w_loaded, 16)
                sp.dma_start(pb[:], proj_b.rearrange("(a c) -> a c", a=1).broadcast_to([TT, C])).then_inc(consts, 16)
                sp.dma_start(dft[:], row_dft_d).then_inc(consts, 16)
                for b in range(B):
                    for t in range(NTT):
                        n = b * NTT + t
                        if t % TPC == 0:
                            j = t // TPC
                            if b:
                                sp.wait_ge(projected, (b - 1) * NTT + (j + 1) * TPC)
                            for i in range(2):
                                sp.dma_start(a[:, j, i].bitcast(F32), a_view[b, i][:, :, j * GK:(j + 1) * GK]
                                             ).then_inc(a_loaded[j], 16)
                        if n >= 4:
                            sp.wait_ge(biased, n - 3)
                        sp.dma_start(xin[:, n % 4], x_view[b, t]).then_inc(x_loaded[n % 4], 16)

            @block.gpsimd
            def _(pool):
                pool.wait_ge(consts, 32)
                with pool.Fori(0, B) as b:
                    for t in range(NTT):
                        pool.wait_ge(x_loaded[t % 4], b * (NTT // 4 * 16) + (t // 4 + 1) * 16)
                        pool.wait_ge(x1_set, b * NTT + max(t - 1, 0))
                        nc.gpsimd.tensor_tensor(xb[:, t % 2], xin[:, t % 4], pb[:], ALU.add).then_inc(biased, 1)

            @block.tensor
            def _(pe):
                pe.wait_ge(consts, 32)
                pe.wait_ge(w_set, 2)
                with pe.Fori(0, B) as b:

                    def transform(t):
                        pe.wait_ge(x1_set, b * NTT + t + 1)
                        pe.wait_ge(f_set, b * NTT + max(t - 1, 0))
                        for i in range(2):
                            mm = nc.tensor.matmul(psF[t % 2][:, i, 0:CH], dft[:], x1[:, t % 2, i * CH:(i + 1) * CH],
                                                  start=True, stop=True)
                        mm.then_inc(transformed, 1)

                    for t in range(NTT):
                        j, u = t // TPC, t % TPC
                        if u == 0:
                            pe.wait_ge(a_loaded[j], (b + 1) * 32)
                        pe.wait_ge(x1_set, b * NTT + max(t - 1, 0))
                        for i in range(2):
                            k = 0
                            for ap, wq in ((0, 0), (0, 1), (1, 0)):
                                for ct in range(CT):
                                    mm = nc.tensor.matmul(psA[t % 2][:, i, 0:CH], a[:, j, ap, ct, u * TT:(u + 1) * TT],
                                                          wp[:, wq, ct, i * CH:(i + 1) * CH],
                                                          start=k == 0, stop=k == 3 * CT - 1)
                                    k += 1
                        mm.then_inc(projected, 1)
                        if t >= 1:
                            transform(t - 1)
                    transform(NTT - 1)

            @block.vector
            def _(dve):
                dve.wait_ge(w_loaded, 32)
                for i in range(2):
                    cols = slice(i * CH, (i + 1) * CH)
                    nc.vector.tensor_copy(wp[:, 0, :, cols], wraw[:, i]).then_inc(w_hi, 1)
                    dve.wait_ge(w_hi, i + 1)
                    nc.vector.tensor_tensor(wp[:, 1, :, cols], wraw[:, i], wp[:, 0, :, cols].bitcast(F32),
                                            ALU.subtract).then_inc(w_set, 1)
                with dve.Fori(0, B) as b:
                    for t in range(NTT):
                        dve.wait_ge(projected, b * NTT + t + 1)
                        dve.wait_ge(biased, b * NTT + t + 1)
                        dve.wait_ge(x1_stored[t % 2], b * (NTT // 2 * 16) + t // 2 * 16)
                        dve.wait_ge(transformed, b * NTT + max(t - 1, 0))
                        nc.vector.tensor_tensor(x1[:, t % 2].rearrange("p (i c) -> p i c", i=2),
                                                psA[t % 2][:, :, 0:CH],
                                                xb[:, t % 2].rearrange("p (i c) -> p i c", i=2),
                                                ALU.add).then_inc(x1_set, 1)

            @block.scalar
            def _(act):
                with act.Fori(0, B) as b:
                    for t in range(NTT):
                        act.wait_ge(x1_set, b * NTT + t + 1)
                        act.dma_start(x1_view[b, t], x1[:, t % 2]).then_inc(x1_stored[t % 2], 16)
                        act.wait_ge(transformed, b * NTT + t + 1)
                        act.wait_ge(f_stored[t % 2], b * (NTT // 2 * 16) + t // 2 * 16)
                        nc.scalar.activation(f[:, t % 2].rearrange("p (i c) -> p i c", i=2), psF[t % 2][:, :, 0:CH],
                                             ACT.Copy).then_inc(f_set, 1)
                        act.wait_ge(f_set, b * NTT + t + 1)
                        act.dma_start(f_view[b, t], f[:, t % 2]).then_inc(f_stored[t % 2], 16)
                for i in range(2):
                    act.wait_ge(x1_stored[i], B * NTT // 2 * 16)
                    act.wait_ge(f_stored[i], B * NTT // 2 * 16)


NG = (KWF + 1) // 2
NF = KWF * H
NQ = 3
FQ = NF // NQ
GB = BS // GC
BH = NB // 2


def spectrum(nc, w1_d, b1_d, w2_d, b2_d, col_dft_d, icol_dft_d, indb_d, indbT_d, rowsD, specD):
    with ExitStack() as ctx:
        def sb(name, shape, dt=F32):
            return ctx.enter_context(nc.sbuf_tensor("spec_" + name, shape, dt))

        def sem(name):
            return ctx.enter_context(nc.semaphore("spec_" + name))

        col = sb("col_dft", [RI * H, RI * H])
        icol = sb("icol_dft", [2 * H, 3, 2 * H])
        w1 = sb("w1", [BS, NB, 3, BS])
        w1s = sb("w1_scaled", [BS, NB, 3, BS])
        w2 = sb("w2", [BS, NB, 2, 2, BS])
        b1 = sb("b1", [BS, NB, RI])
        b2 = sb("b2", [2 * H, NB, RI, BS])
        indb = sb("indb", [BS, GB])
        indbT = sb("indbT", [GB, BS])
        rows = sb("rows", [RI * H, 3, C])
        xf = sb("xf", [BS, NB, RI, KWF, H])
        dc = sb("dc", [BS, NB])
        dcm = sb("dc_centred", [BS, NB])
        energy = sb("energy", [BS, 2, NB])
        power = sb("power", [BS, NB])
        total = sb("total", [BS, NB])
        gsum = sb("group_sum", [GB, NB])
        gvar = sb("group_var", [GB, NB])
        gstd = sb("group_std", [GB, NB])
        grstd = sb("group_rstd", [GB, NB])
        rstd = sb("rstd", [BS, NB])
        epst = sb("eps", [GB, 1])
        hid = sb("hidden", [BS, 2, RI, NF])
        pre = sb("pre", [2 * H, 2, 2, RI, BS])
        clamped = sb("clamped", [2 * H, 2, 2, RI, BS])
        y = sb("y", [2 * H, NG, RI, CH])
        g = sb("g", [2 * H, 2, RI, CH])
        ps = [ctx.enter_context(nc.psum_tensor(f"spec_ps{i}", [P, 512], F32)) for i in range(8)]

        consts = sem("consts")
        ready = sem("ready")
        rows_loaded = [sem(f"rows_loaded{i}") for i in range(3)]
        column = sem("column")
        col_lo = sem("col_lo")
        col_hi = sem("col_hi")
        dc_set = sem("dc_set")
        dc_zero = sem("dc_zero")
        squared = sem("squared")
        group_pe = sem("group_pe")
        gsum_set = sem("gsum_set")
        dcm_set = sem("dcm_set")
        power_set = sem("power_set")
        sq_set = sem("sq_set")
        total_set = sem("total_set")
        gvar_set = sem("gvar_set")
        gstd_set = sem("gstd_set")
        grstd_set = sem("grstd_set")
        rstd_set = sem("rstd_set")
        normed = sem("normed")
        layer1 = sem("layer1")
        gelued = sem("gelued")
        layer2 = sem("layer2")
        pre_set = sem("pre_set")
        clamp_set = sem("clamp_set")
        y_set = sem("y_set")
        inv_re = sem("inv_re")
        inv_im = sem("inv_im")
        g_re = sem("g_re")
        g_im = sem("g_im")
        g_stored = [sem(f"g_stored{i}") for i in range(2)]

        U1 = NB * NQ * RI
        G2 = (NG + 1) // 2
        U2 = NB * G2
        U3 = 2 * NG
        NCONST = 14

        spec_view = specD.rearrange("b h k r c -> b k h r c")

        def kws(i):
            return min(2, KWF - 2 * i)

        def stores_before(b, u):
            return b * KWF + sum(kws(v % NG) for v in range(u) if v % 2 == u % 2)

        with nc.Block() as block:

            @block.sync
            def _(sp):
                for dst, src in ((col[:], col_dft_d), (icol[:], icol_dft_d), (indb[:], indb_d), (indbT[:], indbT_d),
                                 (b1[:], b1_d),
                                 (b2[:].rearrange("p n r c -> p (n r c)"),
                                  b2_d.rearrange("(a c) -> a c", a=1).broadcast_to([2 * H, NB * RI * BS])),
                                 (w1[:, :, 0], w1_d[0].rearrange("n i o -> i n o")),
                                 (w1[:, :, 1], w1_d[1].rearrange("n i o -> i n o")),
                                 (w2[:, :, 0, 0], w2_d[0].rearrange("n i o -> i n o")),
                                 (w2[:, :, 0, 1], w2_d[1].rearrange("n i o -> i n o")),
                                 (w2[:, :, 1, 1], w2_d[0].rearrange("n i o -> i n o"))):
                    sp.dma_start(dst, src).then_inc(consts, 16)
                for b in range(B):
                    for k in range(KWF):
                        n = b * KWF + k
                        if n >= 3:
                            sp.wait_ge(column, n - 2)
                        for r in range(RI):
                            sp.dma_start(rows[r * H:(r + 1) * H, n % 3], rowsD[b, :, k, r]).then_inc(rows_loaded[n % 3], 16)

            @block.gpsimd
            def _(pool):
                with pool.Fori(0, B) as b:
                    for u in range(U3):
                        half, i = u // NG, u % NG
                        m = kws(i)
                        pool.wait_ge(g_re, b * U3 + u + 1)
                        pool.wait_ge(g_im, b * U3 + u + 1)
                        for k in range(m):
                            pool.dma_start(spec_view[b, 2 * i + k][:, :, half * CH:(half + 1) * CH],
                                           g[k * H:(k + 1) * H, u % 2]).then_inc(g_stored[u % 2], 16)
                for i in range(2):
                    pool.wait_ge(g_stored[i], B * 2 * KWF // 2 * 16)

            @block.tensor
            def _(pe):
                pe.wait_ge(consts, 11 * 16)
                pe.wait_ge(ready, 3)
                for b in range(B):
                    for k in range(KWF):
                        n = b * KWF + k
                        pe.wait_ge(rows_loaded[n % 3], (n // 3 + 1) * 32)
                        if n >= 2:
                            pe.wait_ge(col_lo, n - 1)
                            pe.wait_ge(col_hi, n - 1)
                        if k < 2:
                            pe.wait_ge(gelued, b * U1)
                        for blk in range(NB):
                            bank = ps[2 * (n % 2) + blk // BH]
                            mm = nc.tensor.matmul(bank[0:BS, blk % BH * (RI * H):(blk % BH + 1) * (RI * H)],
                                                  rows[:, n % 3, blk * BS:(blk + 1) * BS], col[:],
                                                  start=True, stop=True)
                        mm.then_inc(column, 1)
                    pe.wait_ge(dc_set, b + 1)
                    pe.wait_ge(pre_set, b * U2)
                    nc.tensor.matmul(ps[4][0:GB, 0:NB], indb[:], dc[:], start=True, stop=True).then_inc(group_pe, 1)
                    pe.wait_ge(gsum_set, b + 1)
                    nc.tensor.matmul(ps[5][0:BS, 0:NB], indbT[:], gsum[:], start=True, stop=True).then_inc(group_pe, 1)
                    pe.wait_ge(total_set, b + 1)
                    pe.wait_ge(g_re, b * U3)
                    nc.tensor.matmul(ps[6][0:GB, 0:NB], indb[:], total[:], start=True, stop=True).then_inc(group_pe, 1)
                    pe.wait_ge(grstd_set, b + 1)
                    pe.wait_ge(g_im, b * U3)
                    nc.tensor.matmul(ps[7][0:BS, 0:NB], indbT[:], grstd[:], start=True, stop=True).then_inc(group_pe, 1)
                    pe.wait_ge(normed, b + 1)

                    def first(blk):
                        for q in range(NQ):
                            for r in range(RI):
                                u = (blk * NQ + q) * RI + r
                                if u >= 4:
                                    pe.wait_ge(gelued, b * U1 + u - 3)
                                elif u == 0:
                                    pe.wait_ge(col_lo, (b + 1) * KWF)
                                    pe.wait_ge(col_hi, (b + 1) * KWF)
                                xs = [xf[:, blk, i].rearrange("p k h -> p (k h)")[:, q * FQ:(q + 1) * FQ] for i in range(RI)]
                                nc.tensor.matmul(ps[u % 4][0:BS, 0:FQ], w1s[:, blk, 0], xs[r], start=True, stop=False)
                                nc.tensor.matmul(ps[u % 4][0:BS, 0:FQ], w1s[:, blk, 2 - r], xs[1 - r],
                                                 start=False, stop=True).then_inc(layer1, 1)

                    def second(blk):
                        pe.wait_ge(gelued, b * U1 + (blk + 1) * (NQ * RI))
                        for i in range(NG):
                            u = blk * G2 + i // 2
                            if i % 2 == 0 and u >= 2:
                                pe.wait_ge(pre_set, b * U2 + u - 1)
                            m = kws(i) * H
                            out = ps[4 + u % 2][0:m, i % 2 * (RI * BS):(i % 2 + 1) * (RI * BS)]
                            for r in range(RI):
                                mm = nc.tensor.matmul(out, hid[:, blk % 2, r, 2 * i * H:2 * i * H + m],
                                                      w2[:, blk, r].rearrange("p a o -> p (a o)"),
                                                      start=r == 0, stop=r == RI - 1)
                            if i % 2 or i == NG - 1:
                                mm.then_inc(layer2, 1)

                    def inverse(half):
                        for i in range(NG):
                            u = half * NG + i
                            m = kws(i) * H
                            if i % 2 == 0:
                                pe.wait_ge(y_set, b * U2 + (half * BH + BH - 1) * G2 + i // 2 + 1)
                            for r, bank, done, read in ((0, ps[6], inv_re, g_re), (1, ps[7], inv_im, g_im)):
                                pe.wait_ge(read, b * U3 + u)
                                nc.tensor.matmul(bank[0:m, 0:CH], icol[0:m, 0, 0:m], y[0:m, i, r], start=True, stop=False)
                                nc.tensor.matmul(bank[0:m, 0:CH], icol[0:m, 2 - r, 0:m], y[0:m, i, 1 - r],
                                                 start=False, stop=True).then_inc(done, 1)

                    first(0)
                    for blk in range(1, NB):
                        first(blk)
                        second(blk - 1)
                        if blk == BH:
                            inverse(0)
                    second(NB - 1)
                    inverse(1)

            @block.scalar
            def _(act):
                act.wait_ge(consts, 11 * 16)
                act.wait_ge(ready, 3)
                for b in range(B):
                    for k in range(KWF):
                        n = b * KWF + k
                        act.wait_ge(column, n + 1)
                        if k == 0:
                            act.wait_ge(layer1, b * U1)
                        nc.scalar.activation(xf[:, 0:BH, :, k],
                                             ps[2 * (n % 2)][0:BS, 0:CH].rearrange("p (n r h) -> p n r h", r=RI, h=H),
                                             ACT.Copy).then_inc(col_lo, 1)
                    act.wait_ge(dc_zero, b + 1)
                    act.wait_ge(layer2, b * U2)
                    for blk in range(NB):
                        nc.scalar.activation(hid[:, 0].rearrange("p r f -> p (r f)")[:, 0:RI * (KWF - 2) * H].rearrange(
                            "p (r k h) -> p r k h", r=RI, h=H), xf[:, blk, :, 1:KWF - 1], ACT.Square,
                            accum_out=energy[:, 0, blk:blk + 1]).then_inc(squared, 1)
                        nc.scalar.activation(hid[:, 1].rearrange("p r f -> p (r f)")[:, 0:RI * 2 * H].rearrange(
                            "p (r k h) -> p r k h", r=RI, h=H), xf[:, blk, :, 0:KWF:KWF - 1], ACT.Square,
                            accum_out=energy[:, 1, blk:blk + 1]).then_inc(squared, 1)
                        act.wait_ge(squared, b * (2 * NB) + 2 * blk + 2)
                    act.wait_ge(gvar_set, b + 1)
                    nc.scalar.activation(gstd[:], gvar[:], ACT.Sqrt, bias=epst[:]).then_inc(gstd_set, 1)

                    def gelu(blk):
                        for q in range(NQ):
                            for r in range(RI):
                                u = (blk * NQ + q) * RI + r
                                act.wait_ge(layer1, b * U1 + u + 1)
                                if q == 0 and r == 0 and blk >= 2:
                                    act.wait_ge(layer2, b * U2 + (blk - 1) * G2)
                                nc.scalar.activation(hid[:, blk % 2, r, q * FQ:(q + 1) * FQ], ps[u % 4][0:BS, 0:FQ],
                                                     ACT.Gelu, bias=b1[:, blk, r:r + 1]).then_inc(gelued, 1)

                    def evacuate(half):
                        for i in range(NG):
                            u = half * NG + i
                            m = kws(i) * H
                            act.wait_ge(inv_re, b * U3 + u + 1)
                            act.wait_ge(g_stored[u % 2], stores_before(b, u) * 16)
                            nc.scalar.activation(g[0:m, u % 2, 0], ps[6][0:m, 0:CH], ACT.Copy).then_inc(g_re, 1)

                    for blk in range(NB):
                        gelu(blk)
                        if blk == BH:
                            evacuate(0)
                    evacuate(1)

            @block.vector
            def _(dve):
                dve.wait_ge(consts, 11 * 16)
                nc.vector.memset(epst[:], EPS).then_inc(ready, 1)
                nc.vector.tensor_scalar(w1[:, :, 2], w1[:, :, 1], -1.0, None, ALU.mult).then_inc(ready, 1)
                nc.vector.tensor_scalar(w2[:, :, 1, 0], w2[:, :, 0, 1], -1.0, None, ALU.mult).then_inc(ready, 1)
                dve.wait_ge(ready, 3)
                for b in range(B):
                    for k in range(KWF):
                        n = b * KWF + k
                        dve.wait_ge(column, n + 1)
                        if k == 0:
                            dve.wait_ge(layer1, b * U1)
                        nc.vector.tensor_copy(xf[:, BH:NB, :, k],
                                              ps[2 * (n % 2) + 1][0:BS, 0:CH].rearrange("p (n r h) -> p n r h", r=RI, h=H)
                                              ).then_inc(col_hi, 1)
                    dve.wait_ge(col_lo, (b + 1) * KWF)
                    dve.wait_ge(col_hi, (b + 1) * KWF)
                    nc.vector.tensor_copy(dc[:], xf[:, :, 0, 0, 0]).then_inc(dc_set, 1)
                    dve.wait_ge(dc_set, b + 1)
                    nc.vector.memset(xf[:, :, 0, 0, 0:1], 0.0).then_inc(dc_zero, 1)
                    dve.wait_ge(group_pe, 4 * b + 1)
                    nc.vector.tensor_scalar(gsum[:], ps[4][0:GB, 0:NB], 1.0 / GC, None, ALU.mult).then_inc(gsum_set, 1)
                    dve.wait_ge(group_pe, 4 * b + 2)
                    nc.vector.tensor_tensor(dcm[:], dc[:], ps[5][0:BS, 0:NB], ALU.subtract).then_inc(dcm_set, 1)
                    dve.wait_ge(squared, (b + 1) * (2 * NB))
                    nc.vector.scalar_tensor_tensor(out=power[:], in0=energy[:, 0], scalar=2.0, in1=energy[:, 1],
                                                   op0=ALU.mult, op1=ALU.add).then_inc(power_set, 1)
                    dve.wait_ge(dcm_set, b + 1)
                    nc.vector.tensor_tensor(total[:], dcm[:], dcm[:], ALU.mult).then_inc(sq_set, 1)
                    dve.wait_ge(power_set, b + 1)
                    dve.wait_ge(sq_set, b + 1)
                    nc.vector.tensor_tensor(total[:], total[:], power[:], ALU.add).then_inc(total_set, 1)
                    dve.wait_ge(group_pe, 4 * b + 3)
                    nc.vector.tensor_scalar(gvar[:], ps[6][0:GB, 0:NB], 1.0 / (GC * S), None, ALU.mult).then_inc(gvar_set, 1)
                    dve.wait_ge(gstd_set, b + 1)
                    nc.vector.reciprocal(grstd[:], gstd[:]).then_inc(grstd_set, 1)
                    dve.wait_ge(group_pe, 4 * b + 4)
                    nc.vector.tensor_copy(rstd[:], ps[7][0:BS, 0:NB]).then_inc(rstd_set, 1)
                    dve.wait_ge(rstd_set, b + 1)
                    nc.vector.tensor_copy(xf[:, :, 0, 0, 0], dcm[:])
                    for blk in range(NB):
                        ins = nc.vector.tensor_scalar(w1s[:, blk], w1[:, blk], rstd[:, blk:blk + 1], None, ALU.mult)
                    ins.then_inc(normed, 1)

                    def shrink(blk):
                        for j in range(G2):
                            u = blk * G2 + j
                            w = min(2, NG - 2 * j)
                            m = kws(2 * j) * H
                            bank = ps[4 + u % 2][0:m, 0:w * RI * BS].rearrange("p (i r c) -> p i r c", r=RI, c=BS)
                            bias = b2[0:m, blk].rearrange("p (a r) c -> p a r c", a=1).broadcast_to([m, w, RI, BS])
                            dve.wait_ge(layer2, b * U2 + u + 1)
                            nc.vector.tensor_tensor(pre[0:m, u % 2, 0:w], bank, bias, ALU.add).then_inc(pre_set, 1)
                            dve.wait_ge(pre_set, b * U2 + u + 1)
                            nc.vector.tensor_scalar(clamped[0:m, u % 2, 0:w], pre[0:m, u % 2, 0:w], -SPARSITY, SPARSITY,
                                                    ALU.max, ALU.min).then_inc(clamp_set, 1)
                            dve.wait_ge(clamp_set, b * U2 + u + 1)
                            if blk % BH == 0:
                                dve.wait_ge(inv_im, b * U3 + (blk // BH) * NG)
                            nc.vector.tensor_tensor(y[0:m, 2 * j:2 * j + w, :, blk % BH * BS:(blk % BH + 1) * BS],
                                                    pre[0:m, u % 2, 0:w], clamped[0:m, u % 2, 0:w],
                                                    ALU.subtract).then_inc(y_set, 1)

                    def evacuate(half):
                        for i in range(NG):
                            u = half * NG + i
                            m = kws(i) * H
                            dve.wait_ge(inv_im, b * U3 + u + 1)
                            dve.wait_ge(g_stored[u % 2], stores_before(b, u) * 16)
                            nc.vector.tensor_copy(g[0:m, u % 2, 1], ps[7][0:m, 0:CH]).then_inc(g_im, 1)

                    for blk in range(NB):
                        shrink(blk)
                        if blk % BH == BH - 1:
                            evacuate(blk // BH)


def image(nc, irow_dft_d, x1D, specD, out):
    with ExitStack() as ctx:
        def sb(name, shape, dt=F32):
            return ctx.enter_context(nc.sbuf_tensor("image_" + name, shape, dt))

        def sem(name):
            return ctx.enter_context(nc.semaphore("image_" + name))

        NBUF = 4
        dft = sb("irow_dft", [TR * FR, TT])
        f = sb("spectrum", [TR * FR, NBUF, C])
        x1 = sb("x1", [TT, NBUF, C])
        o = sb("o", [TT, NBUF, C])
        ps = [ctx.enter_context(nc.psum_tensor(f"image_ps{i}", [TT, 2, 512], F32)) for i in range(4)]
        consts = sem("consts")
        loaded = [sem(f"loaded{i}") for i in range(NBUF)]
        transformed = sem("transformed")
        o_set = sem("o_set")
        stored = [sem(f"stored{i}") for i in range(NBUF)]

        f_view = specD.rearrange("b (t h) k r c -> (b t) (h k r) c", h=TR)
        x_view = x1D.rearrange("b (t p) c -> (b t) p c", p=TT)
        o_view = out.rearrange("b (t p) c -> (b t) p c", p=TT)
        NS = B * NTT // NBUF

        with nc.Block() as block:

            @block.sync
            def _(sp):
                sp.dma_start(dft[:], irow_dft_d).then_inc(consts, 16)
                with sp.Fori(0, NS) as g:
                    for i in range(NBUF):
                        sp.wait_ge(o_set, g * NBUF)
                        sp.dma_start(f[:, i], f_view[g * NBUF + i]).then_inc(loaded[i], 16)
                        sp.dma_start(x1[:, i], x_view[g * NBUF + i]).then_inc(loaded[i], 16)

            @block.tensor
            def _(pe):
                pe.wait_ge(consts, 16)
                with pe.Fori(0, NS) as g:
                    for i in range(NBUF):
                        pe.wait_ge(loaded[i], g * 32 + 32)
                        pe.wait_ge(o_set, g * NBUF)
                        for h in range(2):
                            mm = nc.tensor.matmul(ps[i][:, h, 0:CH], dft[:], f[:, i, h * CH:(h + 1) * CH],
                                                  start=True, stop=True)
                        mm.then_inc(transformed, 1)

            @block.vector
            def _(dve):
                with dve.Fori(0, NS) as g:
                    for i in range(NBUF):
                        dve.wait_ge(transformed, g * NBUF + i + 1)
                        dve.wait_ge(stored[i], g * 16)
                        nc.vector.tensor_tensor(o[:, i].rearrange("p (h c) -> p h c", h=2), ps[i][:, :, 0:CH],
                                                x1[:, i].rearrange("p (h c) -> p h c", h=2), ALU.add).then_inc(o_set, 1)

            @block.scalar
            def _(act):
                with act.Fori(0, NS) as g:
                    for i in range(NBUF):
                        act.wait_ge(o_set, g * NBUF + i + 1)
                        act.dma_start(o_view[g * NBUF + i], o[:, i]).then_inc(stored[i], 16)
                for i in range(NBUF):
                    act.wait_ge(stored[i], NS * 16)


def tables():
    def cs(n, m, size):
        k = np.outer(np.arange(n), np.arange(m)) % size
        c, s = np.cos(2 * np.pi * k / size), np.sin(2 * np.pi * k / size)
        s[(2 * k) % size == 0] = 0
        return c, s

    f32 = np.float32
    t = {"ident": np.eye(P, dtype=f32)}
    gi = (np.arange(C)[:, None] // GC == np.arange(GROUPS)).astype(f32)
    t["ind"] = np.ascontiguousarray(gi.reshape(CT, P, GROUPS).transpose(1, 0, 2))
    t["indT"] = np.ascontiguousarray(gi.T)
    gb = (np.arange(BS)[:, None] // GC == np.arange(GB)).astype(f32)
    t["indb"], t["indbT"] = gb, np.ascontiguousarray(gb.T)
    keys = np.arange(S).reshape(H, KG, KW).transpose(1, 0, 2).reshape(-1)
    kh, kw = keys // W, keys % W
    rows = (np.arange(H)[:, None] == kh).astype(f32)
    cols = (np.arange(W)[:, None] == kw).astype(f32)
    part = (np.arange(KW)[:, None] == kw % KW).astype(f32)
    t["hot_max"] = np.concatenate([rows, part])
    t["hot2"] = np.concatenate([cols, rows[:16]])
    t["hot3"] = np.concatenate([cols, rows[16:], rows[:-1], np.ones((1, S), f32)])
    c, s = cs(W, KWF, W)
    row = np.zeros((TR, W, TR, KWF, RI))
    irow = np.zeros((TR, KWF, RI, TR, W))
    mirrored = np.where((np.arange(KWF) == 0) | (np.arange(KWF) == KWF - 1), 1, 2)[:, None]
    for h in range(TR):
        row[h, :, h, :, 0], row[h, :, h, :, 1] = c, -s
        irow[h, :, 0, h], irow[h, :, 1, h] = mirrored * c.T, -mirrored * s.T
    t["row_dft"] = (row.reshape(TT, TR * FR) / W ** 0.5).astype(f32)
    t["irow_dft"] = (irow.reshape(TR * FR, TT) / W ** 0.5).astype(f32)
    c, s = cs(H, H, H)
    col = np.zeros((RI, H, RI, H))
    col[0, :, 0], col[1, :, 0], col[0, :, 1], col[1, :, 1] = c, s, -s, c
    t["col_dft"] = (col.reshape(RI * H, RI * H) / H ** 0.5).astype(f32)
    icol = np.zeros((2, H, 3, 2, H))
    for k in range(2):
        icol[k, :, 0, k], icol[k, :, 1, k], icol[k, :, 2, k] = c, s, -s
    t["icol_dft"] = (icol.reshape(2 * H, 3, 2 * H) / H ** 0.5).astype(f32)
    return t


def build(nc, a, out):
    def scratch(name, shape):
        return nc.dram_tensor(name, shape, F32).ap()

    x = a["x"].rearrange("b h w c -> b (h w) c")
    qF = scratch("q_scratch", (NP, P, S))
    qHL = scratch("q_split_scratch", (NP, P, 2, S))
    kHL = scratch("k_split_scratch", (NP, P, 2, S))
    vD = scratch("v_scratch", (NP, P, KT, P))
    relH = scratch("row_logits_scratch", (NP, 2, 2 * H, S))
    relW = scratch("column_logits_scratch", (NP, 2, 2 * W, S))
    maxD = scratch("maximum_scratch", (NP, 2, S))
    aHL = scratch("attention_scratch", (NP, P, 2, S))
    x1D = scratch("x1_scratch", (B, S, C))
    rowsD = scratch("row_spectrum_scratch", (B, H, KWF, RI, C))
    specD = scratch("mixed_spectrum_scratch", (B, H, KWF, RI, C))
    project(nc, x, a["qkv_w"], a["qk_bias"], a["qkv_b"], a["ident"], a["ind"], a["indT"], qF, qHL, kHL, vD)
    relpos(nc, a["rev_h"], a["rev_w"], qF, relH, relW)
    attend(nc, a["ident"], a["hot_max"], a["hot2"], a["hot3"], qHL, kHL, vD, relH, relW, maxD, aHL)
    out_project(nc, x, a["proj_w"], a["proj_b"], a["row_dft"], aHL, x1D, rowsD)
    spectrum(nc, a["w1"], a["b1"], a["w2"], a["b2"], a["col_dft"], a["icol_dft"], a["indb"], a["indbT"], rowsD, specD)
    image(nc, a["irow_dft"], x1D, specD, out.rearrange("b h w c -> b (h w) c"))


def kernel(**inputs):
    import concourse.bacc as bacc
    from concourse.bass_utils import run_bass_kernel_spmd

    i = {k: np.asarray(v) for k, v in inputs.items()}
    arrays = dict(
        x=i["x"], qkv_w=i["L0_conv_qkv_w"], qkv_b=i["L0_conv_qkv_b"],
        qk_bias=i["L0_conv_qkv_b"][:2 * C].reshape(2 * PAIRS, P).T,
        proj_w=i["L0_conv_proj_w"], proj_b=i["L0_conv_proj_b"],
        rev_h=i["L0_conv_rel_pos_h"][::-1].T, rev_w=i["L0_conv_rel_pos_w"][::-1].T,
        w1=i["L1_conv_w1"], b1=i["L1_conv_b1"].transpose(2, 1, 0),
        w2=i["L1_conv_w2"], b2=i["L1_conv_b2"].transpose(1, 0, 2).reshape(-1), **tables())
    arrays = {k: np.ascontiguousarray(v) for k, v in arrays.items()}
    nc = bacc.Bacc("TRN2", target_bir_lowering=False, num_devices=1)
    aps = {k: nc.dram_tensor(f"in_{k}", v.shape, F32, kind="ExternalInput").ap() for k, v in arrays.items()}
    out = nc.dram_tensor("out_image", (B, H, W, C), F32, kind="ExternalOutput").ap()
    build(nc, aps, out)
    result = run_bass_kernel_spmd(nc, [{f"in_{k}": v for k, v in arrays.items()}], core_ids=[0])
    return result.results[0]["out_image"]
```

```python
from contextlib import ExitStack

import concourse.bass as bass
import numpy as np
from concourse import mybir
from concourse.alu_op_type import AluOpType as ALU

F32 = mybir.dt.float32
F32R = mybir.dt.float32r
ACT = mybir.ActivationFunctionType
AX_X = mybir.AxisListType.X

P = 128
B, H, W, C = 2, 48, 48, 768
S = H * W
CT = C // P
HEADS, D = 12, 64
PAIRS = HEADS // 2
NP = B * PAIRS
KT = S // P
KG = 3
GK = S // KG
KW = W // KG
KR = P // KW
GROUPS = 32
GC = C // GROUPS
EPS = 1e-5
SCALE = D ** -0.5
NREL = 2 * H - 1

QC = 5
ROWS = [10, 10, 10, 10, 8]
QN = [r * W for r in ROWS]
Q0 = [10 * W * c for c in range(QC)]
QMAX = QN[0]

TG = 384
NTG = S // TG
TPG = TG // P

SPARSITY = 0.01
NB, BS = 8, 96
KWF = W // 2 + 1
RI = 2


def natural(ap):
    return ap.rearrange("p (j h w) -> p h j w", j=KG, w=KW)


def project(nc, x, qkv_w, qk_bias, qkv_b, ident_d, ind_d, indT_d, qF, qHL, kHL, vD):
    with ExitStack() as ctx:
        def sb(name, shape, dt=F32):
            return ctx.enter_context(nc.sbuf_tensor("project_" + name, shape, dt))

        def sem(name):
            return ctx.enter_context(nc.semaphore("project_" + name))

        xh = sb("xn_hi", [P, CT, S], F32R)
        xl = sb("xn_lo", [P, CT, S], F32R)
        xtok = sb("x_tokens", [P, 2, TPG, C])
        ident = sb("ident", [P, P])
        ind = sb("ind", [P, CT, GROUPS])
        indT = sb("indT", [GROUPS, C])
        qb = sb("q_bias", [P, 2 * PAIRS])
        vb = sb("v_bias", [P, C])
        stats = sb("stats", [P, CT, NTG, 6])
        mv = sb("mean_var", [P, CT, 2])
        gate = sb("gate", [P, 1])
        dev = sb("deviation", [P, CT])
        within = sb("within", [P, CT])
        gm = sb("group_mean", [GROUPS, 1])
        gv = sb("group_var", [GROUPS, 1])
        gs = sb("group_std", [GROUPS, 1])
        gr = sb("group_rstd", [GROUPS, 1])
        epst = sb("eps", [GROUPS, 1])
        cm = sb("channel_mean", [P, CT])
        cr = sb("channel_rstd", [P, CT])
        cb = sb("channel_shift", [P, CT])
        xn = sb("xn", [P, 4, TG])
        wraw = sb("w_raw", [P, 2, CT, P])
        whl = sb("w_split", [P, 2, 2, CT, P], F32R)
        row = sb("qk_row", [P, 2, QMAX])
        hl = sb("qk_split", [P, 2, S], F32R)
        wv = [sb("wv_split", [P, 2, CT, TG], F32R), hl[:].rearrange("p i (t n) -> p i t n", n=TG)]
        vout = sb("v_out", [P, 2, TG])
        ps = [ctx.enter_context(nc.psum_tensor(f"project_ps{i}", [P, 512], F32)) for i in range(8)]

        consts = sem("consts")
        eps_set = sem("eps_set")
        x_loaded = [sem(f"x_loaded{i}") for i in range(2)]
        transposed = sem("transposed")
        st_done = sem("st_done")
        chain = sem("dve_chain")
        gsum_ready = sem("gsum_ready")
        gmean_set = sem("gmean_set")
        within_set = sem("within_set")
        gvar_set = sem("gvar_set")
        gstd_set = sem("gstd_set")
        grstd_set = sem("grstd_set")
        shift_set = sem("shift_set")
        xn_written = sem("xn_written")
        xh_set = sem("xh_set")
        xhl_written = sem("xhl_written")
        w_loaded = [sem(f"w_loaded{i}") for i in range(2)]
        wh_set = sem("wh_set")
        w_split = sem("w_split_done")
        qk_product = sem("qk_product")
        qk_biased = sem("qk_biased")
        qk_hi = sem("qk_hi")
        qk_lo = sem("qk_lo")
        qrow_stored = [sem(f"qrow_stored{i}") for i in range(2)]
        qk_stored = sem("qk_stored")
        wv_loaded = [sem(f"wv_loaded{i}") for i in range(2)]
        wvh_set = sem("wvh_set")
        wv_split = sem("wv_split_done")
        v_product = sem("v_product")
        v_biased = sem("v_biased")
        v_stored = [sem(f"v_stored{i}") for i in range(2)]

        EARLY = NTG - 2
        NTP = NTG * CT
        OT = 2 * PAIRS
        NVH = C // TG
        x_view = x.rearrange("b (g t p) c -> b g p t c", t=TPG, p=P)
        w_view = qkv_w.rearrange("(t p) n -> p t n", p=P)

        with nc.Block() as block:

            @block.sync
            def _(sp):
                for dst, src in ((ident[:], ident_d), (ind[:], ind_d), (indT[:], indT_d),
                                 (qb[:], qk_bias),
                                 (vb[:], qkv_b[2 * C:3 * C].rearrange("(a c) -> a c", a=1).broadcast_to([P, C]))):
                    sp.dma_start(dst, src).then_inc(consts, 16)
                with sp.Fori(0, B) as b:
                    for o in range(2):
                        sp.wait_ge(w_split, b * OT)
                        sp.dma_start(wraw[:, o], w_view[:, :, o * P:(o + 1) * P]).then_inc(w_loaded[o], 16)
                    for pas in range(2):
                        for g in range(NTG):
                            n = pas * NTG + g
                            if n < 2:
                                sp.wait_ge(wv_split, b * NVH)
                            else:
                                sp.wait_ge(transposed, b * (2 * NTP) + (n - 1) * CT)
                            sp.dma_start(xtok[:, g % 2], x_view[b, g]).then_inc(x_loaded[g % 2], 16)
                    for vh in range(NVH):
                        sp.wait_ge(transposed, (b + 1) * (2 * NTP))
                        sp.dma_start(xtok[:, vh].rearrange("p a (c n) -> p (a c) n", n=TG),
                                     w_view[:, :, 2 * C + vh * TG:2 * C + (vh + 1) * TG]).then_inc(wv_loaded[vh], 16)
                    for o in range(1, OT + 1):
                        if 2 <= o < OT:
                            sp.wait_ge(w_split, b * OT + o - 1)
                            sp.dma_start(wraw[:, o % 2], w_view[:, :, o * P:(o + 1) * P]).then_inc(w_loaded[o % 2], 16)
                        m = o - 1
                        if m < PAIRS:
                            for c in range(QC):
                                n = m * QC + c
                                sp.wait_ge(qk_biased, b * (OT * QC) + n + 1)
                                sp.dma_start(qF[b * PAIRS + m][:, Q0[c]:Q0[c] + QN[c]],
                                             row[:, n % 2, 0:QN[c]]).then_inc(qrow_stored[n % 2], 16)
                        sp.wait_ge(qk_lo, b * (OT * QC) + m * QC + QC)
                        dst = qHL if m < PAIRS else kHL
                        sp.dma_start(dst[b * PAIRS + m % PAIRS], hl[:].bitcast(F32)).then_inc(qk_stored, 16)
                sp.wait_ge(qk_stored, B * OT * 16)
                for i in range(2):
                    sp.wait_ge(qrow_stored[i], B * PAIRS * QC * 8)

            @block.tensor
            def _(pe):
                pe.wait_ge(consts, 5 * 16)
                with pe.Fori(0, B) as b:

                    def qk(n):
                        o, c = n // QC, n % QC
                        if o == 0:
                            pe.wait_ge(xhl_written, b * NTP + -(-(Q0[c] + QN[c]) // TG) * CT)
                        if c == 0:
                            pe.wait_ge(w_split, b * OT + o + 1)
                        if n >= 2:
                            pe.wait_ge(qk_biased, b * (OT * QC) + n - 1)
                        k = 0
                        for wp, xp in ((0, xh), (0, xl), (1, xh)):
                            for ct in range(CT):
                                cols = (natural(xp[:, ct])[:, 10 * c:10 * c + ROWS[c]] if o < PAIRS
                                        else xp[:, ct, Q0[c]:Q0[c] + QN[c]])
                                mm = nc.tensor.matmul(ps[4 + n % 2][:, 0:QN[c]], whl[:, o % 2, wp, ct],
                                                      cols, start=k == 0, stop=k == 3 * CT - 1)
                                k += 1
                        mm.then_inc(qk_product, 1)

                    for pas in range(2):
                        for g in range(NTG):
                            pe.wait_ge(x_loaded[g % 2], (b * NTG + pas * (NTG // 2) + g // 2 + 1) * 16)
                            for ct in range(CT):
                                n = g * CT + ct
                                if pas == 0 and n >= 4:
                                    pe.wait_ge(st_done, b * NTP + n - 3)
                                if pas == 0 and n == 0:
                                    pe.wait_ge(v_biased, b * (NVH * KT))
                                if pas == 1 and n >= 4:
                                    pe.wait_ge(xn_written, b * NTP + n - 3)
                                for t in range(TPG):
                                    mm = nc.tensor.transpose(ps[n % 4][:, t * P:(t + 1) * P],
                                                             xtok[:, g % 2, t, ct * P:(ct + 1) * P], ident[:])
                                mm.then_inc(transposed, 1)
                            if pas == 1 and g >= 2:
                                qk(g - 2)
                        if pas == 0:
                            pe.wait_ge(chain, b * 3 + 1)
                            for ct in range(CT):
                                mm = nc.tensor.matmul(ps[4][0:GROUPS, 0:1], ind[:, ct], mv[:, ct, 0:1],
                                                      start=ct == 0, stop=ct == CT - 1)
                            mm.then_inc(gsum_ready, 1)
                            pe.wait_ge(gmean_set, b + 1)
                            for ct in range(CT):
                                mm = nc.tensor.matmul(ps[5][:, ct:ct + 1], indT[:, ct * P:(ct + 1) * P], gm[:],
                                                      start=True, stop=True)
                            mm.then_inc(gsum_ready, 1)
                            pe.wait_ge(within_set, b + 1)
                            for ct in range(CT):
                                mm = nc.tensor.matmul(ps[6][0:GROUPS, 0:1], ind[:, ct], within[:, ct:ct + 1],
                                                      start=ct == 0, stop=ct == CT - 1)
                            mm.then_inc(gsum_ready, 1)
                            pe.wait_ge(grstd_set, b + 1)
                            for ct in range(CT):
                                mm = nc.tensor.matmul(ps[7][:, ct:ct + 1], indT[:, ct * P:(ct + 1) * P], gr[:],
                                                      start=True, stop=True)
                            mm.then_inc(gsum_ready, 1)
                    for n in range(EARLY, OT * QC):
                        qk(n)
                    for n in range(NVH * KT):
                        vh, t = n // KT, n % KT
                        if t == 0:
                            pe.wait_ge(wv_split, b * NVH + vh + 1)
                        if n >= 2:
                            pe.wait_ge(v_biased, b * (NVH * KT) + n - 1)
                        k = 0
                        for xp, wp in ((xh, 0), (xh, 1), (xl, 0)):
                            for ct in range(CT):
                                mm = nc.tensor.matmul(ps[6 + n % 2][:, 0:TG], xp[:, ct, t * P:(t + 1) * P], wv[vh][:, wp, ct],
                                                      start=k == 0, stop=k == 3 * CT - 1)
                                k += 1
                        mm.then_inc(v_product, 1)

            @block.scalar
            def _(act):
                act.wait_ge(consts, 5 * 16)
                act.wait_ge(eps_set, 1)
                with act.Fori(0, B) as b:

                    def bias(n):
                        o, c = n // QC, n % QC
                        act.wait_ge(qk_product, b * (OT * QC) + n + 1)
                        if n >= 2:
                            act.wait_ge(qk_lo, b * (OT * QC) + n - 1)
                        if o < PAIRS:
                            act.wait_ge(qrow_stored[n % 2], b * (PAIRS * QC * 8) + n // 2 * 16)
                        elif n < PAIRS * QC + 2:
                            act.wait_ge(qrow_stored[n % 2], (b + 1) * (PAIRS * QC * 8))
                        nc.scalar.activation(row[:, n % 2, 0:QN[c]], ps[4 + n % 2][:, 0:QN[c]], ACT.Identity,
                                             bias=qb[:, o:o + 1], scale=1.0).then_inc(qk_biased, 1)

                    act.wait_ge(gvar_set, b + 1)
                    nc.scalar.activation(gs[:], gv[:], ACT.Sqrt, bias=epst[:]).then_inc(gstd_set, 1)
                    act.wait_ge(shift_set, b + 1)
                    for n in range(NTP):
                        ct = n % CT
                        act.wait_ge(transposed, b * (2 * NTP) + NTP + n + 1)
                        if n >= 4:
                            act.wait_ge(xhl_written, b * NTP + n - 3)
                        nc.scalar.activation(xn[:, n % 4], ps[n % 4][:, 0:TG], ACT.Identity,
                                             bias=cb[:, ct:ct + 1], scale=cr[:, ct:ct + 1]).then_inc(xn_written, 1)
                        if ct == CT - 1 and n // CT >= 3:
                            bias(n // CT - 3)
                    for n in range(NTG - 3, OT * QC):
                        bias(n)
                    for n in range(NVH * KT):
                        act.wait_ge(v_biased, b * (NVH * KT) + n + 1)
                        act.dma_start(vD.rearrange("(b v o) p t d -> b v t p o d", b=B, v=NVH)[b, n // KT, n % KT],
                                      vout[:, n % 2].rearrange("p (o d) -> p o d", d=P)
                                      ).then_inc(v_stored[n % 2], 16)
                for i in range(2):
                    act.wait_ge(v_stored[i], B * NVH * KT // 2 * 16)

            @block.vector
            def _(dve):
                nc.vector.memset(epst[:], EPS).then_inc(eps_set, 1)
                dve.wait_ge(consts, 5 * 16)
                with dve.Fori(0, B) as b:
                    for g in range(NTG):
                        for ct in range(CT):
                            n = g * CT + ct
                            dve.wait_ge(transposed, b * (2 * NTP) + n + 1)
                            nc.vector.bn_stats(stats[:, ct, g], ps[n % 4][:, 0:TG]).then_inc(st_done, 1)
                    dve.wait_ge(st_done, (b + 1) * NTP)
                    nc.vector.memset(gate[:], 0.0)
                    for ct in range(CT):
                        ins = nc.vector.bn_aggr(mv[:, ct], stats[:, ct])
                    ins.then_inc(chain, 1)
                    dve.wait_ge(gsum_ready, b * 4 + 1)
                    nc.vector.tensor_scalar(gm[:], ps[4][0:GROUPS, 0:1], 1.0 / GC, None, ALU.mult).then_inc(gmean_set, 1)
                    dve.wait_ge(gsum_ready, b * 4 + 2)
                    nc.vector.tensor_copy(cm[:], ps[5][:, 0:CT]).then_inc(chain, 1)
                    dve.wait_ge(chain, b * 3 + 2)
                    nc.vector.tensor_tensor(dev[:], mv[:, :, 0], cm[:], ALU.subtract).then_inc(chain, 1)
                    dve.wait_ge(chain, b * 3 + 3)
                    for ct in range(CT):
                        ins = nc.vector.scalar_tensor_tensor(out=within[:, ct:ct + 1], in0=dev[:, ct:ct + 1],
                                                             scalar=dev[:, ct:ct + 1], in1=mv[:, ct, 1:2],
                                                             op0=ALU.mult, op1=ALU.add)
                    ins.then_inc(within_set, 1)
                    dve.wait_ge(gsum_ready, b * 4 + 3)
                    nc.vector.tensor_scalar(gv[:], ps[6][0:GROUPS, 0:1], 1.0 / GC, None, ALU.mult).then_inc(gvar_set, 1)
                    dve.wait_ge(gstd_set, b + 1)
                    nc.vector.reciprocal(gr[:], gs[:]).then_inc(grstd_set, 1)
                    dve.wait_ge(gsum_ready, b * 4 + 4)
                    nc.vector.scalar_tensor_tensor(out=cb[:], in0=ps[7][:, 0:CT], scalar=-1.0, in1=cm[:],
                                                   op0=ALU.mult, op1=ALU.mult)
                    nc.vector.tensor_copy(cr[:], ps[7][:, 0:CT]).then_inc(shift_set, 1)
                    def split_w(o):
                        dve.wait_ge(w_loaded[o % 2], (b * PAIRS + o // 2 + 1) * 16)
                        if o >= 2:
                            dve.wait_ge(qk_product, b * (OT * QC) + (o - 1) * QC)
                        nc.vector.tensor_copy(whl[:, o % 2, 0], wraw[:, o % 2]).then_inc(wh_set, 1)
                        dve.wait_ge(wh_set, b * OT + o + 1)
                        nc.vector.tensor_tensor(whl[:, o % 2, 1], wraw[:, o % 2], whl[:, o % 2, 0].bitcast(F32),
                                                ALU.subtract).then_inc(w_split, 1)

                    def split_qk(n):
                        o, c = n // QC, n % QC
                        s = SCALE if o < PAIRS else 1.0
                        dve.wait_ge(qk_biased, b * (OT * QC) + n + 1)
                        if c == 0:
                            dve.wait_ge(qk_stored, (b * OT + o) * 16)
                        src = row[:, n % 2, 0:QN[c]]
                        hi, lo = (hl[:, i, Q0[c]:Q0[c] + QN[c]] for i in range(2))
                        nc.vector.tensor_scalar(hi, src, s, None, ALU.mult).then_inc(qk_hi, 1)
                        dve.wait_ge(qk_hi, b * (OT * QC) + n + 1)
                        nc.vector.scalar_tensor_tensor(out=lo, in0=src, scalar=s, in1=hi.bitcast(F32),
                                                       op0=ALU.mult, op1=ALU.subtract).then_inc(qk_lo, 1)

                    split_w(0)
                    for n in range(NTP):
                        g, ct = n // CT, n % CT
                        dve.wait_ge(xn_written, b * NTP + n + 1)
                        if n == 0:
                            dve.wait_ge(v_product, b * (NVH * KT))
                        src = xn[:, n % 4].rearrange("p (h j w) -> p h j w", j=KG, w=KW)
                        hi, lo = (natural(t[:, ct])[:, g * (TG // W):(g + 1) * (TG // W)] for t in (xh, xl))
                        nc.vector.tensor_copy(hi, src).then_inc(xh_set, 1)
                        dve.wait_ge(xh_set, b * NTP + n + 1)
                        nc.vector.tensor_tensor(lo, src, hi.bitcast(F32), ALU.subtract).then_inc(xhl_written, 1)
                        if ct == CT - 1 and g >= 3:
                            split_qk(g - 3)

                    def split_v(vh, part):
                        raw = xtok[:, vh].rearrange("p a (c n) -> p (a c) n", n=TG)
                        dve.wait_ge(wv_loaded[vh], (b + 1) * 16)
                        if part == 0:
                            nc.vector.tensor_copy(wv[vh][:, 0], raw).then_inc(wvh_set, 1)
                            return
                        dve.wait_ge(wvh_set, b * NVH + vh + 1)
                        nc.vector.tensor_tensor(wv[vh][:, 1], raw, wv[vh][:, 0].bitcast(F32),
                                                ALU.subtract).then_inc(wv_split, 1)

                    for o in range(OT):
                        if o == OT - 1:
                            split_v(0, 0)
                            split_v(0, 1)
                        if o + 1 < OT:
                            split_w(o + 1)
                        for n in range(max(o * QC, NTG - 3), (o + 1) * QC):
                            split_qk(n)
                    for vh in range(NVH):
                        for t in range(KT):
                            n = vh * KT + t
                            dve.wait_ge(v_product, b * (NVH * KT) + n + 1)
                            dve.wait_ge(v_stored[n % 2], (b * (NVH * KT // 2) + n // 2) * 16)
                            nc.vector.tensor_tensor(vout[:, n % 2], ps[6 + n % 2][:, 0:TG],
                                                    vb[:, vh * TG:(vh + 1) * TG], ALU.add).then_inc(v_biased, 1)
                            if n == 3:
                                dve.wait_ge(qk_stored, (b + 1) * (OT * 16))
                                split_v(1, 0)
                            if n == 6:
                                split_v(1, 1)


RQ = 4
NU = H
NRP = NU // RQ


def relpos(nc, rev_h, rev_w, qF, relH, relW):
    with ExitStack() as ctx:
        def sb(name, shape, dt=F32):
            return ctx.enter_context(nc.sbuf_tensor("relpos_" + name, shape, dt))

        def sem(name):
            return ctx.enter_context(nc.semaphore("relpos_" + name))

        q = sb("q", [P, PAIRS, S])
        tab = sb("tab", [P, 2, NREL, 2])
        diff = sb("diff", [P, H, H, 2])
        w_hl = sb("w_split", [2 * W, 2, 2, PAIRS, S // 2], F32R)
        h_hl = sb("h_split", [2 * H, 2, 2, PAIRS, RQ * W], F32R)
        ps = [ctx.enter_context(nc.psum_tensor(f"relpos_ps{i}", [2 * H, 512], F32)) for i in range(8)]

        zeroed = sem("zeroed")
        tab_loaded = sem("tab_loaded")
        diff_set = sem("diff_set")
        q_loaded = [sem(f"q_loaded{j}") for j in range(KG)]
        product = sem("product")
        hi_set = sem("hi_set")
        lo_set = sem("lo_set")
        w_stored = [sem(f"w_stored{i}") for i in range(2)]
        h_stored = [sem(f"h_stored{i}") for i in range(2)]

        def size(u):
            return PAIRS * W if u < NU else PAIRS * H // 2

        UB = 3 * NU

        def kind_of(u):
            return (0, u, 0) if u < NU else (1, (u - NU) % NU, (u - NU) // NU)


        with nc.Block() as block:

            @block.gpsimd
            def _(pool):
                nc.gpsimd.memset(tab[:], 0.0).then_inc(zeroed, 1)
                nc.gpsimd.memset(diff[:], 0.0).then_inc(zeroed, 1)

            @block.sync
            def _(sp):
                def load_q(b):
                    for j in range(KG):
                        rows = slice(j * GK, (j + 1) * GK)
                        sp.dma_start(q[:, :, rows], qF.rearrange("(b o) p q -> b p o q", b=B)[b][:, :, rows]
                                     ).then_inc(q_loaded[j], 16)

                sp.wait_ge(zeroed, 1)
                for i, rev in enumerate((rev_h, rev_w)):
                    for s in range(2):
                        sp.dma_start(tab[s * D:(s + 1) * D, i, :, s:s + 1], rev.rearrange("c (r a) -> c r a", a=1),
                                     allow_slow_non_contiguous=True).then_inc(tab_loaded, 16)
                def store_w(b, half, part):
                    sp.dma_start(relW.rearrange("(b o) a r q -> b a r o q", b=B)[
                        b, part, :, :, half * (S // 2):(half + 1) * (S // 2)],
                                 w_hl[:, half, part].bitcast(F32)).then_inc(w_stored[half], 16)

                load_q(0)
                for b in range(B):
                    for g in range(NRP):
                        if b and 1 <= g < 3:
                            sp.wait_ge(lo_set, b * UB)
                            store_w(b - 1, 1, g - 1)
                        sp.wait_ge(lo_set, b * UB + (g + 1) * RQ)
                        for part in range(2):
                            sp.dma_start(relH.rearrange("(b o) a r q -> b a r o q", b=B)[b, part][:, :, g * RQ * W:(g + 1) * RQ * W],
                                         h_hl[:, g % 2, part].bitcast(F32)).then_inc(h_stored[g % 2], 16)
                    sp.wait_ge(lo_set, b * UB + 2 * NU)
                    for part in range(2):
                        store_w(b, 0, part)
                    if b + 1 < B:
                        sp.wait_ge(product, (b + 1) * UB)
                        load_q(b + 1)
                sp.wait_ge(lo_set, B * UB)
                for part in range(2):
                    store_w(B - 1, 1, part)
                for i in range(2):
                    sp.wait_ge(w_stored[i], B * 2 * 16)
                    sp.wait_ge(h_stored[i], B * NRP * 16)

            @block.tensor
            def _(pe):
                with pe.Fori(0, B) as b:
                    for u in range(UB):
                        kind, r, half = kind_of(u)
                        if u >= 8:
                            pe.wait_ge(lo_set, b * UB + u - 7)
                        else:
                            pe.wait_ge(lo_set, b * UB)
                        if kind == 0:
                            pe.wait_ge(diff_set, r + 1)
                            if r % (H // KG) == 0:
                                pe.wait_ge(q_loaded[r // (H // KG)], (b + 1) * 16)
                        if kind == 1:
                            cols = q[:].rearrange("p o (h w) -> p o h w", w=W)[:, :, half * (H // 2):(half + 1) * (H // 2), r]
                            win = tab[:, 1].rearrange("p r s -> p (r s)")[:, 2 * (W - 1 - r):2 * (W - 1 - r) + 2 * W]
                        else:
                            cols = q[:, :, r * W:(r + 1) * W]
                            win = diff[:, r].rearrange("p k s -> p (k s)")
                        nc.tensor.matmul(ps[u % 8][:, 0:size(u)], win, cols, start=True, stop=True).then_inc(product, 1)

            def part_of(u, part):
                kind, r, half = kind_of(u)
                if kind == 1:
                    return w_hl[:, half, part].rearrange("p o (h w) -> p o h w", w=W)[:, :, :, r]
                return h_hl[:, r // RQ % 2, part, :, r % RQ * W:(r % RQ + 1) * W]

            @block.scalar
            def _(act):
                with act.Fori(0, B) as b:
                    for u in range(UB):
                        act.wait_ge(product, b * UB + u + 1)
                        if u in (NU, 2 * NU):
                            act.wait_ge(w_stored[u // NU - 1], b * 2 * 16)
                        if u < NU and u % RQ == 0:
                            g = u // RQ
                            act.wait_ge(h_stored[g % 2], b * (NRP * 16) + g // 2 * 32)
                        nc.scalar.activation(part_of(u, 0), ps[u % 8][:, 0:size(u)].rearrange("p (o n) -> p o n", o=PAIRS),
                                             ACT.Copy).then_inc(hi_set, 1)

            @block.vector
            def _(dve):
                dve.wait_ge(tab_loaded, 4 * 16)
                dve.wait_ge(zeroed, 2)
                for r in range(H):
                    for s in range(2):
                        rows = slice(s * D, (s + 1) * D)
                        ins = nc.vector.tensor_scalar(diff[rows, r, :, s], tab[rows, 0, H - 1 - r:2 * H - 1 - r, s],
                                                      tab[rows, 0, 2 * H - 2 - r, s:s + 1], None, ALU.subtract)
                    ins.then_inc(diff_set, 1)
                with dve.Fori(0, B) as b:
                    for u in range(UB):
                        dve.wait_ge(hi_set, b * UB + u + 1)
                        nc.vector.tensor_tensor(part_of(u, 1), ps[u % 8][:, 0:size(u)].rearrange("p (o n) -> p o n", o=PAIRS),
                                                part_of(u, 0).bitcast(F32), ALU.subtract).then_inc(lo_set, 1)


AN = [464, 464, 464, 464, 448]
A0 = [sum(AN[:c]) for c in range(QC)]
AMAX = max(AN)
SLOTS = QC * KT
NPB = 4
NSB = 3
UNITS = 2 * KT * KG
UH = KT * KG
PIECES = 4
UP = UNITS // PIECES
AHEAD = SLOTS - 7


def units_of(m):
    return range(-(-m * UNITS // AHEAD), min(-(-(m + 1) * UNITS // AHEAD), UNITS))


def guests():
    slots = []
    for m in range(SLOTS):
        c, t = m // KT, m % KT
        units = [("unit", u) for u in units_of(m)]
        before, after = units[:1], units[1:]
        if c >= 1 and t == 2:
            after.append(("sum", c - 1))
        for s in range(2):
            if m >= 2 and (s + 1) * UH - 1 in units_of(m - 2):
                after.append(("turn", s))
        slots.append((before, after))
    order = [g for before, after in slots for g in before + after] + [("sum", QC - 1)]
    return slots, order


GUESTS, GUEST_ORDER = guests()
GUEST_AT = {g: i for i, g in enumerate(GUEST_ORDER)}
READS = 2 * KT * KG + 2


def guest_at(what, ahead):
    return GUEST_AT[what] if ahead else what[1]


def reads_until(at):
    return sum(1 for kind, _ in GUEST_ORDER[:at + 1] if kind != "sum")


KI = KT // KG
IG = KI // 3
QROWS = D + 2 * KW + 2 * KR + 1


def key_tile(t):
    return t % KG * KI + t // KG


def attend(nc, ident_d, hot_max_d, hot_d, qHL, kHL, vD, relH, relW, maxD, aD, sumD):
    with ExitStack() as ctx:
        def sb(name, shape, dt=F32):
            return ctx.enter_context(nc.sbuf_tensor("attend_" + name, shape, dt))

        def sem(name):
            return ctx.enter_context(nc.semaphore("attend_" + name))

        stage = sb("stage", [P, S])
        q0 = sb("q_block0", [P, 2, S], F32R)
        q1 = sb("q_block1", [QROWS, 2, KG, S], F32R)
        k0 = sb("k_block0", [P, 2, S], F32R)
        k1 = sb("k_block1", [QROWS, 2, S], F32R)
        v = sb("v", [P, KT, P])
        pe_ones = sb("ones", [P, D])
        prob = sb("prob", [P, NPB, 2, AMAX])
        acc = sb("prob_sum", [P, 2, 2, AMAX])
        o = sb("o", [P, 2, AMAX])
        total = sb("total", [P, 2, AMAX])
        qa = [sb(f"qa{i}", [P, KG, S // 2], F32R) for i in range(2)]
        ka = sb("ka", [P, 2, S], F32R)
        ident = sb("ident", [P, P])
        part_max = sb("part_max", [P, 2, KT, KG])
        mx = sb("max", [P, 2, KT])
        neg = sb("negated", [KT, 2, P], F32R)
        psS = [ctx.enter_context(nc.psum_tensor(f"attend_s{i}", [P, 512], F32)) for i in range(NSB)]
        psO = ctx.enter_context(nc.psum_tensor("attend_sum", [P, 512], F32))
        psG = [ctx.enter_context(nc.psum_tensor(f"attend_guest{i}", [P, 2, 512], F32)) for i in range(2)]

        hot_loaded = sem("hot_loaded")
        hot_set = sem("hot_set")
        ones_set = sem("ones_set")
        q_loaded = [sem(f"q_loaded{c}") for c in range(QC)]
        kv_loaded = [sem(f"kv_loaded{g}") for g in range(3)]
        rows_loaded = [sem(f"rows_loaded{j}") for j in range(KG)]
        max_loaded = [sem(f"max_loaded{i}") for i in range(2)]
        qa_loaded = [sem(f"qa_loaded{i}") for i in range(2)]
        ka_loaded = [sem(f"ka_loaded{s}") for s in range(2)]
        scores = sem("scores")
        exped = sem("exped")
        sum_copied = sem("sum_copied")
        weighed = sem("weighed")
        added = sem("added")
        unit_done = sem("unit_done")
        summed = sem("summed")
        turned = sem("turned")
        guest_read = sem("guest_read")
        max_set = sem("max_set")
        max_stored = [sem(f"max_stored{s}") for s in range(2)]
        o_copied = sem("o_copied")
        stored = [sem(f"stored{i}") for i in range(2)]

        QL, KL, QAL = 12, 7, 3 * KG
        HN = GK // 2
        LAST = NP - 1

        def head_rows(rel, n, a, s):
            return rel[n, a].rearrange("(k s) q -> k s q", s=2)[:, s]

        def both(d, n, part):
            return d[n, part].rearrange("(k s) q -> k s q", s=2)

        def load_rows(sp, n, c, i, j, part, done):
            cols = slice(A0[c], A0[c] + AN[c])
            at = D + 2 * KW + part * KR
            sp.dma_start(q1.bitcast(F32)[at:at + KR, :, j, cols], both(relH, n, part)[i * KR:(i + 1) * KR, :, cols]
                         ).then_inc(done, 16)

        def load_q(sp, n, c, step):
            cols = slice(A0[c], A0[c] + AN[c])
            n_cols = AN[c]
            s = step % 2

            def every_group(ap, rows):
                return ap.rearrange("p (a q) -> p a q", a=1).broadcast_to([rows, KG, n_cols])

            if step < 2:
                src = qHL[n].rearrange("(s p) i q -> p s i q", s=2)[:, :, 0, cols]
                dst = q0.bitcast(F32)[step * D:(step + 1) * D, :, cols]
            elif step < 4:
                src = every_group(qHL[n, s * D:(s + 1) * D, 1, cols], D)
                dst = q1.bitcast(F32)[0:D, s, :, cols]
            elif step < 8:
                part = step // 2 - 2
                at = D + part * KW
                src = relW[n, part].rearrange("(j k s) q -> k s j q", s=2, j=KG)[:, s, :, cols]
                dst = q1.bitcast(F32)[at:at + KW, s, :, cols]
            else:
                part = step // 2 - 4
                at = D + 2 * KW + part * KR
                src = every_group(both(relH, n, part)[0:KR, s, cols], KR)
                dst = q1.bitcast(F32)[at:at + KR, s, :, cols]
            sp.dma_start(dst, src).then_inc(q_loaded[c], 16)

        def load_max(sp, n, i, j):
            cols = slice(0, A0[QC - 1]) if i == 0 else slice(A0[QC - 1], S)
            sp.dma_start(q1.bitcast(F32)[QROWS - 1:QROWS, :, j, cols], maxD[n:n + 1, :, cols] if isinstance(n, int)
                         else maxD[n].rearrange("(a s) q -> a s q", a=1)[:, :, cols]).then_inc(max_loaded[i], 16)

        def load_kv(sp, n, g, step):
            def keys(ap):
                return ap.rearrange("p (j k) -> p j k", j=KG)[:, :, g * IG * P:(g + 1) * IG * P]

            if step < 6:
                s, what = step // 3, step % 3
                part, dst = ((0, k0[0:D]), (1, k0[D:P]), (0, k1[0:D]))[what]
                sp.dma_start(keys(dst.bitcast(F32)[:, s]), keys(kHL[n, s * D:(s + 1) * D, part])
                             ).then_inc(kv_loaded[g], 16)
            else:
                sp.dma_start(v[:].rearrange("p (j i) d -> p j i d", j=KG)[:, :, g * IG:(g + 1) * IG],
                             vD[n].rearrange("p (j i) d -> p j i d", j=KG)[:, :, g * IG:(g + 1) * IG]
                             ).then_inc(kv_loaded[g], 16)

        def load_qa(eng, n, p):
            s, cols = p // 2, slice(p % 2 * (S // 2), (p % 2 + 1) * (S // 2))
            d = qa[p % 2].bitcast(F32)
            for j in range(KG):
                for dst, src in ((d[D:D + H, j], head_rows(relH, n, 0, s)[:, cols]),
                                 (d[0:D, j], qHL[n, s * D:(s + 1) * D, 0, cols]),
                                 (d[D + H:P, j], head_rows(relW, n, 0, s)[j * KW:(j + 1) * KW, cols])):
                    eng.dma_start(dst, src).then_inc(qa_loaded[p % 2], 16)

        def load_ka(eng, n, s):
            eng.dma_start(ka.bitcast(F32)[0:D, s], kHL[n, s * D:(s + 1) * D, 0]).then_inc(ka_loaded[s], 16)

        def store_max(eng, n, s):
            eng.dma_start(maxD[n, s].rearrange("(t p) -> t p", p=P), neg[:, s].bitcast(F32)).then_inc(max_stored[s], 16)

        with nc.Block() as block:

            @block.sync
            def _(sp):
                sp.dma_start(prob[D:P].rearrange("p a b q -> p (a b q)")[:, 0:S], hot_max_d).then_inc(hot_loaded, 16)
                sp.dma_start(ident[:], ident_d).then_inc(hot_loaded, 16)
                sp.dma_start(stage[D:QROWS], hot_d).then_inc(hot_loaded, 16)
                sp.wait_ge(unit_done, 1)
                for step in range(KL):
                    load_kv(sp, 0, 0, step)
                for c in range(QC - 1):
                    for step in range(QL):
                        load_q(sp, 0, c, step)
                for s in range(2):
                    sp.wait_ge(max_stored[s], 16)
                for j in range(KG):
                    load_max(sp, 0, 0, j)

                def pair(n, more):
                    sp.wait_ge(weighed, n * SLOTS)
                    for m in range(SLOTS):
                        c, t = m // KT, m % KT
                        i, j = t // KG, t % KG
                        if c == 0 and t < 4:
                            for step in range(2 * t, min(2 * t + 2, KL)):
                                load_kv(sp, n, 1, step)
                        if t >= KT - KG and c not in (1, 2) and not (more and c == QC - 1):
                            continue
                        sp.wait_ge(scores, n * (2 * SLOTS) + 2 * m + 2)
                        if i + 1 < KI:
                            for part in range(2):
                                load_rows(sp, n, c, i + 1, j, part, rows_loaded[j])
                        if c == 0 and 4 <= t < 8:
                            for step in range(2 * (t - 4), min(2 * (t - 4) + 2, KL)):
                                load_kv(sp, n, 2, step)
                        if c == 3 and QL <= t < QL + KG:
                            load_max(sp, n, 1, t - QL)
                        if c in (1, 2) and t >= QL:
                            load_q(sp, n, QC - 1, (c - 1) * (KT - QL) + t - QL)
                        if more and c >= 1 and t < QL:
                            load_q(sp, n + 1, c - 1, t)
                        if more and c == QC - 1 and 10 <= t < 10 + KL:
                            if t == 10:
                                sp.wait_ge(weighed, n * SLOTS + (QC - 1) * KT + 2 * KG)
                            load_kv(sp, n + 1, 0, t - 10)
                        if more and c == QC - 1 and t >= KT - KG:
                            if t == KT - KG:
                                for s in range(2):
                                    sp.wait_ge(max_stored[s], (n + 2) * 16)
                            load_max(sp, n + 1, 0, t - (KT - KG))

                with sp.Fori(0, LAST) as n:
                    pair(n, True)
                pair(LAST, False)

            @block.gpsimd
            def _(pool):
                nc.gpsimd.memset(pe_ones[:], 1.0).then_inc(ones_set, 1)
                for s in range(2):
                    load_ka(pool, 0, s)
                    load_qa(pool, 0, s)
                for p in range(PIECES):
                    pool.wait_ge(unit_done, (p + 1) * UP)
                    if p % 2 == 1:
                        pool.wait_ge(guest_read, (p // 2 + 1) * (UH + 1))
                        store_max(pool, 0, p // 2)
                    load_qa(pool, *((0, p + 2) if p < 2 else (1, p - 2)))
                    if p % 2 == 1:
                        load_ka(pool, 1, p // 2)

                def store_out(n, c):
                    cols = slice(A0[c], A0[c] + AN[c])
                    pool.wait_ge(o_copied, n * QC + c + 1)
                    pool.wait_ge(sum_copied, n * QC + c + 1)
                    pool.dma_start(aD[n][:, cols], o[:, c % 2, 0:AN[c]]).then_inc(stored[c % 2], 16)
                    for s in range(2):
                        pool.dma_start(sumD[n, s:s + 1, cols], total[s * D:s * D + 1, c % 2, 0:AN[c]]
                                       ).then_inc(stored[c % 2], 16)

                def prepare(n, p, more):
                    pool.wait_ge(unit_done, (n + 1) * UNITS + (p + 1) * UP)
                    if p < 2:
                        load_qa(pool, n + 1, p + 2)
                    elif more:
                        load_qa(pool, n + 2, p - 2)
                    if p % 2 == 1:
                        if more:
                            load_ka(pool, n + 2, p // 2)
                        pool.wait_ge(guest_read, (n + 1) * READS + reads_until(GUEST_AT["turn", p // 2]))
                        store_max(pool, n + 1, p // 2)

                def pair(n, more):
                    prepare(n, 0, more)
                    store_out(n, 0)
                    store_out(n, 1)
                    prepare(n, 1, more)
                    store_out(n, 2)
                    prepare(n, 2, more)
                    store_out(n, 3)
                    prepare(n, 3, more)
                    store_out(n, 4)

                with pool.Fori(0, LAST - 1) as n:
                    pair(n, True)
                pair(LAST - 1, False)
                for c in range(QC):
                    store_out(LAST, c)
                pool.wait_ge(stored[0], NP * 3 * 48)
                pool.wait_ge(stored[1], NP * 2 * 48)
                for s in range(2):
                    pool.wait_ge(max_stored[s], NP * 16)

            @block.tensor
            def _(pe):

                def unit(n, u, g):
                    s, t, j = u // UH, u % UH // KG, u % KG
                    p = u // UP
                    if u % UP == 0:
                        pe.wait_ge(qa_loaded[p % 2], n * (2 * QAL * 16) + (p // 2 + 1) * (QAL * 16))
                    if u % UH == 0:
                        pe.wait_ge(ka_loaded[s], (n + 1) * 16)
                    tq = t % (KT // 2)
                    for i in range(2):
                        mm = nc.tensor.matmul(psG[g][:, i, 0:HN], qa[p % 2][:, j, tq * P:(tq + 1) * P],
                                              ka[:, s, j * GK + i * HN:j * GK + (i + 1) * HN], start=True, stop=True)
                    mm.then_inc(unit_done, 1)

                def turn(n, s, g):
                    pe.wait_ge(max_set, n * 2 + s + 1)
                    nc.tensor.transpose(psG[g][0:KT, 0, 0:P], mx[:, s], ident[:]).then_inc(turned, 1)

                def sum_probs(n, c, g):
                    pe.wait_ge(added, n * SLOTS + (c + 1) * KT)
                    for s in range(2):
                        mm = nc.tensor.matmul(psG[g][s * D:(s + 1) * D, 0, 0:AN[c]], pe_ones[:],
                                              acc[:, c % 2, s, 0:AN[c]], start=True, stop=True)
                    mm.then_inc(summed, 1)

                def guest(n, what, ahead):
                    kind, i = what
                    at = guest_at(what, ahead)
                    if at < 2:
                        pe.wait_ge(guest_read, (n + 1) * READS)
                        pe.wait_ge(sum_copied, n * QC)
                    elif not ahead:
                        pe.wait_ge(sum_copied, n * QC + at - 1)
                    elif GUEST_ORDER[at - 2][0] == "sum":
                        pe.wait_ge(sum_copied, n * QC + GUEST_ORDER[at - 2][1] + 1)
                    else:
                        pe.wait_ge(guest_read, (n + 1) * READS + reads_until(at - 2))
                    if kind == "unit":
                        unit(n + 1, i, at % 2)
                    elif kind == "turn":
                        turn(n + 1, i, at % 2)
                    else:
                        sum_probs(n, i, at % 2)

                def weigh(n, m):
                    c, t = m // KT, m % KT
                    pe.wait_ge(exped, n * (2 * SLOTS) + 2 * m + 2)
                    if t == 0:
                        pe.wait_ge(o_copied, n * QC + c)
                    for s in range(2):
                        mm = nc.tensor.matmul(psO[s * D:(s + 1) * D, 0:AN[c]], v[:, key_tile(t), s * D:(s + 1) * D],
                                              prob[:, m % NPB, s, 0:AN[c]], start=t == 0, stop=t == KT - 1)
                    mm.then_inc(weighed, 1)

                def pair(n, ahead):
                    for m in range(SLOTS):
                        c, t = m // KT, m % KT
                        before, after = ([g for g in gs if ahead or g[0] == "sum"] for gs in GUESTS[m])
                        for g in before:
                            guest(n, g, ahead)
                        if t == 0:
                            pe.wait_ge(q_loaded[c], (n + 1) * (QL * 16))
                            if c in (0, QC - 1):
                                pe.wait_ge(max_loaded[c // (QC - 1)], (n + 1) * (KG * 16))
                        if c == 0 and t % (KG * IG) == 0:
                            pe.wait_ge(kv_loaded[t // (KG * IG)], (n + 1) * (KL * 16))
                        i, j = t // KG, t % KG
                        if i >= 1:
                            pe.wait_ge(rows_loaded[j], (n * QC + c) * ((KI - 1) * 32) + i * 32)
                        cols = slice(A0[c], A0[c] + AN[c])
                        keys = slice(key_tile(t) * P, (key_tile(t) + 1) * P)
                        for s in range(2):
                            k = 2 * m + s
                            pe.wait_ge(exped, n * (2 * SLOTS) + max(k - NSB + 1, 0))
                            out = psS[k % NSB][:, 0:AN[c]]
                            nc.tensor.matmul(out, k0[:, s, keys], q0[:, s, cols], start=True, stop=False)
                            nc.tensor.matmul(out, k1[:, s, keys], q1[:, s, j, cols], start=False, stop=True
                                             ).then_inc(scores, 1)
                        for g in after:
                            guest(n, g, ahead)
                        if m >= 1:
                            weigh(n, m - 1)
                    weigh(n, SLOTS - 1)
                    guest(n, ("sum", QC - 1), ahead)

                pe.wait_ge(hot_set, 4)
                pe.wait_ge(ones_set, 1)
                for s in range(2):
                    for u in range(s * UH, (s + 1) * UH):
                        if u + s >= 2:
                            pe.wait_ge(guest_read, u + s - 1)
                        unit(0, u, (u + s) % 2)
                    pe.wait_ge(guest_read, (s + 1) * (UH + 1) - 2)
                    turn(0, s, ((s + 1) * (UH + 1) - 1) % 2)
                with pe.Fori(0, LAST) as n:
                    pair(n, True)
                pair(LAST, False)

            @block.scalar
            def _(act):

                def copy_out(n, c):
                    act.wait_ge(weighed, n * SLOTS + (c + 1) * KT)
                    act.wait_ge(stored[c % 2], n * ((3 - c % 2) * 48) + c // 2 * 48)
                    nc.scalar.activation(o[:, c % 2, 0:AN[c]], psO[:, 0:AN[c]], ACT.Copy).then_inc(o_copied, 1)

                def copy_sum(n, c, g):
                    act.wait_ge(summed, n * QC + c + 1)
                    nc.scalar.activation(total[:, c % 2, 0:AN[c]], psG[g][:, 0, 0:AN[c]], ACT.Copy).then_inc(sum_copied, 1)

                def pair(n, ahead):
                    for m in range(SLOTS):
                        c, t = m // KT, m % KT
                        for s in range(2):
                            act.wait_ge(scores, n * (2 * SLOTS) + 2 * m + s + 1)
                            if s == 0:
                                if m == 0:
                                    act.wait_ge(hot_set, 4)
                                act.wait_ge(weighed, n * SLOTS + max(m - NPB + 1, 0))
                                act.wait_ge(added, n * SLOTS + max(m - NPB + 1, 0))
                            nc.scalar.activation(prob[:, m % NPB, s, 0:AN[c]], psS[(2 * m + s) % NSB][:, 0:AN[c]],
                                                 ACT.Exp).then_inc(exped, 1)
                        if c >= 1 and t == 0:
                            copy_out(n, c - 1)
                        if c >= 1 and t == 2:
                            copy_sum(n, c - 1, guest_at(("sum", c - 1), ahead) % 2)
                    copy_out(n, QC - 1)
                    copy_sum(n, QC - 1, guest_at(("sum", QC - 1), ahead) % 2)

                with act.Fori(0, LAST) as n:
                    pair(n, True)
                pair(LAST, False)

            @block.vector
            def _(dve):

                def reduce_unit(n, u, g):
                    s, t, j = u // UH, u % UH // KG, u % KG
                    dve.wait_ge(unit_done, n * UNITS + u + 1)
                    nc.vector.tensor_reduce(part_max[:, s, t, j:j + 1], psG[g][:, :, 0:HN],
                                            mybir.AxisListType.XY, ALU.max).then_inc(guest_read, 1)

                def reduce_head(n, s, units_read):
                    dve.wait_ge(guest_read, units_read)
                    nc.vector.tensor_reduce(mx[:, s], part_max[:, s], AX_X, ALU.max).then_inc(max_set, 1)

                def negate(n, s, g):
                    dve.wait_ge(turned, n * 2 + s + 1)
                    dve.wait_ge(max_stored[s], n * 16)
                    nc.vector.tensor_scalar(neg[:, s], psG[g][0:KT, 0, 0:P], -1.0, None, ALU.mult).then_inc(guest_read, 1)

                def add(n, m):
                    c, t = m // KT, m % KT
                    if t == 0:
                        return
                    sums = acc[:, c % 2, :, 0:AN[c]]
                    dve.wait_ge(exped, n * (2 * SLOTS) + 2 * m + 2)
                    if t == 1:
                        dve.wait_ge(summed, n * QC + max(c - 1, 0))
                        nc.vector.tensor_tensor(sums, prob[:, (m - 1) % NPB, :, 0:AN[c]],
                                                prob[:, m % NPB, :, 0:AN[c]], ALU.add).then_inc(added, 2)
                    else:
                        dve.wait_ge(added, n * SLOTS + m)
                        nc.vector.tensor_tensor(sums, sums, prob[:, m % NPB, :, 0:AN[c]],
                                                ALU.add).then_inc(added, 1)

                def guest(n, what):
                    kind, i = what
                    g = GUEST_AT[what] % 2
                    if kind == "unit":
                        reduce_unit(n + 1, i, g)
                    elif kind == "turn":
                        negate(n + 1, i, g)

                def pair(n, ahead):
                    for m in range(SLOTS):
                        c, t = m // KT, m % KT
                        before, after = (gs if ahead else [] for gs in GUESTS[m])
                        for g in before:
                            guest(n, g)
                        if m >= 1:
                            add(n, m - 1)
                        for g in after:
                            guest(n, g)
                        for s in range(2):
                            if ahead and (s + 1) * UH - 1 in units_of(m):
                                reduce_head(n + 1, s, (n + 1) * READS
                                            + reads_until(GUEST_AT["unit", (s + 1) * UH - 1]))
                    add(n, SLOTS - 1)

                dve.wait_ge(hot_loaded, 3 * 16)
                for s in range(2):
                    nc.vector.tensor_copy(ka[D:P, s], prob[D:P].rearrange("p a b q -> p (a b q)")[:, 0:S]
                                          ).then_inc(hot_set, 1)
                for s in range(2):
                    nc.vector.tensor_copy(k1[D:QROWS, s], stage[D:QROWS]).then_inc(hot_set, 1)
                for s in range(2):
                    for u in range(s * UH, (s + 1) * UH):
                        reduce_unit(0, u, (u + s) % 2)
                    reduce_head(0, s, (s + 1) * (UH + 1) - 1)
                    negate(0, s, ((s + 1) * (UH + 1) - 1) % 2)
                with dve.Fori(0, LAST) as n:
                    pair(n, True)
                pair(LAST, False)


TR = 2
TT = TR * W
NTT = H // TR
FR = KWF * RI
CH = C // 2
TPU = 2
UT = TPU * TT
NUI = NTT // TPU
NRB = 4


def out_project(nc, x, proj_w, proj_b, row_dft_d, aD, sumD, invD, x1D, rowsD):
    with ExitStack() as ctx:
        def sb(name, shape, dt=F32):
            return ctx.enter_context(nc.sbuf_tensor("out_" + name, shape, dt))

        def sem(name):
            return ctx.enter_context(nc.semaphore("out_" + name))

        sums = sb("sums", [P, NP * 2 * S // P])
        inverse = sb("inverse", [P, NP * 2 * S // P])
        raw = sb("raw", [P, NRB, CT, UT])
        inv = sb("inv", [P, NRB, CT, UT])
        a = sb("attention", [P, NRB, 2, CT, UT], F32R)
        wraw = sb("w_raw", [P, 2, CT, CH])
        wp = sb("w_split", [P, 2, CT, C], F32R)
        pb = sb("bias", [TT, C])
        dft = sb("row_dft", [TT, TR * FR])
        xin = sb("x", [TT, 4, C])
        xb = sb("x_plus_bias", [TT, 2, C])
        x1 = sb("x1", [TT, 2, C])
        f = sb("spectrum", [TR * FR, 2, C])
        psA = [ctx.enter_context(nc.psum_tensor(f"out_a{i}", [TT, 2, 512], F32)) for i in range(2)]
        psF = [ctx.enter_context(nc.psum_tensor(f"out_f{i}", [TR * FR, 2, 512], F32)) for i in range(2)]

        consts = sem("consts")
        w_loaded = [sem(f"w_loaded{i}") for i in range(2)]
        w_hi = sem("w_hi")
        w_set = sem("w_set")
        sums_moved = sem("sums_moved")
        inverted = sem("inverted")
        a_loaded = [sem(f"a_loaded{i}") for i in range(NRB)]
        normalised = sem("normalised")
        a_hi = sem("a_hi")
        a_set = sem("a_set")
        x_loaded = [sem(f"x_loaded{i}") for i in range(4)]
        biased = sem("biased")
        projected = sem("projected")
        x1_set = sem("x1_set")
        transformed = sem("transformed")
        f_set = sem("f_set")
        x1_stored = [sem(f"x1_stored{i}") for i in range(2)]
        f_stored = [sem(f"f_stored{i}") for i in range(2)]

        x_view = x.rearrange("b (t p) c -> b t p c", p=TT)
        x1_view = x1D.rearrange("b (t p) c -> b t p c", p=TT)
        f_view = rowsD.rearrange("b (t h) k r c -> b t (h k r) c", h=TR)
        a_view = aD.rearrange("(b o) p q -> b p o q", b=B)
        inv_view = invD.rearrange("(b o) s q -> b s o q", b=B)

        def flat(d):
            return d.rearrange("n s q -> (n s q)").rearrange("(p f) -> p f", p=P)

        with nc.Block() as block:

            @block.sync
            def _(sp):
                sp.dma_start(sums[:], flat(sumD)).then_inc(sums_moved, 16)
                def load_w(i):
                    sp.dma_start(wraw[:, i], proj_w.rearrange("(t p) n -> p t n", p=P)[:, :, i * CH:(i + 1) * CH]
                                 ).then_inc(w_loaded[i], 16)

                load_w(0)
                sp.wait_ge(inverted, 1)
                sp.dma_start(flat(invD), inverse[:]).then_inc(sums_moved, 16)
                load_w(1)
                sp.dma_start(pb[:], proj_b.rearrange("(a c) -> a c", a=1).broadcast_to([TT, C])).then_inc(consts, 16)
                sp.dma_start(dft[:], row_dft_d).then_inc(consts, 16)
                sp.wait_ge(sums_moved, 32)
                for b in range(B):
                    for t in range(NTT):
                        n = b * NTT + t
                        if t % TPU == 0:
                            u = n // TPU
                            if u >= NRB:
                                sp.wait_ge(a_set, u - NRB + 1)
                            toks = slice(t * TT, t * TT + UT)
                            sp.dma_start(raw[:, u % NRB], a_view[b][:, :, toks]).then_inc(a_loaded[u % NRB], 16)
                            for s in range(2):
                                sp.dma_start(inv[s * D:(s + 1) * D, u % NRB],
                                             inv_view[b, s:s + 1, :, toks].broadcast_to([D, PAIRS, UT])
                                             ).then_inc(a_loaded[u % NRB], 16)
                        if n >= 4:
                            sp.wait_ge(biased, n - 3)
                        sp.dma_start(xin[:, n % 4], x_view[b, t]).then_inc(x_loaded[n % 4], 16)

            @block.gpsimd
            def _(pool):
                pool.wait_ge(consts, 32)
                with pool.Fori(0, B) as b:
                    for t in range(NTT):
                        pool.wait_ge(x_loaded[t % 4], b * (NTT // 4 * 16) + (t // 4 + 1) * 16)
                        pool.wait_ge(x1_set, b * NTT + max(t - 1, 0))
                        nc.gpsimd.tensor_tensor(xb[:, t % 2], xin[:, t % 4], pb[:], ALU.add).then_inc(biased, 1)

            @block.tensor
            def _(pe):
                pe.wait_ge(consts, 32)
                with pe.Fori(0, B) as b:

                    def transform(t):
                        pe.wait_ge(x1_set, b * NTT + t + 1)
                        pe.wait_ge(f_set, b * NTT + max(t - 1, 0))
                        for i in range(2):
                            mm = nc.tensor.matmul(psF[t % 2][:, i, 0:CH], dft[:], x1[:, t % 2, i * CH:(i + 1) * CH],
                                                  start=True, stop=True)
                        mm.then_inc(transformed, 1)

                    for t in range(NTT):
                        u, v = t // TPU, t % TPU
                        if v == 0:
                            pe.wait_ge(a_set, b * NUI + u + 1)
                        pe.wait_ge(x1_set, b * NTT + max(t - 1, 0))
                        for i in range(2):
                            if t == 0:
                                pe.wait_ge(w_set, i + 1)
                            k = 0
                            for ap, wq in ((0, 0), (0, 1), (1, 0)):
                                for ct in range(CT):
                                    mm = nc.tensor.matmul(psA[t % 2][:, i, 0:CH], a[:, u % NRB, ap, ct, v * TT:(v + 1) * TT],
                                                          wp[:, wq, ct, i * CH:(i + 1) * CH],
                                                          start=k == 0, stop=k == 3 * CT - 1)
                                    k += 1
                        mm.then_inc(projected, 1)
                        if t >= 1:
                            transform(t - 1)
                    transform(NTT - 1)

            @block.vector
            def _(dve):
                dve.wait_ge(sums_moved, 16)
                nc.vector.reciprocal(inverse[:], sums[:]).then_inc(inverted, 1)
                for i in range(2):
                    dve.wait_ge(w_loaded[i], 16)
                    cols = slice(i * CH, (i + 1) * CH)
                    nc.vector.tensor_copy(wp[:, 0, :, cols], wraw[:, i]).then_inc(w_hi, 1)
                    dve.wait_ge(w_hi, i + 1)
                    nc.vector.tensor_tensor(wp[:, 1, :, cols], wraw[:, i], wp[:, 0, :, cols].bitcast(F32),
                                            ALU.subtract).then_inc(w_set, 1)
                with dve.Fori(0, B) as b:

                    def normalise(u):
                        dve.wait_ge(a_loaded[u % NRB], b * (NUI // NRB * 48) + (u // NRB + 1) * 48)
                        nc.vector.tensor_tensor(raw[:, u % NRB], raw[:, u % NRB], inv[:, u % NRB], ALU.mult
                                                ).then_inc(normalised, 1)

                    def split(u):
                        dve.wait_ge(a_hi, b * NUI + u + 1)
                        nc.vector.tensor_tensor(a[:, u % NRB, 1], raw[:, u % NRB], a[:, u % NRB, 0].bitcast(F32),
                                                ALU.subtract).then_inc(a_set, 1)

                    for u in range(2):
                        normalise(u)
                        split(u)
                    for t in range(NTT):
                        if t % TPU == 0 and t // TPU + 2 < NUI:
                            normalise(t // TPU + 2)
                        if t % TPU == 1 and t // TPU + 2 < NUI:
                            split(t // TPU + 2)
                        dve.wait_ge(projected, b * NTT + t + 1)
                        dve.wait_ge(biased, b * NTT + t + 1)
                        dve.wait_ge(x1_stored[t % 2], b * (NTT // 2 * 16) + t // 2 * 16)
                        dve.wait_ge(transformed, b * NTT + max(t - 1, 0))
                        nc.vector.tensor_tensor(x1[:, t % 2].rearrange("p (i c) -> p i c", i=2),
                                                psA[t % 2][:, :, 0:CH],
                                                xb[:, t % 2].rearrange("p (i c) -> p i c", i=2),
                                                ALU.add).then_inc(x1_set, 1)

            @block.scalar
            def _(act):
                with act.Fori(0, B) as b:

                    def round_to_hi(u):
                        act.wait_ge(normalised, b * NUI + u + 1)
                        act.wait_ge(projected, b * NTT + max(u - NRB + 1, 0) * TPU)
                        nc.scalar.activation(a[:, u % NRB, 0], raw[:, u % NRB], ACT.Copy).then_inc(a_hi, 1)

                    for u in range(2):
                        round_to_hi(u)
                    for t in range(NTT):
                        if t % TPU == 0 and t // TPU + 2 < NUI:
                            round_to_hi(t // TPU + 2)
                        act.wait_ge(x1_set, b * NTT + t + 1)
                        act.dma_start(x1_view[b, t], x1[:, t % 2]).then_inc(x1_stored[t % 2], 16)
                        act.wait_ge(transformed, b * NTT + t + 1)
                        act.wait_ge(f_stored[t % 2], b * (NTT // 2 * 16) + t // 2 * 16)
                        nc.scalar.activation(f[:, t % 2].rearrange("p (i c) -> p i c", i=2), psF[t % 2][:, :, 0:CH],
                                             ACT.Copy).then_inc(f_set, 1)
                        act.wait_ge(f_set, b * NTT + t + 1)
                        act.dma_start(f_view[b, t], f[:, t % 2]).then_inc(f_stored[t % 2], 16)
                for i in range(2):
                    act.wait_ge(x1_stored[i], B * NTT // 2 * 16)
                    act.wait_ge(f_stored[i], B * NTT // 2 * 16)


NG = (KWF + 1) // 2
NF = KWF * H
NQ = 3
FQ = NF // NQ
GB = BS // GC
BH = NB // 2


RANGES = ((0, 0, 2, 2), (1, 10, 12, 2), (11, 19, 20, 2), (20, KWF - 2, KWF - 1, NB), (KWF - 1, KWF - 1, KWF - 1, NB))


def spectrum(nc, w1_d, b1_d, w2_d, b2_d, col_dft_d, icol_dft_d, indb_d, indbT_d, rowsD, specD):
    with ExitStack() as ctx:
        def sb(name, shape, dt=F32):
            return ctx.enter_context(nc.sbuf_tensor("spec_" + name, shape, dt))

        def sem(name):
            return ctx.enter_context(nc.semaphore("spec_" + name))

        col = sb("col_dft", [RI * H, RI * H])
        icol = sb("icol_dft", [2 * H, 3, 2 * H])
        w1 = sb("w1", [BS, NB, 3, BS])
        w1s = sb("w1_scaled", [BS, NB, 3, BS])
        w2 = sb("w2", [BS, NB, 2, 2, BS])
        b1 = sb("b1", [BS, NB, RI])
        b2 = sb("b2", [2 * H, NB, RI, BS])
        indb = sb("indb", [BS, GB])
        indbT = sb("indbT", [GB, BS])
        rows = sb("rows", [RI * H, 3, C])
        xf = sb("xf", [BS, NB, RI, KWF, H])
        dc = sb("dc", [BS, NB])
        dcm = sb("dc_centred", [BS, NB])
        energy = sb("energy", [BS, len(RANGES), NB])
        inner = sb("inner_energy", [BS, NB])
        power = sb("power", [BS, NB])
        total = sb("total", [BS, NB])
        gsum = sb("group_sum", [GB, NB])
        gvar = sb("group_var", [GB, NB])
        gstd = sb("group_std", [GB, NB])
        grstd = sb("group_rstd", [GB, NB])
        rstd = sb("rstd", [BS, NB])
        epst = sb("eps", [GB, 1])
        hid = sb("hidden", [BS, 2, RI, NF])
        pre = sb("pre", [2 * H, 2, 2, RI, BS])
        clamped = sb("clamped", [2 * H, 2, 2, RI, BS])
        y = sb("y", [2 * H, NG, RI, CH])
        g = sb("g", [2 * H, 2, RI, CH])
        ps = [ctx.enter_context(nc.psum_tensor(f"spec_ps{i}", [P, 512], F32)) for i in range(8)]

        col_loaded = sem("col_loaded")
        consts = sem("consts")
        ready = sem("ready")
        rows_loaded = [sem(f"rows_loaded{i}") for i in range(3)]
        column = sem("column")
        col_lo = sem("col_lo")
        col_hi = sem("col_hi")
        dc_set = sem("dc_set")
        dc_zero = sem("dc_zero")
        squared = sem("squared")
        group_pe = sem("group_pe")
        gsum_set = sem("gsum_set")
        dcm_set = sem("dcm_set")
        power_set = sem("power_set")
        sq_set = sem("sq_set")
        total_set = sem("total_set")
        gvar_set = sem("gvar_set")
        gstd_set = sem("gstd_set")
        grstd_set = sem("grstd_set")
        rstd_set = sem("rstd_set")
        normed = sem("normed")
        layer1 = sem("layer1")
        gelued = sem("gelued")
        layer2 = sem("layer2")
        pre_set = sem("pre_set")
        clamp_set = sem("clamp_set")
        y_set = sem("y_set")
        inv_re = sem("inv_re")
        inv_im = sem("inv_im")
        g_re = sem("g_re")
        g_im = sem("g_im")
        g_stored = [sem(f"g_stored{i}") for i in range(2)]

        U1 = NB * NQ * RI
        G2 = (NG + 1) // 2
        U2 = NB * G2
        U3 = 2 * NG

        spec_view = specD.rearrange("b h k r c -> b k h r c")

        def kws(i):
            return min(2, KWF - 2 * i)

        def stores_before(b, u):
            return b * KWF + sum(kws(v % NG) for v in range(u) if v % 2 == u % 2)

        with nc.Block() as block:

            @block.sync
            def _(sp):

                def load_rows(n):
                    for r in range(RI):
                        sp.dma_start(rows[r * H:(r + 1) * H, n % 3], rowsD[n // KWF, :, n % KWF, r]
                                     ).then_inc(rows_loaded[n % 3], 16)

                sp.dma_start(col[:], col_dft_d).then_inc(col_loaded, 16)
                for n in range(3):
                    load_rows(n)
                others = ((icol[:], icol_dft_d), (indb[:], indb_d), (indbT[:], indbT_d),
                           (b1[:], b1_d),
                           (b2[:].rearrange("p n r c -> p (n r c)"),
                            b2_d.rearrange("(a c) -> a c", a=1).broadcast_to([2 * H, NB * RI * BS])),
                           (w1[:, :, 0], w1_d[0].rearrange("n i o -> i n o")),
                           (w1[:, :, 1], w1_d[1].rearrange("n i o -> i n o")),
                           (w2[:, :, 0, 0], w2_d[0].rearrange("n i o -> i n o")),
                           (w2[:, :, 0, 1], w2_d[1].rearrange("n i o -> i n o")),
                           (w2[:, :, 1, 1], w2_d[0].rearrange("n i o -> i n o")))
                for n in range(3, B * KWF):
                    sp.wait_ge(column, n - 2)
                    load_rows(n)
                    if n - 3 < len(others):
                        dst, src = others[n - 3]
                        sp.dma_start(dst, src).then_inc(consts, 16)

            @block.gpsimd
            def _(pool):
                with pool.Fori(0, B) as b:
                    for u in range(U3):
                        half, i = u // NG, u % NG
                        m = kws(i)
                        pool.wait_ge(g_re, b * U3 + u + 1)
                        pool.wait_ge(g_im, b * U3 + u + 1)
                        for k in range(m):
                            pool.dma_start(spec_view[b, 2 * i + k][:, :, half * CH:(half + 1) * CH],
                                           g[k * H:(k + 1) * H, u % 2]).then_inc(g_stored[u % 2], 16)
                for i in range(2):
                    pool.wait_ge(g_stored[i], B * 2 * KWF // 2 * 16)

            @block.tensor
            def _(pe):
                pe.wait_ge(col_loaded, 16)
                for b in range(B):
                    for k in range(KWF):
                        n = b * KWF + k
                        pe.wait_ge(rows_loaded[n % 3], (n // 3 + 1) * 32)
                        if n >= 2:
                            pe.wait_ge(col_lo, n - 1)
                            pe.wait_ge(col_hi, n - 1)
                        if k < 2:
                            pe.wait_ge(gelued, b * U1)
                        for blk in range(NB):
                            bank = ps[2 * (n % 2) + blk // BH]
                            mm = nc.tensor.matmul(bank[0:BS, blk % BH * (RI * H):(blk % BH + 1) * (RI * H)],
                                                  rows[:, n % 3, blk * BS:(blk + 1) * BS], col[:],
                                                  start=True, stop=True)
                        mm.then_inc(column, 1)
                    if b == 0:
                        pe.wait_ge(consts, 10 * 16)
                        pe.wait_ge(ready, 3)
                    pe.wait_ge(dc_set, b + 1)
                    pe.wait_ge(pre_set, b * U2)
                    nc.tensor.matmul(ps[4][0:GB, 0:NB], indb[:], dc[:], start=True, stop=True).then_inc(group_pe, 1)
                    pe.wait_ge(gsum_set, b + 1)
                    nc.tensor.matmul(ps[5][0:BS, 0:NB], indbT[:], gsum[:], start=True, stop=True).then_inc(group_pe, 1)
                    pe.wait_ge(total_set, b + 1)
                    pe.wait_ge(g_re, b * U3)
                    nc.tensor.matmul(ps[6][0:GB, 0:NB], indb[:], total[:], start=True, stop=True).then_inc(group_pe, 1)
                    pe.wait_ge(grstd_set, b + 1)
                    pe.wait_ge(g_im, b * U3)
                    nc.tensor.matmul(ps[7][0:BS, 0:NB], indbT[:], grstd[:], start=True, stop=True).then_inc(group_pe, 1)
                    pe.wait_ge(normed, b + 1)

                    def first(blk):
                        for q in range(NQ):
                            for r in range(RI):
                                u = (blk * NQ + q) * RI + r
                                if u >= 4:
                                    pe.wait_ge(gelued, b * U1 + u - 3)
                                elif u == 0:
                                    pe.wait_ge(col_lo, (b + 1) * KWF)
                                    pe.wait_ge(col_hi, (b + 1) * KWF)
                                xs = [xf[:, blk, i].rearrange("p k h -> p (k h)")[:, q * FQ:(q + 1) * FQ] for i in range(RI)]
                                nc.tensor.matmul(ps[u % 4][0:BS, 0:FQ], w1s[:, blk, 0], xs[r], start=True, stop=False)
                                nc.tensor.matmul(ps[u % 4][0:BS, 0:FQ], w1s[:, blk, 2 - r], xs[1 - r],
                                                 start=False, stop=True).then_inc(layer1, 1)

                    def second(blk):
                        pe.wait_ge(gelued, b * U1 + (blk + 1) * (NQ * RI))
                        for i in range(NG):
                            u = blk * G2 + i // 2
                            if i % 2 == 0 and u >= 2:
                                pe.wait_ge(pre_set, b * U2 + u - 1)
                            m = kws(i) * H
                            out = ps[4 + u % 2][0:m, i % 2 * (RI * BS):(i % 2 + 1) * (RI * BS)]
                            for r in range(RI):
                                mm = nc.tensor.matmul(out, hid[:, blk % 2, r, 2 * i * H:2 * i * H + m],
                                                      w2[:, blk, r].rearrange("p a o -> p (a o)"),
                                                      start=r == 0, stop=r == RI - 1)
                            if i % 2 or i == NG - 1:
                                mm.then_inc(layer2, 1)

                    def inverse(half):
                        for i in range(NG):
                            u = half * NG + i
                            m = kws(i) * H
                            if i % 2 == 0:
                                pe.wait_ge(y_set, b * U2 + (half * BH + BH - 1) * G2 + i // 2 + 1)
                            for r, bank, done, read in ((0, ps[6], inv_re, g_re), (1, ps[7], inv_im, g_im)):
                                pe.wait_ge(read, b * U3 + u)
                                nc.tensor.matmul(bank[0:m, 0:CH], icol[0:m, 0, 0:m], y[0:m, i, r], start=True, stop=False)
                                nc.tensor.matmul(bank[0:m, 0:CH], icol[0:m, 2 - r, 0:m], y[0:m, i, 1 - r],
                                                 start=False, stop=True).then_inc(done, 1)

                    first(0)
                    for blk in range(1, NB):
                        first(blk)
                        second(blk - 1)
                        if blk == BH:
                            inverse(0)
                    second(NB - 1)
                    inverse(1)

            @block.scalar
            def _(act):

                def add_energy(b, i, k):
                    first_k, last_k, due, per_k = RANGES[i]
                    if k == due:
                        act.wait_ge(col_lo, b * KWF + last_k + 1)
                        act.wait_ge(col_hi, b * KWF + last_k + 1)
                        act.wait_ge(layer2, b * U2)
                        if first_k == 0:
                            act.wait_ge(dc_zero, b + 1)
                    size = RI * (last_k - first_k + 1) * H
                    for blk in range((k - due) * per_k, (k - due + 1) * per_k):
                        junk = hid[:, blk % 2].rearrange("p r f -> p (r f)")[:, 0:size].rearrange(
                            "p (r k h) -> p r k h", r=RI, h=H)
                        done = (b * len(RANGES) + i) * NB + blk
                        if done >= 2:
                            act.wait_ge(squared, done - 1)
                        nc.scalar.activation(junk, xf[:, blk, :, first_k:last_k + 1], ACT.Square,
                                             accum_out=energy[:, i, blk:blk + 1]).then_inc(squared, 1)

                for b in range(B):
                    for k in range(KWF):
                        n = b * KWF + k
                        act.wait_ge(column, n + 1)
                        if k == 0:
                            act.wait_ge(layer1, b * U1)
                        nc.scalar.activation(xf[:, 0:BH, :, k],
                                             ps[2 * (n % 2)][0:BS, 0:CH].rearrange("p (n r h) -> p n r h", r=RI, h=H),
                                             ACT.Copy).then_inc(col_lo, 1)
                        for i, (_, _, due, per_k) in enumerate(RANGES):
                            if due <= k < due + NB // per_k:
                                add_energy(b, i, k)
                    if b == 0:
                        act.wait_ge(consts, 10 * 16)
                        act.wait_ge(ready, 3)
                    act.wait_ge(gvar_set, b + 1)
                    nc.scalar.activation(gstd[:], gvar[:], ACT.Sqrt, bias=epst[:]).then_inc(gstd_set, 1)

                    def gelu(blk):
                        for q in range(NQ):
                            for r in range(RI):
                                u = (blk * NQ + q) * RI + r
                                act.wait_ge(layer1, b * U1 + u + 1)
                                if q == 0 and r == 0 and blk >= 2:
                                    act.wait_ge(layer2, b * U2 + (blk - 1) * G2)
                                nc.scalar.activation(hid[:, blk % 2, r, q * FQ:(q + 1) * FQ], ps[u % 4][0:BS, 0:FQ],
                                                     ACT.Gelu, bias=b1[:, blk, r:r + 1]).then_inc(gelued, 1)

                    def evacuate(half):
                        for i in range(NG):
                            u = half * NG + i
                            m = kws(i) * H
                            act.wait_ge(inv_re, b * U3 + u + 1)
                            act.wait_ge(g_stored[u % 2], stores_before(b, u) * 16)
                            nc.scalar.activation(g[0:m, u % 2, 0], ps[6][0:m, 0:CH], ACT.Copy).then_inc(g_re, 1)

                    for blk in range(NB):
                        gelu(blk)
                        if blk == BH:
                            evacuate(0)
                    evacuate(1)

            @block.vector
            def _(dve):
                nc.vector.memset(epst[:], EPS).then_inc(ready, 1)
                for b in range(B):
                    for k in range(KWF):
                        n = b * KWF + k
                        dve.wait_ge(column, n + 1)
                        if k == 0:
                            dve.wait_ge(layer1, b * U1)
                        nc.vector.tensor_copy(xf[:, BH:NB, :, k],
                                              ps[2 * (n % 2) + 1][0:BS, 0:CH].rearrange("p (n r h) -> p n r h", r=RI, h=H)
                                              ).then_inc(col_hi, 1)
                        if k == 0:
                            dve.wait_ge(col_lo, b * KWF + 1)
                            dve.wait_ge(col_hi, b * KWF + 1)
                            nc.vector.tensor_copy(dc[:], xf[:, :, 0, 0, 0]).then_inc(dc_set, 1)
                            dve.wait_ge(dc_set, b + 1)
                            nc.vector.memset(xf[:, :, 0, 0, 0:1], 0.0).then_inc(dc_zero, 1)
                    if b == 0:
                        dve.wait_ge(consts, 10 * 16)
                        nc.vector.tensor_scalar(w1[:, :, 2], w1[:, :, 1], -1.0, None, ALU.mult).then_inc(ready, 1)
                        nc.vector.tensor_scalar(w2[:, :, 1, 0], w2[:, :, 0, 1], -1.0, None, ALU.mult).then_inc(ready, 1)
                        dve.wait_ge(ready, 3)
                    dve.wait_ge(group_pe, 4 * b + 1)
                    nc.vector.tensor_scalar(gsum[:], ps[4][0:GB, 0:NB], 1.0 / GC, None, ALU.mult).then_inc(gsum_set, 1)
                    dve.wait_ge(group_pe, 4 * b + 2)
                    nc.vector.tensor_tensor(dcm[:], dc[:], ps[5][0:BS, 0:NB], ALU.subtract).then_inc(dcm_set, 1)
                    dve.wait_ge(squared, (b + 1) * (len(RANGES) * NB))
                    nc.vector.tensor_tensor(inner[:], energy[:, 1], energy[:, 2], ALU.add).then_inc(power_set, 1)
                    dve.wait_ge(power_set, 4 * b + 1)
                    nc.vector.tensor_tensor(inner[:], inner[:], energy[:, 3], ALU.add).then_inc(power_set, 1)
                    dve.wait_ge(power_set, 4 * b + 2)
                    nc.vector.scalar_tensor_tensor(out=inner[:], in0=inner[:], scalar=2.0, in1=energy[:, 0],
                                                   op0=ALU.mult, op1=ALU.add).then_inc(power_set, 1)
                    dve.wait_ge(power_set, 4 * b + 3)
                    nc.vector.tensor_tensor(power[:], inner[:], energy[:, 4], ALU.add).then_inc(power_set, 1)
                    dve.wait_ge(dcm_set, b + 1)
                    nc.vector.tensor_tensor(total[:], dcm[:], dcm[:], ALU.mult).then_inc(sq_set, 1)
                    dve.wait_ge(power_set, 4 * b + 4)
                    dve.wait_ge(sq_set, b + 1)
                    nc.vector.tensor_tensor(total[:], total[:], power[:], ALU.add).then_inc(total_set, 1)
                    dve.wait_ge(group_pe, 4 * b + 3)
                    nc.vector.tensor_scalar(gvar[:], ps[6][0:GB, 0:NB], 1.0 / (GC * S), None, ALU.mult).then_inc(gvar_set, 1)
                    dve.wait_ge(gstd_set, b + 1)
                    nc.vector.reciprocal(grstd[:], gstd[:]).then_inc(grstd_set, 1)
                    dve.wait_ge(group_pe, 4 * b + 4)
                    nc.vector.tensor_copy(rstd[:], ps[7][0:BS, 0:NB]).then_inc(rstd_set, 1)
                    dve.wait_ge(rstd_set, b + 1)
                    nc.vector.tensor_copy(xf[:, :, 0, 0, 0], dcm[:])
                    for blk in range(NB):
                        ins = nc.vector.tensor_scalar(w1s[:, blk], w1[:, blk], rstd[:, blk:blk + 1], None, ALU.mult)
                    ins.then_inc(normed, 1)

                    def shrink(blk):
                        for j in range(G2):
                            u = blk * G2 + j
                            w = min(2, NG - 2 * j)
                            m = kws(2 * j) * H
                            bank = ps[4 + u % 2][0:m, 0:w * RI * BS].rearrange("p (i r c) -> p i r c", r=RI, c=BS)
                            bias = b2[0:m, blk].rearrange("p (a r) c -> p a r c", a=1).broadcast_to([m, w, RI, BS])
                            dve.wait_ge(layer2, b * U2 + u + 1)
                            nc.vector.tensor_tensor(pre[0:m, u % 2, 0:w], bank, bias, ALU.add).then_inc(pre_set, 1)
                            dve.wait_ge(pre_set, b * U2 + u + 1)
                            nc.vector.tensor_scalar(clamped[0:m, u % 2, 0:w], pre[0:m, u % 2, 0:w], -SPARSITY, SPARSITY,
                                                    ALU.max, ALU.min).then_inc(clamp_set, 1)
                            dve.wait_ge(clamp_set, b * U2 + u + 1)
                            if blk % BH == 0:
                                dve.wait_ge(inv_im, b * U3 + (blk // BH) * NG)
                            nc.vector.tensor_tensor(y[0:m, 2 * j:2 * j + w, :, blk % BH * BS:(blk % BH + 1) * BS],
                                                    pre[0:m, u % 2, 0:w], clamped[0:m, u % 2, 0:w],
                                                    ALU.subtract).then_inc(y_set, 1)

                    def evacuate(half):
                        for i in range(NG):
                            u = half * NG + i
                            m = kws(i) * H
                            dve.wait_ge(inv_im, b * U3 + u + 1)
                            dve.wait_ge(g_stored[u % 2], stores_before(b, u) * 16)
                            nc.vector.tensor_copy(g[0:m, u % 2, 1], ps[7][0:m, 0:CH]).then_inc(g_im, 1)

                    for blk in range(NB):
                        shrink(blk)
                        if blk % BH == BH - 1:
                            evacuate(blk // BH)


def image(nc, irow_dft_d, x1D, specD, out):
    with ExitStack() as ctx:
        def sb(name, shape, dt=F32):
            return ctx.enter_context(nc.sbuf_tensor("image_" + name, shape, dt))

        def sem(name):
            return ctx.enter_context(nc.semaphore("image_" + name))

        NBUF = 4
        dft = sb("irow_dft", [TR * FR, TT])
        f = sb("spectrum", [TR * FR, NBUF, C])
        x1 = sb("x1", [TT, NBUF, C])
        o = sb("o", [TT, NBUF, C])
        ps = [ctx.enter_context(nc.psum_tensor(f"image_ps{i}", [TT, 2, 512], F32)) for i in range(4)]
        consts = sem("consts")
        loaded = [sem(f"loaded{i}") for i in range(NBUF)]
        transformed = sem("transformed")
        o_set = sem("o_set")
        stored = [sem(f"stored{i}") for i in range(NBUF)]

        f_view = specD.rearrange("b (t h) k r c -> (b t) (h k r) c", h=TR)
        x_view = x1D.rearrange("b (t p) c -> (b t) p c", p=TT)
        o_view = out.rearrange("b (t p) c -> (b t) p c", p=TT)
        NS = B * NTT // NBUF

        with nc.Block() as block:

            @block.sync
            def _(sp):
                sp.dma_start(dft[:], irow_dft_d).then_inc(consts, 16)
                def load(g, i):
                    sp.dma_start(f[:, i], f_view[g * NBUF + i]).then_inc(loaded[i], 16)
                    sp.dma_start(x1[:, i], x_view[g * NBUF + i]).then_inc(loaded[i], 16)

                for i in range(NBUF):
                    load(0, i)
                with sp.Fori(0, NS - 1) as g:
                    for i in range(NBUF):
                        sp.wait_ge(o_set, g * NBUF + i + 1)
                        load(g + 1, i)

            @block.tensor
            def _(pe):
                pe.wait_ge(consts, 16)
                def transform(g, i):
                    pe.wait_ge(loaded[i], g * 32 + 32)
                    for h in range(2):
                        mm = nc.tensor.matmul(ps[i][:, h, 0:CH], dft[:], f[:, i, h * CH:(h + 1) * CH],
                                              start=True, stop=True)
                    mm.then_inc(transformed, 1)

                for i in range(NBUF):
                    transform(0, i)
                with pe.Fori(0, NS - 1) as g:
                    for i in range(NBUF):
                        pe.wait_ge(o_set, g * NBUF + i + 1)
                        transform(g + 1, i)

            @block.vector
            def _(dve):
                with dve.Fori(0, NS) as g:
                    for i in range(NBUF):
                        dve.wait_ge(transformed, g * NBUF + i + 1)
                        dve.wait_ge(stored[i], g * 16)
                        nc.vector.tensor_tensor(o[:, i].rearrange("p (h c) -> p h c", h=2), ps[i][:, :, 0:CH],
                                                x1[:, i].rearrange("p (h c) -> p h c", h=2), ALU.add).then_inc(o_set, 1)

            @block.scalar
            def _(act):
                with act.Fori(0, NS) as g:
                    for i in range(NBUF):
                        act.wait_ge(o_set, g * NBUF + i + 1)
                        act.dma_start(o_view[g * NBUF + i], o[:, i]).then_inc(stored[i], 16)
                for i in range(NBUF):
                    act.wait_ge(stored[i], NS * 16)


def tables():
    def cs(n, m, size):
        k = np.outer(np.arange(n), np.arange(m)) % size
        c, s = np.cos(2 * np.pi * k / size), np.sin(2 * np.pi * k / size)
        s[(2 * k) % size == 0] = 0
        return c, s

    f32 = np.float32
    t = {"ident": np.eye(P, dtype=f32)}
    gi = (np.arange(C)[:, None] // GC == np.arange(GROUPS)).astype(f32)
    t["ind"] = np.ascontiguousarray(gi.reshape(CT, P, GROUPS).transpose(1, 0, 2))
    t["indT"] = np.ascontiguousarray(gi.T)
    gb = (np.arange(BS)[:, None] // GC == np.arange(GB)).astype(f32)
    t["indb"], t["indbT"] = gb, np.ascontiguousarray(gb.T)
    keys = np.arange(S).reshape(H, KG, KW).transpose(1, 0, 2).reshape(-1)
    kh, kw = keys // W, keys % W
    rows = (np.arange(H)[:, None] == kh).astype(f32)
    part = (np.arange(KW)[:, None] == kw % KW).astype(f32)
    t["hot_max"] = np.concatenate([rows, part])
    tile_rows = (np.arange(KR)[:, None] == kh % KR).astype(f32)
    t["hot"] = np.concatenate([part, part, tile_rows, tile_rows, np.ones((1, S), f32)])
    c, s = cs(W, KWF, W)
    row = np.zeros((TR, W, TR, KWF, RI))
    irow = np.zeros((TR, KWF, RI, TR, W))
    mirrored = np.where((np.arange(KWF) == 0) | (np.arange(KWF) == KWF - 1), 1, 2)[:, None]
    for h in range(TR):
        row[h, :, h, :, 0], row[h, :, h, :, 1] = c, -s
        irow[h, :, 0, h], irow[h, :, 1, h] = mirrored * c.T, -mirrored * s.T
    t["row_dft"] = (row.reshape(TT, TR * FR) / W ** 0.5).astype(f32)
    t["irow_dft"] = (irow.reshape(TR * FR, TT) / W ** 0.5).astype(f32)
    c, s = cs(H, H, H)
    col = np.zeros((RI, H, RI, H))
    col[0, :, 0], col[1, :, 0], col[0, :, 1], col[1, :, 1] = c, s, -s, c
    t["col_dft"] = (col.reshape(RI * H, RI * H) / H ** 0.5).astype(f32)
    icol = np.zeros((2, H, 3, 2, H))
    for k in range(2):
        icol[k, :, 0, k], icol[k, :, 1, k], icol[k, :, 2, k] = c, s, -s
    t["icol_dft"] = (icol.reshape(2 * H, 3, 2 * H) / H ** 0.5).astype(f32)
    return t


def build(nc, a, out):
    def scratch(name, shape):
        return nc.dram_tensor(name, shape, F32).ap()

    x = a["x"].rearrange("b h w c -> b (h w) c")
    qF = scratch("q_scratch", (NP, P, S))
    qHL = scratch("q_split_scratch", (NP, P, 2, S))
    kHL = scratch("k_split_scratch", (NP, P, 2, S))
    vD = scratch("v_scratch", (NP, P, KT, P))
    relH = scratch("row_logits_scratch", (NP, 2, 2 * H, S))
    relW = scratch("column_logits_scratch", (NP, 2, 2 * W, S))
    maxD = scratch("maximum_scratch", (NP, 2, S))
    aD = scratch("attention_scratch", (NP, P, S))
    sumD = scratch("probability_sum_scratch", (NP, 2, S))
    invD = scratch("inverse_sum_scratch", (NP, 2, S))
    x1D = scratch("x1_scratch", (B, S, C))
    rowsD = scratch("row_spectrum_scratch", (B, H, KWF, RI, C))
    specD = scratch("mixed_spectrum_scratch", (B, H, KWF, RI, C))
    project(nc, x, a["qkv_w"], a["qk_bias"], a["qkv_b"], a["ident"], a["ind"], a["indT"], qF, qHL, kHL, vD)
    relpos(nc, a["rev_h"], a["rev_w"], qF, relH, relW)
    attend(nc, a["ident"], a["hot_max"], a["hot"], qHL, kHL, vD, relH, relW, maxD, aD, sumD)
    out_project(nc, x, a["proj_w"], a["proj_b"], a["row_dft"], aD, sumD, invD, x1D, rowsD)
    spectrum(nc, a["w1"], a["b1"], a["w2"], a["b2"], a["col_dft"], a["icol_dft"], a["indb"], a["indbT"], rowsD, specD)
    image(nc, a["irow_dft"], x1D, specD, out.rearrange("b h w c -> b (h w) c"))


def kernel(**inputs):
    import concourse.bacc as bacc
    from concourse.bass_utils import run_bass_kernel_spmd

    i = {k: np.asarray(v) for k, v in inputs.items()}
    arrays = dict(
        x=i["x"], qkv_w=i["L0_conv_qkv_w"], qkv_b=i["L0_conv_qkv_b"],
        qk_bias=i["L0_conv_qkv_b"][:2 * C].reshape(2 * PAIRS, P).T,
        proj_w=i["L0_conv_proj_w"], proj_b=i["L0_conv_proj_b"],
        rev_h=i["L0_conv_rel_pos_h"][::-1].T, rev_w=i["L0_conv_rel_pos_w"][::-1].T,
        w1=i["L1_conv_w1"], b1=i["L1_conv_b1"].transpose(2, 1, 0),
        w2=i["L1_conv_w2"], b2=i["L1_conv_b2"].transpose(1, 0, 2).reshape(-1), **tables())
    arrays = {k: np.ascontiguousarray(v) for k, v in arrays.items()}
    nc = bacc.Bacc("TRN2", target_bir_lowering=False, num_devices=1)
    aps = {k: nc.dram_tensor(f"in_{k}", v.shape, F32, kind="ExternalInput").ap() for k, v in arrays.items()}
    out = nc.dram_tensor("out_image", (B, H, W, C), F32, kind="ExternalOutput").ap()
    build(nc, aps, out)
    result = run_bass_kernel_spmd(nc, [{f"in_{k}": v for k, v in arrays.items()}], core_ids=[0])
    return result.results[0]["out_image"]
```
